# Optimizing a Trainium2 kernel written in Bass

```python
import numpy as np
import jax
import jax.numpy as jnp

def _softmax(x, axis=-1):
    return jax.nn.softmax(x, axis=axis)

def _gelu(x):
    return jax.nn.gelu(x, approximate=True)

def _silu(x):
    return jax.nn.silu(x)

def _sigmoid(x):
    return jax.nn.sigmoid(x)

def _layernorm(x, axis=-1, eps=1e-05):
    m = jnp.mean(x, axis=axis, keepdims=True)
    v = jnp.var(x, axis=axis, keepdims=True)
    return (x - m) / jnp.sqrt(v + eps)

def _scatter_add(tgt, idx, src, axis=0):
    return tgt.at[idx].add(src)

def _segment_sum(src, seg, n):
    return jax.ops.segment_sum(src, seg, n)
kernel_name = 'mk_hybrid_d1_jaxref_r8_6ca77a'

def setup_inputs(seed: int=0):
    np.random.seed(seed)
    _w = jnp.asarray

    def _L0_attn_a_setup():
        import jax, jax.numpy as jnp
        import numpy as np
        from jax import lax
        D_MODEL = 128
        D_STATE = 16
        D_CONV = 4
        EXPAND = 2
        D_INNER = EXPAND * D_MODEL
        DT_RANK = -(-D_MODEL // 16)
        BATCH = 2
        T = 128

        def _silu(u):
            return u * jax.nn.sigmoid(u)

        def _forward(x, W_in, conv_w, conv_b, W_xproj, W_dt, b_dt, A_log, D_param, W_out):
            B, Tlen, _ = x.shape
            xz = x @ W_in
            x_b, z = jnp.split(xz, 2, axis=-1)
            xpad = jnp.pad(x_b, ((0, 0), (D_CONV - 1, 0), (0, 0)))
            xc = conv_b
            for k in range(D_CONV):
                xc = xc + xpad[:, k:k + Tlen, :] * conv_w[:, k]
            xc = _silu(xc)
            proj = xc @ W_xproj
            delta_raw = proj[..., :DT_RANK]
            B_in = proj[..., DT_RANK:DT_RANK + D_STATE]
            C_in = proj[..., DT_RANK + D_STATE:]
            delta = jax.nn.softplus(delta_raw @ W_dt + b_dt)
            A = -jnp.exp(A_log)
            A_bar = jnp.exp(delta[..., None] * A)
            Bx = delta[..., None] * B_in[:, :, None, :] * xc[..., None]

            def step(h, ins):
                a_t, bx_t, c_t, xc_t = ins
                h = a_t * h + bx_t
                y_t = jnp.einsum('bds,bs->bd', h, c_t) + D_param * xc_t
                return (h, y_t)
            h0 = jnp.zeros((B, D_INNER, D_STATE), dtype=x.dtype)
            ins = (jnp.swapaxes(A_bar, 0, 1), jnp.swapaxes(Bx, 0, 1), jnp.swapaxes(C_in, 0, 1), jnp.swapaxes(xc, 0, 1))
            _, ys = lax.scan(step, h0, ins)
            y = jnp.swapaxes(ys, 0, 1) * _silu(z)
            return y @ W_out
        key = jax.random.key(seed)
        ks = jax.random.split(key, 9)
        s = 0.02
        x = jax.random.normal(ks[0], (BATCH, T, D_MODEL), dtype=jnp.float32)
        W_in = jax.random.normal(ks[1], (D_MODEL, 2 * D_INNER), dtype=jnp.float32) * s
        conv_w = jax.random.normal(ks[2], (D_INNER, D_CONV), dtype=jnp.float32) * 0.2
        conv_b = jax.random.normal(ks[3], (D_INNER,), dtype=jnp.float32) * 0.02
        W_xproj = jax.random.normal(ks[4], (D_INNER, DT_RANK + 2 * D_STATE), dtype=jnp.float32) * s
        W_dt = jax.random.normal(ks[5], (DT_RANK, D_INNER), dtype=jnp.float32) * s
        b_dt = jax.random.normal(ks[6], (D_INNER,), dtype=jnp.float32) * 0.02
        A_log = jnp.broadcast_to(jnp.log(jnp.arange(1, D_STATE + 1, dtype=jnp.float32)), (D_INNER, D_STATE)).copy()
        D_param = jnp.ones((D_INNER,), dtype=jnp.float32)
        W_out = jax.random.normal(ks[7], (D_INNER, D_MODEL), dtype=jnp.float32) * s
        return {'x': x, 'W_in': W_in, 'conv_w': conv_w, 'conv_b': conv_b, 'W_xproj': W_xproj, 'W_dt': W_dt, 'b_dt': b_dt, 'A_log': A_log, 'D_param': D_param, 'W_out': W_out}
    _L0_attn_a_in = _L0_attn_a_setup()

    def _L0_attn_b_setup():
        import jax, jax.numpy as jnp
        import numpy as np
        B, CTX, DIMS, HEAD = (8, 512, 128, 16)
        HD = DIMS // HEAD
        EPS = 1e-05
        THRESH = 0.01
        FACTOR = 0.1
        MAX_IT = 3

        def _ln(x, w):
            m = jnp.mean(x, axis=-1, keepdims=True)
            v = jnp.mean((x - m) ** 2, axis=-1, keepdims=True)
            return (x - m) * jax.lax.rsqrt(v + EPS) * w
        key = jax.random.key(seed)
        ks = jax.random.split(key, 9)
        w = lambda k, shp: jax.random.normal(k, shp, jnp.float32) * 0.02
        return {'x': jax.random.normal(ks[0], (B, CTX, DIMS), jnp.float32), 'qw': w(ks[1], (DIMS, DIMS)), 'qb': jnp.zeros((DIMS,), jnp.float32), 'kw': w(ks[2], (DIMS, DIMS)), 'vw': w(ks[3], (DIMS, DIMS)), 'vb': jnp.zeros((DIMS,), jnp.float32), 'ow': w(ks[4], (DIMS, DIMS)), 'ob': jnp.zeros((DIMS,), jnp.float32), 'lna_w': jnp.ones((DIMS,), jnp.float32), 'lnb_w': jnp.ones((DIMS,), jnp.float32), 'lnc_w': jnp.ones((HD,), jnp.float32), 'lnd_w': jnp.ones((HD,), jnp.float32), 'lqw': w(ks[5], (HD, HD)), 'lqb': jnp.zeros((HD,), jnp.float32), 'lkw': w(ks[6], (HD, HD)), 'lkb': jnp.zeros((HD,), jnp.float32), 'lvw': w(ks[7], (HD, HD)), 'lvb': jnp.zeros((HD,), jnp.float32)}
    _L0_attn_b_in = _L0_attn_b_setup()

    def _L0_ffn_setup():
        import jax, jax.numpy as jnp
        import numpy as np
        D_IN, D_HID = (128, 512)

        def _ternary(key, shape):
            return jax.random.randint(key, shape, -1, 2).astype(jnp.float32)

        def _tlin(x, w, s):
            return jnp.einsum('bsi,oi->bso', x, w) * s
        key = jax.random.key(seed)
        ks = jax.random.split(key, 12)
        inv = lambda fan: 1.0 / np.sqrt(fan).astype(np.float32)
        return {'x': jax.random.normal(ks[0], (4, 256, D_IN), dtype=jnp.float32), 'w1_w': _ternary(ks[1], (D_HID, D_IN)), 'w1_s': jax.random.uniform(ks[2], (D_HID,), dtype=jnp.float32) * inv(D_IN), 'w2_w': _ternary(ks[3], (D_HID, D_IN)), 'w2_s': jax.random.uniform(ks[4], (D_HID,), dtype=jnp.float32) * inv(D_IN), 'h1_w': _ternary(ks[5], (D_HID, D_HID)), 'h1_s': jax.random.uniform(ks[6], (D_HID,), dtype=jnp.float32) * inv(D_HID), 'h2_w': _ternary(ks[7], (D_HID, D_HID)), 'h2_s': jax.random.uniform(ks[8], (D_HID,), dtype=jnp.float32) * inv(D_HID), 'w3_w': _ternary(ks[9], (D_IN, D_HID)), 'w3_s': jax.random.uniform(ks[10], (D_IN,), dtype=jnp.float32) * inv(D_HID)}
    _L0_ffn_in = _L0_ffn_setup()
    _d = {'L0_attn_a_x': _L0_attn_a_in['x'], 'L0_attn_a_W_in': _L0_attn_a_in['W_in'], 'L0_attn_a_conv_w': _L0_attn_a_in['conv_w'], 'L0_attn_a_conv_b': _L0_attn_a_in['conv_b'], 'L0_attn_a_W_xproj': _L0_attn_a_in['W_xproj'], 'L0_attn_a_W_dt': _L0_attn_a_in['W_dt'], 'L0_attn_a_b_dt': _L0_attn_a_in['b_dt'], 'L0_attn_a_A_log': _L0_attn_a_in['A_log'], 'L0_attn_a_D_param': _L0_attn_a_in['D_param'], 'L0_attn_a_W_out': _L0_attn_a_in['W_out'], 'L0_attn_b_qw': _L0_attn_b_in['qw'], 'L0_attn_b_qb': _L0_attn_b_in['qb'], 'L0_attn_b_kw': _L0_attn_b_in['kw'], 'L0_attn_b_vw': _L0_attn_b_in['vw'], 'L0_attn_b_vb': _L0_attn_b_in['vb'], 'L0_attn_b_ow': _L0_attn_b_in['ow'], 'L0_attn_b_ob': _L0_attn_b_in['ob'], 'L0_attn_b_lna_w': _L0_attn_b_in['lna_w'], 'L0_attn_b_lnb_w': _L0_attn_b_in['lnb_w'], 'L0_attn_b_lnc_w': _L0_attn_b_in['lnc_w'], 'L0_attn_b_lnd_w': _L0_attn_b_in['lnd_w'], 'L0_attn_b_lqw': _L0_attn_b_in['lqw'], 'L0_attn_b_lqb': _L0_attn_b_in['lqb'], 'L0_attn_b_lkw': _L0_attn_b_in['lkw'], 'L0_attn_b_lkb': _L0_attn_b_in['lkb'], 'L0_attn_b_lvw': _L0_attn_b_in['lvw'], 'L0_attn_b_lvb': _L0_attn_b_in['lvb'], 'L0_ffn_w1_w': _L0_ffn_in['w1_w'], 'L0_ffn_w1_s': _L0_ffn_in['w1_s'], 'L0_ffn_w2_w': _L0_ffn_in['w2_w'], 'L0_ffn_w2_s': _L0_ffn_in['w2_s'], 'L0_ffn_h1_w': _L0_ffn_in['h1_w'], 'L0_ffn_h1_s': _L0_ffn_in['h1_s'], 'L0_ffn_h2_w': _L0_ffn_in['h2_w'], 'L0_ffn_h2_s': _L0_ffn_in['h2_s'], 'L0_ffn_w3_w': _L0_ffn_in['w3_w'], 'L0_ffn_w3_s': _L0_ffn_in['w3_s']}
    _x0 = _d['L0_attn_a_x']
    _d['L0_attn_a_x'] = jax.random.normal(jax.random.fold_in(jax.random.key(seed), 1), (4, 1024, 128), dtype=_x0.dtype)
    del _x0
    return _d

def reference(L0_attn_a_x, L0_attn_a_W_in, L0_attn_a_conv_w, L0_attn_a_conv_b, L0_attn_a_W_xproj, L0_attn_a_W_dt, L0_attn_a_b_dt, L0_attn_a_A_log, L0_attn_a_D_param, L0_attn_a_W_out, L0_attn_b_qw, L0_attn_b_qb, L0_attn_b_kw, L0_attn_b_vw, L0_attn_b_vb, L0_attn_b_ow, L0_attn_b_ob, L0_attn_b_lna_w, L0_attn_b_lnb_w, L0_attn_b_lnc_w, L0_attn_b_lnd_w, L0_attn_b_lqw, L0_attn_b_lqb, L0_attn_b_lkw, L0_attn_b_lkb, L0_attn_b_lvw, L0_attn_b_lvb, L0_ffn_w1_w, L0_ffn_w1_s, L0_ffn_w2_w, L0_ffn_w2_s, L0_ffn_h1_w, L0_ffn_h1_s, L0_ffn_h2_w, L0_ffn_h2_s, L0_ffn_w3_w, L0_ffn_w3_s):

    def _L0_attn_a_ref(x, W_in, conv_w, conv_b, W_xproj, W_dt, b_dt, A_log, D_param, W_out):
        import jax, jax.numpy as jnp
        import numpy as np
        from jax import lax
        D_MODEL = 128
        D_STATE = 16
        D_CONV = 4
        EXPAND = 2
        D_INNER = EXPAND * D_MODEL
        DT_RANK = -(-D_MODEL // 16)
        BATCH = 2
        T = 128

        def _silu(u):
            return u * jax.nn.sigmoid(u)

        def _forward(x, W_in, conv_w, conv_b, W_xproj, W_dt, b_dt, A_log, D_param, W_out):
            B, Tlen, _ = x.shape
            xz = x @ W_in
            x_b, z = jnp.split(xz, 2, axis=-1)
            xpad = jnp.pad(x_b, ((0, 0), (D_CONV - 1, 0), (0, 0)))
            xc = conv_b
            for k in range(D_CONV):
                xc = xc + xpad[:, k:k + Tlen, :] * conv_w[:, k]
            xc = _silu(xc)
            proj = xc @ W_xproj
            delta_raw = proj[..., :DT_RANK]
            B_in = proj[..., DT_RANK:DT_RANK + D_STATE]
            C_in = proj[..., DT_RANK + D_STATE:]
            delta = jax.nn.softplus(delta_raw @ W_dt + b_dt)
            A = -jnp.exp(A_log)
            A_bar = jnp.exp(delta[..., None] * A)
            Bx = delta[..., None] * B_in[:, :, None, :] * xc[..., None]

            def step(h, ins):
                a_t, bx_t, c_t, xc_t = ins
                h = a_t * h + bx_t
                y_t = jnp.einsum('bds,bs->bd', h, c_t) + D_param * xc_t
                return (h, y_t)
            h0 = jnp.zeros((B, D_INNER, D_STATE), dtype=x.dtype)
            ins = (jnp.swapaxes(A_bar, 0, 1), jnp.swapaxes(Bx, 0, 1), jnp.swapaxes(C_in, 0, 1), jnp.swapaxes(xc, 0, 1))
            _, ys = lax.scan(step, h0, ins)
            y = jnp.swapaxes(ys, 0, 1) * _silu(z)
            return y @ W_out
        return _forward(x, W_in, conv_w, conv_b, W_xproj, W_dt, b_dt, A_log, D_param, W_out)

    def _L0_attn_b_ref(x, qw, qb, kw, vw, vb, ow, ob, lna_w, lnb_w, lnc_w, lnd_w, lqw, lqb, lkw, lkb, lvw, lvb):
        import jax, jax.numpy as jnp
        import numpy as np
        B, CTX, DIMS, HEAD = (8, 512, 128, 16)
        HD = DIMS // HEAD
        EPS = 1e-05
        THRESH = 0.01
        FACTOR = 0.1
        MAX_IT = 3

        def _ln(x, w):
            m = jnp.mean(x, axis=-1, keepdims=True)
            v = jnp.mean((x - m) ** 2, axis=-1, keepdims=True)
            return (x - m) * jax.lax.rsqrt(v + EPS) * w
        b, ctx, dims = x.shape
        q = _ln(x, lna_w) @ qw.T + qb
        xb = _ln(x, lnb_w)
        k = xb @ kw.T
        v = xb @ vw.T + vb
        split = lambda t: t.reshape(b, ctx, HEAD, HD).transpose(0, 2, 1, 3)
        query, key_t, value = (split(q), split(k), split(v))
        eff = min(ctx, HEAD)
        kn = _ln(key_t[:, :, :eff, :] @ lkw.T + lkb, lnd_w)
        vi = value[:, :, :eff, :] @ lvw.T + lvb
        scale = 1.0 / np.sqrt(HD)

        def step(qcur):
            qn = _ln(qcur[:, :, :eff, :] @ lqw.T + lqb, lnc_w)
            logits = jnp.einsum('bhqd,bhkd->bhqk', qn, kn) * scale
            attn = jax.nn.softmax(logits, axis=-1) @ vi
            return jnp.zeros_like(qcur).at[:, :, :eff, :].set(attn)
        prev = jnp.zeros_like(query)
        attn_out = jnp.zeros_like(query)
        qcur = query
        done = jnp.asarray(False)
        for it in range(MAX_IT):
            iter_out = step(qcur)
            diff = jnp.mean(jnp.abs(iter_out - prev))
            brk = (diff < THRESH + FACTOR * diff) & jnp.asarray(it > 0) & ~done
            attn_out = jnp.where(done, attn_out, iter_out)
            prev = jnp.where(done, prev, iter_out)
            qcur = jnp.where(done | brk, qcur, qcur + iter_out)
            done = done | brk
        out = attn_out.transpose(0, 2, 1, 3).reshape(b, ctx, dims)
        return out @ ow.T + ob

    def _L0_ffn_ref(x, w1_w, w1_s, w2_w, w2_s, h1_w, h1_s, h2_w, h2_s, w3_w, w3_s):
        import jax, jax.numpy as jnp
        import numpy as np
        D_IN, D_HID = (128, 512)

        def _ternary(key, shape):
            return jax.random.randint(key, shape, -1, 2).astype(jnp.float32)

        def _tlin(x, w, s):
            return jnp.einsum('bsi,oi->bso', x, w) * s
        h = jax.nn.silu(_tlin(x, w1_w, w1_s)) * _tlin(x, w2_w, w2_s)
        h = jax.nn.gelu(_tlin(h, h1_w, h1_s), approximate=False)
        h = jax.nn.gelu(_tlin(h, h2_w, h2_s), approximate=False)
        return _tlin(h, w3_w, w3_s)
    x = L0_attn_a_x
    x = x + _L0_attn_a_ref(_layernorm(x, axis=-1), L0_attn_a_W_in, L0_attn_a_conv_w, L0_attn_a_conv_b, L0_attn_a_W_xproj, L0_attn_a_W_dt, L0_attn_a_b_dt, L0_attn_a_A_log, L0_attn_a_D_param, L0_attn_a_W_out)
    x = x + _L0_ffn_ref(_layernorm(x, axis=-1), L0_ffn_w1_w, L0_ffn_w1_s, L0_ffn_w2_w, L0_ffn_w2_s, L0_ffn_h1_w, L0_ffn_h1_s, L0_ffn_h2_w, L0_ffn_h2_s, L0_ffn_w3_w, L0_ffn_w3_s)
    x = x + _L0_attn_b_ref(_layernorm(x, axis=-1), L0_attn_b_qw, L0_attn_b_qb, L0_attn_b_kw, L0_attn_b_vw, L0_attn_b_vb, L0_attn_b_ow, L0_attn_b_ob, L0_attn_b_lna_w, L0_attn_b_lnb_w, L0_attn_b_lnc_w, L0_attn_b_lnd_w, L0_attn_b_lqw, L0_attn_b_lqb, L0_attn_b_lkw, L0_attn_b_lkb, L0_attn_b_lvw, L0_attn_b_lvb)
    x = x + _L0_ffn_ref(_layernorm(x, axis=-1), L0_ffn_w1_w, L0_ffn_w1_s, L0_ffn_w2_w, L0_ffn_w2_s, L0_ffn_h1_w, L0_ffn_h1_s, L0_ffn_h2_w, L0_ffn_h2_s, L0_ffn_w3_w, L0_ffn_w3_s)
    return x

_drawn_inputs = setup_inputs


def setup_inputs(seed=0):
    import zlib

    import numpy as np

    out = dict(_drawn_inputs(seed))
    spreads = {'L0_attn_a_D_param': (1.0, 0.2),
     'L0_attn_b_qb': (0.0, 0.1),
     'L0_attn_b_vb': (0.0, 0.1),
     'L0_attn_b_ob': (0.0, 0.1),
     'L0_attn_b_lna_w': (1.0, 0.2),
     'L0_attn_b_lnb_w': (1.0, 0.2),
     'L0_attn_b_lnc_w': (1.0, 0.2),
     'L0_attn_b_lnd_w': (1.0, 0.2),
     'L0_attn_b_lqb': (0.0, 0.1),
     'L0_attn_b_lkb': (0.0, 0.1),
     'L0_attn_b_lvb': (0.0, 0.1)}
    factors = {}
    for name, (base, spread) in spreads.items():
        noise = np.random.default_rng([zlib.crc32(name.encode()), seed]).standard_normal(out[name].shape)
        drawn = base * np.exp(spread * noise) if base else spread * noise
        out[name] = jnp.asarray(drawn.astype(out[name].dtype))
    for name, factor in factors.items():
        out[name] = (out[name] * factor).astype(out[name].dtype)
    return out
```

```python
from contextlib import ExitStack

import numpy as np

import concourse.bass as bass
from concourse import mybir

P = 128
D = 128
NB, T = 4, 1024
H = T // 2
DI, NS, DC, DTR = 256, 16, 4, 8
DT = DI // P
HID = 512
MT = HID // P
NH, HD, EFF = 16, 8, 16
NT = NB * EFF
EPS = 1e-5
Q = 4
SQ = NS // Q
NU = 5
NA = 2 * SQ

MATS = [("w_in", 2 * DI), ("w_xproj", DT * 104), ("w_out", DT * D), ("w_dt", DI), ("w1", HID), ("w2", HID),
        ("h1", MT * HID), ("h2", MT * HID), ("w3", MT * D), ("qw", D), ("kw", D), ("vw", D), ("ow", D),
        ("ident", P), ("group", P)]
COLS = [("conv_w", DT * DC), ("conv_b", DT), ("b_dt", DT), ("a_log", DT * NS), ("d_param", DT), ("s1", MT), ("s2", MT),
        ("sh1", MT), ("sh2", MT), ("s3", 1), ("qb", 1), ("vb", 1), ("ob", 1), ("lna", 1), ("lnb", 1), ("lnc", 1),
        ("lnd", 1), ("lqb", 1), ("lkb", 1), ("lvb", 1), ("lqw", HD), ("lkw", HD), ("lvw", HD), ("pick", 2 * NS),
        ("head_of", NH), ("vhead_of", 2 * NH)]


def offsets(parts):
    at, out = 0, {}
    for name, n in parts:
        out[name] = (at, at + n)
        at += n
    return out, at


MAT_AT, NMAT = offsets(MATS)
COL_AT, NCOL = offsets(COLS)


class Signal:

    def __init__(self, ctx, nc, name, per):
        self.sem, self.per = ctx.enter_context(nc.semaphore(name)), per

    def at(self, b, n):
        return b * self.per + n


class Steps:

    def __init__(self, ctx, nc, name, names):
        self.sem = ctx.enter_context(nc.semaphore(name))
        self.names = list(names)

    def after(self, name):
        return self.names.index(name) + 1


def hybrid_kernel(nc, xT, mats, cols, rep, outT):
    fp32, f32r = mybir.dt.float32, mybir.dt.float32r
    ALU, ACT, AX = mybir.AluOpType, mybir.ActivationFunctionType, mybir.AxisListType

    ctx = ExitStack()
    with ctx:
        def sb(name, shape, dt=fp32):
            return ctx.enter_context(nc.sbuf_tensor(name, shape, dt))

        def signal(name, per):
            return Signal(ctx, nc, name, per)

        X = sb("X", [P, NB * T])
        M = sb("M", [P, NMAT])
        C = sb("C", [P, NCOL])
        mean_w = sb("mean_w", [P, P])
        eps_col = sb("eps_col", [P, 1])
        one_col = sb("one_col", [P, 1])
        pick = sb("pick", [P, 2 * NS], f32r)
        a_neg = sb("a_neg", [P, DT * NS])
        mc = sb("mc", [P, T])
        mr = sb("mr", [P, T])
        xb = sb("xb", [P, DT, T + DC - 1])
        xs = sb("xs", [P, DT, T])
        zs = sb("zs", [P, DT, T])
        dl = sb("dl", [P, DT, T])
        dx = sb("dx", [P, DT, T])
        bc = sb("bc", [P, T], f32r)
        dr = mc
        A = sb("A", [P, NA, T])
        U = sb("U", [P, NU, T])
        cs = sb("cs", [P, 2, T])
        yz = xb
        XF = sb("XF", [P, T])
        fc = sb("fc", [P, T])
        fr = sb("fr", [P, T])
        XO = fr
        gs = sb("gs", [P, 2, H])
        hA = sb("hA", [P, 2, MT, H])
        hB = sb("hB", [P, 2, MT, H])
        spec = sb("spec", [P, NT])

        PY = ctx.enter_context(nc.psum_tensor("PY", [P, DT, 2, H], fp32))
        PR = ctx.enter_context(nc.psum_tensor("PR", [P, 2, H], fp32))
        PF = ctx.enter_context(nc.psum_tensor("PF", [P, 2, H], fp32))
        Y4 = PY[:, :, :, :].rearrange("p d h t -> p (d h) t")

        def mat(name, k=0, w=None, rows=slice(0, P)):
            lo, hi = MAT_AT[name]
            w = w or hi - lo
            return M[rows, lo + k * w:lo + (k + 1) * w]

        def col(name, k=0, w=1):
            lo, _ = COL_AT[name]
            return C[:, lo + k * w:lo + (k + 1) * w]

        def half(t, j):
            return t[:, j * H:(j + 1) * H]

        x_in = [ctx.enter_context(nc.semaphore(f"x_in{b}")) for b in range(NB)]
        w_in = ctx.enter_context(nc.semaphore("weights_in"))
        rep_in = ctx.enter_context(nc.semaphore("rep_in"))
        stored = ctx.enter_context(nc.semaphore("stored"))
        s_set = ctx.enter_context(nc.semaphore("constants_set"))
        s_aneg = ctx.enter_context(nc.semaphore("a_neg_set"))
        m_mean, m_cent, m_sq, m_var = signal("m_mean", 2), signal("m_cent", 2), signal("m_sq", 2), signal("m_var", 2)
        m_ln, m_rs, m_norm, m_proj = signal("m_ln", 2), signal("m_rs", 2), signal("m_norm", 2), signal("m_proj", 8)
        m_evac, m_conv, m_xs = signal("m_evac", 8), signal("m_conv", DC * DT), signal("m_xs", DT)
        m_xp, m_hi, m_bc, m_dr = signal("m_xp", 2), signal("m_hi", 2), signal("m_bc", 2), signal("m_dr", 2)
        m_dps, m_soft, m_dl, m_dx = signal("m_dps", DT), signal("m_soft", 4 * DT), signal("m_dl", DT), signal("m_dx", DT)
        b_ready, c_ready = signal("b_ready", NS), signal("c_ready", NS)
        c_copied = signal("c_copied", NS)
        a_ready, u_ready, h_ready, g_ready = (signal(n, NS * DT) for n in ("a_ready", "u_ready", "h_ready", "g_ready"))
        g_summed = signal("g_summed", NS * DT)
        m_yd, m_yz, m_out, m_res = signal("m_yd", DT), signal("m_yz", DT), signal("m_out", 2), signal("m_res", 2)
        f_mean, f_cent, f_sq, f_var = signal("f_mean", 4), signal("f_cent", 4), signal("f_sq", 4), signal("f_var", 4)
        f_ln, f_rs, f_norm = signal("f_ln", 4), signal("f_rs", 4), signal("f_norm", 4)
        f_gu, f_silu, f_act = signal("f_gu", 4 * MT), signal("f_silu", 4 * MT), signal("f_act", 4 * MT)
        f_hps, f_gelu = signal("f_hps", 8 * MT), signal("f_gelu", 8 * MT)
        f_ops, f_res, f_ob = signal("f_ops", 4), signal("f_res", 4), signal("f_ob", 2)
        f_spec = signal("f_spec", 1)
        xo_free = signal("xo_free", 1)

        ITERS = range(3)
        V = Steps(ctx, nc, "attn_dve", ["zero", "c_o", "n_o", "c_i", "n_i", "qa", "ka", "q", "k", "v", "bdq", "bdk", "bdv", "k0", "vi",
                                        "c_k", "n_k", "kblk", "vi_sb", "v_sb", "vblk0", "vblk1"]
                  + [f"{n}{t}" for t in ITERS for n in ("q0", "c_q", "n_q", "max", "sub", "sum", "rec", "prob", "pt", "att")
                     + (("qcur",) if t < 2 else ()) + (("diff", ) if t == 1 else ())]
                  + ["mean_abs", "limit", "brk", "keep", "old", "sel", "x3", "x4", "c_f", "n_f"] + [f"act{m}" for m in range(MT)] + ["x5"])
        S = Steps(ctx, nc, "attn_act", ["sq_o", "ln_o", "rs_o", "sq_i", "ln_i", "rs_i", "sq_k", "ln_k", "rs_k"]
                  + [f"{n}{t}" for t in ITERS for n in ("sq_q", "ln_q", "rs_q", "exp") + (("abs",) if t == 1 else ())]
                  + ["sq_f", "ln_f", "rs_f"] + [f"{n}{m}" for n in ("silu", "gelu_a", "gelu_b") for m in range(MT)])
        E = Steps(ctx, nc, "attn_pe", ["mean_o", "var_o", "mean_i", "var_i", "q", "k", "v", "kk", "vv", "mean_k", "var_k", "vi_t", "rep"]
                  + [f"{n}{t}" for t in ITERS for n in ("qq", "mean_q", "var_q", "logits", "pt", "att") + (("diff",) if t == 1 else ())]
                  + ["ow", "mean_f", "var_f", "gu", "ha", "hb", "w3"])

        AT = A[:, :, :].rearrange("p a t -> p (a t)")
        at_used = [0]

        def part(n):
            at_used[0] += n
            return AT[:, at_used[0] - n:at_used[0]]

        t_c, t_r, t_n, t_qa, t_ka = (part(NT) for _ in range(5))
        t_q, t_k, t_v, t_k0, t_kn, t_vi, t_q0, t_qn = (part(NT) for _ in range(8))
        bdq, bdk, bdv = (part(P) for _ in range(3))
        t_vsb = part(P)
        t_rep = part(NB * P)
        qpad = part(NB * 32)
        kblk = part(NB * NH * EFF)
        vrep = part(NB * P)
        vblk = part(2 * NB * P)
        prob = part(NH * EFF)
        pT = part(2 * P)
        att = [part(NT) for _ in ITERS]
        t_d, t_old = part(NT), part(NT)
        tiny = part(8)
        smax, ssum = part(NH), part(NH)
        f_h0, f_h1, f_h2, f_g = (part(MT * NT) for _ in range(4))
        x3, x5 = part(NT), part(NT)

        block = ctx.enter_context(nc.Block())

        SCHED = []
        for f in range(2):
            SCHED += [[("ln", f, 0), ("up", f, 0)], [("up", f, 1), ("up", f, 2)], [("up", f, 3), ("h1", f, 0)],
                      [("h1", f, 1), ("h1", f, 2)],
                      [("h1", f, 3)], [("h2", f, 0), ("h2", f, 1)], [("h2", f, 2)], [("h2", f, 3), ("down", f, 0)]]

        @block.sync
        def _(sp):
            sp.dma_start(X[:, 0:T], xT[:, 0:T]).then_inc(x_in[0], 16)
            sp.dma_start(C[:, :], cols).then_inc(w_in, 16)
            sp.dma_start(M[:, :], mats).then_inc(w_in, 16)
            for b in range(1, NB):
                sp.dma_start(X[:, b * T:(b + 1) * T], xT[:, b * T:(b + 1) * T]).then_inc(x_in[b], 16)

            def store(b):
                sp.wait_ge(f_res.sem, f_res.at(b, 4))
                sp.dma_start(outT[:, bass.ds(b * T + EFF, T - EFF)], XO[:, EFF:T]).then_inc(stored, 16)
                sp.wait_ge(stored, 16 * (b + 1))
                sp.sem_inc(xo_free.sem, 1)

            with sp.Fori(0, NB) as i:
                store(i)
            sp.wait_ge(h_ready.sem, h_ready.at(NB - 1, NS * DT))
            sp.dma_start(t_rep[0:NT, :], rep).then_inc(rep_in, 16)
            sp.wait_ge(V.sem, V.after("x5"))
            sp.dma_start(outT.rearrange("p (b t) -> p b t", b=NB)[:, :, 0:EFF],
                         x5.rearrange("p (b t) -> p b t", b=NB)).then_inc(stored, 16)
            sp.wait_ge(stored, 16 * (NB + 1))

        @block.gpsimd
        def _(pool):
            pool.memset(mean_w[:, :], 1.0 / P).then_inc(s_set, 1)
            pool.memset(eps_col[:, :], EPS).then_inc(s_set, 1)
            pool.sem_inc(xo_free.sem, 1)
            pool.memset(one_col[:, :], 1.0).then_inc(s_set, 1)
            pool.memset(bc[:, :].bitcast(fp32), 0.0).then_inc(s_set, 1)
            pool.memset(xb[:, :, 0:DC - 1], 0.0).then_inc(s_set, 1)

            def scale_states(b):
                for s in range(NS):
                    for d in range(DT):
                        k = DT * s + d
                        if d == 0:
                            pool.wait_ge(c_copied.sem, c_copied.at(b, s + 1))
                        pool.wait_ge(h_ready.sem, h_ready.at(b, k + 1))
                        u = U[:, k % NU, :]
                        pool.tensor_tensor(u, u, cs[:, s % 2, :], ALU.mult).then_inc(g_ready.sem, 1)

            with pool.Fori(0, NB) as i:
                scale_states(i)

        @block.scalar
        def _(act):
            act.wait_ge(w_in, 32)
            act.wait_ge(s_set, 5)
            act.activation(a_neg[:, :], C[:, slice(*COL_AT["a_log"])], ACT.Exp).then_inc(s_aneg, 1)

            def rsqrt(src, dst, ln, rs, b, n, waits_ps):
                act.wait_ge(waits_ps.sem, waits_ps.at(b, n + 1))
                act.activation(dst, src, ACT.Ln, bias=eps_col[:, :]).then_inc(ln.sem, 1)
                act.wait_ge(ln.sem, ln.at(b, n + 1))
                act.activation(dst, dst, ACT.Exp, scale=-0.5).then_inc(rs.sem, 1)

            def mixer_first(b):
                for j in range(2):
                    act.wait_ge(m_cent.sem, m_cent.at(b, j + 1))
                    act.activation(half(mr, j), half(mc, j), ACT.Square).then_inc(m_sq.sem, 1)
                for j in range(2):
                    rsqrt(Y4[:, 2 + j, :], half(mr, j), m_ln, m_rs, b, j, m_var)
                for n in range(8):
                    m, j = n // 2, n % 2
                    act.wait_ge(m_proj.sem, m_proj.at(b, n + 1))
                    if m < DT:
                        dst = xb[:, m, DC - 1 + j * H:DC - 1 + (j + 1) * H]
                        act.activation(dst, Y4[:, n % 4, :], ACT.Copy).then_inc(m_evac.sem, 1)
                    else:
                        act.activation(half(zs[:, m - DT, :], j), Y4[:, n % 4, :], ACT.Silu).then_inc(m_evac.sem, 1)
                for d in range(DT):
                    act.wait_ge(m_conv.sem, m_conv.at(b, DC * (d + 1)))
                    act.activation(xs[:, d, :], xs[:, d, :], ACT.Silu).then_inc(m_xs.sem, 1)
                for d in range(DT):
                    ps = PY[:, d, :, :].rearrange("p h t -> p (h t)")
                    act.wait_ge(m_dps.sem, m_dps.at(b, d + 1))
                    act.activation(dx[:, d, :], ps, ACT.Abs, bias=col("b_dt", d)).then_inc(m_soft.sem, 1)
                    act.activation(dl[:, d, :], ps, ACT.Relu, bias=col("b_dt", d)).then_inc(m_soft.sem, 1)
                    act.wait_ge(m_soft.sem, m_soft.at(b, 4 * d + 1))
                    act.activation(dx[:, d, :], dx[:, d, :], ACT.Exp, scale=-1.0).then_inc(m_soft.sem, 1)
                    act.wait_ge(m_soft.sem, m_soft.at(b, 4 * d + 3))
                    act.activation(dx[:, d, :], dx[:, d, :], ACT.Ln, bias=one_col[:, :]).then_inc(m_soft.sem, 1)

            def decays(b, q):
                for s in range(SQ * q, SQ * (q + 1)):
                    for d in range(DT):
                        k = DT * s + d
                        act.wait_ge(m_dl.sem, m_dl.at(b, d + 1))
                        if k >= NA:
                            act.wait_ge(h_ready.sem, h_ready.at(b, k - NA + 1))
                        act.activation(A[:, k % NA, :], dl[:, d, :], ACT.Exp,
                                       scale=a_neg[:, d * NS + s:d * NS + s + 1]).then_inc(a_ready.sem, 1)

            def copy_c(b, s):
                act.wait_ge(c_ready.sem, c_ready.at(b, s + 1))
                if s >= 2:
                    act.wait_ge(g_ready.sem, g_ready.at(b, DT * (s - 1)))
                act.activation(cs[:, s % 2, :], PR[:, :, :].rearrange("p h t -> p (h t)"), ACT.Copy).then_inc(c_copied.sem, 1)

            def ffn(b, stage, f, m):
                for j in range(2):
                    if stage == "ln":
                        act.wait_ge(f_cent.sem, f_cent.at(b, 2 * f + j + 1))
                        if f == 0 and j == 0:
                            act.wait_ge(xo_free.sem, xo_free.at(b, 1))
                        act.activation(half(fr, j), half(fc, j), ACT.Square).then_inc(f_sq.sem, 1)
                    elif stage == "up":
                        n = 2 * MT * f + 2 * m + j
                        act.wait_ge(f_gu.sem, f_gu.at(b, n + 1))
                        if n >= 2:
                            act.wait_ge(f_act.sem, f_act.at(b, n - 1))
                        act.activation(gs[:, j, :], PF[:, 0, :], ACT.Silu, scale=col("s1", m)).then_inc(f_silu.sem, 1)
                    elif stage in ("h1", "h2"):
                        n = 4 * MT * f + (2 * MT if stage == "h2" else 0) + 2 * m + j
                        dst = hB if stage == "h1" else hA
                        act.wait_ge(f_hps.sem, f_hps.at(b, n + 1))
                        act.activation(dst[:, j, m, :], PF[:, j, :], ACT.Gelu,
                                       scale=col("s" + stage, m)).then_inc(f_gelu.sem, 1)
                if stage == "ln":
                    for j in range(2):
                        rsqrt(PF[:, j, :], half(fr, j), f_ln, f_rs, b, 2 * f + j, f_var)

            def body(b, fb):
                if b is not None:
                    mixer_first(b)
                for q in range(Q):
                    if b is not None:
                        decays(b, q)
                    for s in range(SQ * q, SQ * (q + 1)):
                        if b is not None:
                            copy_c(b, s)
                        if fb is not None:
                            for unit in SCHED[s]:
                                ffn(fb, *unit)

            body(0, None)
            with act.Fori(1, NB) as i:
                body(i, i - 1)
            body(None, NB - 1)

            def a_rsqrt(pe_step, n, src, w):
                act.wait_ge(E.sem, E.after(pe_step))
                act.activation(w, src, ACT.Ln, bias=eps_col[:, :]).then_inc(S.sem, 1)
                act.wait_ge(S.sem, S.after("ln_" + n))
                act.activation(w, w, ACT.Exp, scale=-0.5).then_inc(S.sem, 1)

            def a_square(dve_step):
                act.wait_ge(V.sem, V.after(dve_step))
                act.activation(t_r, t_c, ACT.Square).then_inc(S.sem, 1)

            for n in ("o", "i", "k"):
                a_square("c_" + n)
                a_rsqrt("var_" + n, n, Y4[:, 1, 0:NT], t_r)
            for t in ITERS:
                a_square(f"c_q{t}")
                a_rsqrt(f"var_q{t}", f"q{t}", Y4[:, 1, 0:NT], t_r)
                act.wait_ge(V.sem, V.after(f"sub{t}"))
                act.activation(prob, prob, ACT.Exp, scale=float(HD) ** -0.5).then_inc(S.sem, 1)
                if t == 1:
                    act.wait_ge(V.sem, V.after("diff1"))
                    act.activation(t_old, t_d, ACT.Abs, accum_out=tiny[:, 0:1]).then_inc(S.sem, 1)
            a_square("c_f")
            a_rsqrt("var_f", "f", Y4[:, 1, 0:NT], t_r)
            act.wait_ge(E.sem, E.after("gu"))
            for m in range(MT):
                act.activation(f_g[:, m * NT:(m + 1) * NT], Y4[:, 2, m * NT:(m + 1) * NT], ACT.Silu,
                               scale=col("s1", m)).then_inc(S.sem, 1)
            for step, ps, sc, dst in (("ha", 0, "sh1", f_h1), ("hb", 1, "sh2", f_h2)):
                act.wait_ge(E.sem, E.after(step))
                for m in range(MT):
                    act.activation(dst[:, m * NT:(m + 1) * NT], Y4[:, ps, m * NT:(m + 1) * NT], ACT.Gelu,
                                   scale=col(sc, m)).then_inc(S.sem, 1)

        @block.vector
        def _(dve):
            dve.wait_ge(w_in, 32)
            dve.wait_ge(s_set, 5)
            dve.tensor_copy(pick[:, :], C[:, slice(*COL_AT["pick"])]).then_inc(s_set, 1)
            dve.wait_ge(s_aneg, 1)
            dve.tensor_scalar(a_neg[:, :], a_neg[:, :], -1.0, None, ALU.mult).then_inc(s_aneg, 1)

            def mixer_first(b):
                for j in range(2):
                    dve.wait_ge(m_mean.sem, m_mean.at(b, j + 1))
                    dve.tensor_tensor(half(mc, j), X[:, bass.ds(b * T + j * H, H)], Y4[:, j, :],
                                      ALU.subtract).then_inc(m_cent.sem, 1)
                for j in range(2):
                    dve.wait_ge(m_rs.sem, m_rs.at(b, j + 1))
                    dve.tensor_tensor(half(mc, j), half(mc, j), half(mr, j), ALU.mult).then_inc(m_norm.sem, 1)
                for d in range(DT):
                    dve.wait_ge(m_evac.sem, m_evac.at(b, 2 * d + 2))
                    for k in range(DC):
                        w = col("conv_w", DC * d + k)
                        src = xb[:, d, k:k + T]
                        if k == 0:
                            dve.tensor_scalar(xs[:, d, :], src, w, col("conv_b", d), ALU.mult, ALU.add).then_inc(m_conv.sem, 1)
                        else:
                            dve.wait_ge(m_conv.sem, m_conv.at(b, DC * d + k))
                            dve.scalar_tensor_tensor(xs[:, d, :], src, w, xs[:, d, :], ALU.mult, ALU.add).then_inc(m_conv.sem, 1)
                for j in range(2):
                    ps = Y4[:, j, :]
                    dve.wait_ge(m_xp.sem, m_xp.at(b, j + 1))
                    dve.tensor_copy(bc[0:96, j * H:(j + 1) * H], ps[0:96, :]).then_inc(m_hi.sem, 1)
                    dve.tensor_copy(dr[96:104, j * H:(j + 1) * H], ps[96:104, :]).then_inc(m_dr.sem, 1)
                    dve.wait_ge(m_hi.sem, m_hi.at(b, j + 1))
                    lo = bc[64:96, j * H:(j + 1) * H]
                    dve.tensor_tensor(lo, ps[64:96, :], lo.bitcast(fp32), ALU.subtract).then_inc(m_bc.sem, 1)
                for d in range(DT):
                    dve.wait_ge(m_soft.sem, m_soft.at(b, 4 * d + 4))
                    dve.tensor_tensor(dl[:, d, :], dl[:, d, :], dx[:, d, :], ALU.add).then_inc(m_dl.sem, 1)
                    dve.wait_ge(m_dl.sem, m_dl.at(b, d + 1))
                    dve.tensor_tensor(dx[:, d, :], dl[:, d, :], xs[:, d, :], ALU.mult).then_inc(m_dx.sem, 1)

            def state(b, s):
                dve.wait_ge(b_ready.sem, b_ready.at(b, s + 1))
                for d in range(DT):
                    k = DT * s + d
                    dve.wait_ge(m_dx.sem, m_dx.at(b, d + 1))
                    if k >= NU:
                        dve.wait_ge(g_summed.sem, g_summed.at(b, k - NU + 1))
                    dve.tensor_tensor(U[:, k % NU, :], dx[:, d, :], PR[:, :, :].rearrange("p h t -> p (h t)"),
                                      ALU.mult).then_inc(u_ready.sem, 1)
                for d in range(DT):
                    k = DT * s + d
                    u = U[:, k % NU, :]
                    dve.wait_ge(a_ready.sem, a_ready.at(b, k + 1))
                    dve.wait_ge(u_ready.sem, u_ready.at(b, k + 1))
                    dve.tensor_tensor_scan(u, A[:, k % NA, :], u, 0.0, ALU.mult, ALU.add).then_inc(h_ready.sem, 1)

            def mixer_last(b):
                for d in range(DT):
                    dve.wait_ge(g_summed.sem, g_summed.at(b, NS * DT - DT + d + 1))
                    ps = PY[:, d, :, :].rearrange("p h t -> p (h t)")
                    dst = yz[:, d, DC - 1:]
                    dve.scalar_tensor_tensor(dst, xs[:, d, :], col("d_param", d), ps, ALU.mult, ALU.add).then_inc(m_yd.sem, 1)
                    dve.wait_ge(m_yd.sem, m_yd.at(b, d + 1))
                    dve.tensor_tensor(dst, dst, zs[:, d, :], ALU.mult).then_inc(m_yz.sem, 1)
                for j in range(2):
                    dve.wait_ge(m_out.sem, m_out.at(b, j + 1))
                    dve.tensor_tensor(half(XF, j), X[:, bass.ds(b * T + j * H, H)], PR[:, j, :], ALU.add).then_inc(m_res.sem, 1)

            def ffn(b, stage, f, m):
                if stage == "ln":
                    for j in range(2):
                        dve.wait_ge(f_mean.sem, f_mean.at(b, 2 * f + j + 1))
                        dve.tensor_tensor(half(fc, j), half(XF, j), PF[:, j, :], ALU.subtract).then_inc(f_cent.sem, 1)
                    for j in range(2):
                        dve.wait_ge(f_rs.sem, f_rs.at(b, 2 * f + j + 1))
                        dve.tensor_tensor(half(fc, j), half(fc, j), half(fr, j), ALU.mult).then_inc(f_norm.sem, 1)
                for j in range(2):
                    if stage == "up":
                        n = 2 * MT * f + 2 * m + j
                        dve.wait_ge(f_silu.sem, f_silu.at(b, n + 1))
                        dve.scalar_tensor_tensor(hA[:, j, m, :], PF[:, 1, :], col("s2", m), gs[:, j, :],
                                                 ALU.mult, ALU.mult).then_inc(f_act.sem, 1)
                    elif stage == "down":
                        n = 2 * f + j
                        dve.wait_ge(f_ops.sem, f_ops.at(b, n + 1))
                        dst = XF if f == 0 else XO
                        dve.scalar_tensor_tensor(half(dst, j), PF[:, j, :], col("s3"), half(XF, j),
                                                 ALU.mult, ALU.add).then_inc(f_res.sem, 1)
                        if f == 0:
                            dve.wait_ge(f_res.sem, f_res.at(b, n + 1))
                            if j == 0:
                                dve.tensor_copy(spec[:, bass.ds(b * EFF, EFF)], XF[:, 0:EFF]).then_inc(f_spec.sem, 1)
                                dve.wait_ge(f_spec.sem, f_spec.at(b, 1))
                            dve.tensor_scalar(half(XF, j), half(XF, j), col("ob"), None, ALU.add).then_inc(f_ob.sem, 1)

            def body(b, fb):
                if b is not None:
                    mixer_first(b)
                for s in range(NS):
                    if b is not None:
                        state(b, s)
                    if fb is not None:
                        for unit in SCHED[s]:
                            ffn(fb, *unit)
                if b is not None:
                    mixer_last(b)

            body(0, None)
            with dve.Fori(1, NB) as i:
                body(i, i - 1)
            body(None, NB - 1)

            def step(ins):
                return ins.then_inc(V.sem, 1)

            def pe(name):
                dve.wait_ge(E.sem, E.after(name))

            def own(name):
                dve.wait_ge(V.sem, V.after(name))

            def act_done(name):
                dve.wait_ge(S.sem, S.after(name))

            dve.wait_ge(f_spec.sem, f_spec.at(NB - 1, 1))
            step(dve.memset(qpad, 0.0))
            src = spec[:, :]
            for n in ("o", "i"):
                pe("mean_" + n)
                step(dve.tensor_tensor(t_c, src, Y4[:, 0, 0:NT], ALU.subtract))
                act_done("rs_" + n)
                step(dve.tensor_tensor(t_n, t_c, t_r, ALU.mult))
                own("n_" + n)
                src = t_n
            step(dve.tensor_scalar(t_qa, t_n, col("lna"), None, ALU.mult))
            step(dve.tensor_scalar(t_ka, t_n, col("lnb"), None, ALU.mult))
            pe("v")
            step(dve.tensor_scalar(t_q, Y4[:, 2, 0:NT], col("qb"), None, ALU.add))
            step(dve.tensor_copy(t_k, Y4[:, 2, NT:2 * NT]))
            step(dve.tensor_scalar(t_v, Y4[:, 2, 2 * NT:3 * NT], col("vb"), None, ALU.add))
            heads = C[:, slice(*COL_AT["head_of"])]
            for bd, w in ((bdq, "lqw"), (bdk, "lkw"), (bdv, "lvw")):
                wide = C[:, slice(*COL_AT[w])].unsqueeze(1).broadcast_to([P, NH, HD])
                step(dve.tensor_tensor(bd.rearrange("p (h d) -> p h d", h=NH), wide,
                                       heads.unsqueeze(2).broadcast_to([P, NH, HD]), ALU.mult))
            pe("vv")
            step(dve.tensor_scalar(t_k0, Y4[:, 3, 0:NT], col("lkb"), None, ALU.add))
            step(dve.tensor_scalar(t_vi, Y4[:, 3, NT:2 * NT], col("lvb"), None, ALU.add))
            pe("mean_k")
            step(dve.tensor_tensor(t_c, t_k0, Y4[:, 0, 0:NT], ALU.subtract))
            act_done("rs_k")
            step(dve.scalar_tensor_tensor(t_kn, t_c, col("lnd"), t_r, ALU.mult, ALU.mult))
            own("n_k")
            step(dve.tensor_tensor(kblk.rearrange("p (b h k) -> p b h k", b=NB, h=NH),
                                   t_kn.rearrange("p (b k) -> p b k", b=NB).unsqueeze(2).broadcast_to([P, NB, NH, EFF]),
                                   heads.unsqueeze(1).unsqueeze(3).broadcast_to([P, NB, NH, EFF]), ALU.mult))
            pe("vi_t")
            step(dve.tensor_copy(t_vsb[0:NT, :], Y4[0:NT, 3, 2 * NT:2 * NT + P]))
            pe("rep")
            step(dve.tensor_copy(vrep, PR[:, 0, :]))
            own("v_sb")
            for hf in range(2):
                mask = C[:, COL_AT["vhead_of"][0] + hf * NH:COL_AT["vhead_of"][0] + (hf + 1) * NH]
                step(dve.tensor_tensor(vblk[:, hf * NB * P:(hf + 1) * NB * P].rearrange("p (b h d) -> p b h d", b=NB, h=NH),
                                       vrep.rearrange("p (b h d) -> p b h d", b=NB, h=NH),
                                       mask.unsqueeze(1).unsqueeze(3).broadcast_to([P, NB, NH, HD]), ALU.mult))
            lg = PF[:, 0, 0:NH * EFF].rearrange("p (h k) -> p h k", h=NH)
            pr3 = prob.rearrange("p (h k) -> p h k", h=NH)
            for t in ITERS:
                pe(f"qq{t}")
                step(dve.tensor_scalar(t_q0, Y4[:, 2, 0:NT], col("lqb"), None, ALU.add))
                pe(f"mean_q{t}")
                step(dve.tensor_tensor(t_c, t_q0, Y4[:, 0, 0:NT], ALU.subtract))
                act_done(f"rs_q{t}")
                step(dve.scalar_tensor_tensor(qpad.rearrange("p (b q) -> p b q", b=NB)[:, :, 0:EFF],
                                              t_c.rearrange("p (b q) -> p b q", b=NB), col("lnc"),
                                              t_r.rearrange("p (b q) -> p b q", b=NB), ALU.mult, ALU.mult))
                pe(f"logits{t}")
                step(dve.reduce_max(smax, lg, AX.X))
                own(f"max{t}")
                step(dve.tensor_tensor(pr3, lg, smax.unsqueeze(2).broadcast_to([P, NH, EFF]), ALU.subtract))
                act_done(f"exp{t}")
                step(dve.tensor_reduce(ssum, pr3, AX.X, ALU.add))
                own(f"sum{t}")
                step(dve.reciprocal(ssum, ssum))
                own(f"rec{t}")
                step(dve.tensor_tensor(pr3, pr3, ssum.unsqueeze(2).broadcast_to([P, NH, EFF]), ALU.mult))
                pe(f"pt{t}")
                step(dve.tensor_copy(pT, PF[:, 1, 0:2 * P]))
                pe(f"att{t}")
                step(dve.tensor_copy(att[t], Y4[:, 3, 0:NT]))
                own(f"att{t}")
                if t < 2:
                    step(dve.tensor_tensor(t_q, t_q, att[t], ALU.add))
                if t == 1:
                    step(dve.tensor_tensor(t_d, att[1], att[0], ALU.subtract))
            pe("diff1")
            step(dve.tensor_scalar(tiny[:, 1:2], Y4[:, 2, NT:NT + 1], float(P) / (NB * NH * T * HD), None, ALU.mult))
            own("mean_abs")
            step(dve.tensor_scalar(tiny[:, 2:3], tiny[:, 1:2], 0.1, 0.01, ALU.mult, ALU.add))
            own("limit")
            step(dve.tensor_tensor(tiny[:, 3:4], tiny[:, 1:2], tiny[:, 2:3], ALU.is_lt))
            own("brk")
            step(dve.tensor_scalar(tiny[:, 4:5], tiny[:, 3:4], -1.0, 1.0, ALU.mult, ALU.add))
            step(dve.tensor_scalar(t_d, att[1], tiny[:, 3:4], None, ALU.mult))
            own("old")
            step(dve.scalar_tensor_tensor(att[0], att[2], tiny[:, 4:5], t_d, ALU.mult, ALU.add))
            pe("ow")
            step(dve.scalar_tensor_tensor(x3, Y4[:, 2, 0:NT], col("ob"), spec[:, :], ALU.add, ALU.add))
            own("x3")
            step(dve.tensor_copy(x5, x3))
            pe("mean_f")
            step(dve.tensor_tensor(t_c, x3, Y4[:, 0, 0:NT], ALU.subtract))
            act_done("rs_f")
            step(dve.tensor_tensor(t_n, t_c, t_r, ALU.mult))
            for m in range(MT):
                act_done(f"silu{m}")
                step(dve.scalar_tensor_tensor(f_h0[:, m * NT:(m + 1) * NT], Y4[:, 3, m * NT:(m + 1) * NT], col("s2", m),
                                              f_g[:, m * NT:(m + 1) * NT], ALU.mult, ALU.mult))
            pe("w3")
            step(dve.scalar_tensor_tensor(x5, PF[:, 0, 0:NT], col("s3"), x3, ALU.mult, ALU.add))

        @block.tensor
        def _(te):
            te.wait_ge(w_in, 32)
            te.wait_ge(s_set, 6)

            def mixer_first(b):
                if isinstance(b, int):
                    te.wait_ge(x_in[0], 16)
                for j in range(2):
                    if not isinstance(b, int):
                        te.wait_ge(m_yz.sem, m_yz.at(b, 0))
                    te.matmul(Y4[:, j, :], mean_w[:, :], X[:, bass.ds(b * T + j * H, H)], start=True, stop=True).then_inc(m_mean.sem, 1)
                for j in range(2):
                    te.wait_ge(m_sq.sem, m_sq.at(b, j + 1))
                    te.matmul(Y4[:, 2 + j, :], mean_w[:, :], half(mr, j), start=True, stop=True).then_inc(m_var.sem, 1)
                for n in range(8):
                    m, j = n // 2, n % 2
                    if m == 0:
                        te.wait_ge(m_norm.sem, m_norm.at(b, j + 1))
                    if n >= 4:
                        te.wait_ge(m_evac.sem, m_evac.at(b, n - 3))
                    te.matmul(Y4[:, n % 4, :], mat("w_in", m, P), half(mc, j), start=True, stop=True).then_inc(m_proj.sem, 1)
                te.wait_ge(m_evac.sem, m_evac.at(b, 8))
                for j in range(2):
                    for d in range(DT):
                        te.wait_ge(m_xs.sem, m_xs.at(b, d + 1))
                        last = te.matmul(Y4[0:104, j, :], mat("w_xproj", d, 104), half(xs[:, d, :], j),
                                         start=(d == 0), stop=(d == DT - 1))
                    last.then_inc(m_xp.sem, 1)
                te.wait_ge(m_bc.sem, m_bc.at(b, 2))
                te.wait_ge(m_dr.sem, m_dr.at(b, 2))
                for d in range(DT):
                    for j in range(2):
                        last = te.matmul(PY[:, d, j, :], mat("w_dt", d, P, slice(96, 104)), dr[96:104, j * H:(j + 1) * H],
                                         start=True, stop=True)
                    last.then_inc(m_dps.sem, 1)

            def spread(n, done):
                for j in range(2):
                    last = te.matmul(PR[:, j, :], pick[0:96, n:n + 1].broadcast_to([96, P]), bc[0:96, j * H:(j + 1) * H],
                                     start=True, stop=True)
                last.then_inc(done.sem, 1)

            LAG = 2

            def state(b, s):
                if s == 0:
                    if not isinstance(b, int):
                        te.wait_ge(m_res.sem, m_res.at(b, 0))
                else:
                    te.wait_ge(c_copied.sem, c_copied.at(b, s))
                spread(s, b_ready)
                if s >= LAG:
                    sum_up(b, s - LAG)
                te.wait_ge(u_ready.sem, u_ready.at(b, DT * (s + 1)))
                spread(NS + s, c_ready)

            def sum_up(b, s):
                if s == 0:
                    te.wait_ge(m_soft.sem, m_soft.at(b, 4 * DT))
                for d in range(DT):
                    k = DT * s + d
                    te.wait_ge(g_ready.sem, g_ready.at(b, k + 1))
                    for j in range(2):
                        last = te.matmul(PY[:, d, j, :], mat("ident"), half(U[:, k % NU, :], j),
                                         start=(s == 0), stop=(s == NS - 1))
                    last.then_inc(g_summed.sem, 1)

            def mixer_last(b):
                te.wait_ge(m_yz.sem, m_yz.at(b, DT))
                te.wait_ge(c_copied.sem, c_copied.at(b, NS))
                for j in range(2):
                    for d in range(DT):
                        last = te.matmul(PR[:, j, :], mat("w_out", d, D), yz[:, d, DC - 1 + j * H:DC - 1 + (j + 1) * H],
                                         start=(d == 0), stop=(d == DT - 1))
                    last.then_inc(m_out.sem, 1)

            def ffn(b, stage, f, m):
                if stage == "ln":
                    for j in range(2):
                        if f == 0:
                            te.wait_ge(m_res.sem, m_res.at(b, j + 1))
                        else:
                            te.wait_ge(f_ob.sem, f_ob.at(b, j + 1))
                        te.matmul(PF[:, j, :], mean_w[:, :], half(XF, j), start=True, stop=True).then_inc(f_mean.sem, 1)
                    for j in range(2):
                        te.wait_ge(f_sq.sem, f_sq.at(b, 2 * f + j + 1))
                        te.matmul(PF[:, j, :], mean_w[:, :], half(fr, j), start=True, stop=True).then_inc(f_var.sem, 1)
                for j in range(2):
                    if stage == "up":
                        n = 2 * MT * f + 2 * m + j
                        te.wait_ge(f_norm.sem, f_norm.at(b, 2 * f + 2))
                        if n > 2 * MT * f:
                            te.wait_ge(f_act.sem, f_act.at(b, n))
                        te.matmul(PF[:, 0, :], mat("w1", m, P), half(fc, j), start=True, stop=True)
                        te.matmul(PF[:, 1, :], mat("w2", m, P), half(fc, j), start=True, stop=True).then_inc(f_gu.sem, 1)
                    elif stage in ("h1", "h2"):
                        first = 4 * MT * f + (2 * MT if stage == "h2" else 0)
                        n = first + 2 * m + j
                        src = hA if stage == "h1" else hB
                        if stage == "h1" and m == 0:
                            te.wait_ge(f_act.sem, f_act.at(b, 2 * MT * (f + 1)))
                        elif m == 0:
                            te.wait_ge(f_gelu.sem, f_gelu.at(b, first - 1 + j))
                        else:
                            te.wait_ge(f_gelu.sem, f_gelu.at(b, n - 1))
                        for k in range(MT):
                            lo = MAT_AT[stage][0] + k * HID + m * P
                            last = te.matmul(PF[:, j, :], M[:, lo:lo + P], src[:, j, k, :], start=(k == 0), stop=(k == MT - 1))
                        last.then_inc(f_hps.sem, 1)
                    elif stage == "down":
                        te.wait_ge(f_gelu.sem, f_gelu.at(b, 4 * MT * (f + 1) - 1 + j))
                        for k in range(MT):
                            last = te.matmul(PF[:, j, :], mat("w3", k, D), hA[:, j, k, :], start=(k == 0), stop=(k == MT - 1))
                        last.then_inc(f_ops.sem, 1)

            def body(b, fb):
                if b is not None:
                    if not isinstance(b, int):
                        for n in range(1, NB):
                            te.wait_ge(x_in[n], 16)
                    mixer_first(b)
                for s in range(NS):
                    if b is not None:
                        state(b, s)
                    if fb is not None:
                        for unit in SCHED[s]:
                            ffn(fb, *unit)
                if b is not None:
                    for s in range(NS - LAG, NS):
                        sum_up(b, s)
                    mixer_last(b)

            body(0, None)
            with te.Fori(1, NB) as i:
                body(i, i - 1)
            body(None, NB - 1)

            def mm(out, w, x, **kw):
                kw = {"start": True, "stop": True} | kw
                return te.matmul(out, w, x, **kw)

            def dve(name):
                te.wait_ge(V.sem, V.after(name))

            def done(ins):
                ins.then_inc(E.sem, 1)

            def norm(n, src, w, before=None):
                if before:
                    dve(before)
                done(mm(Y4[:, 0, 0:NT], w, src))
                te.wait_ge(S.sem, S.after("sq_" + n))
                done(mm(Y4[:, 1, 0:NT], w, t_r))

            te.wait_ge(f_spec.sem, f_spec.at(NB - 1, 1))
            te.wait_ge(f_res.sem, f_res.at(NB - 1, 4))
            norm("o", spec[:, :], mean_w[:, :])
            norm("i", t_n, mean_w[:, :], "n_o")
            dve("qa")
            done(mm(Y4[:, 2, 0:NT], mat("qw"), t_qa))
            dve("ka")
            done(mm(Y4[:, 2, NT:2 * NT], mat("kw"), t_ka))
            done(mm(Y4[:, 2, 2 * NT:3 * NT], mat("vw"), t_ka))
            dve("bdk")
            done(mm(Y4[:, 3, 0:NT], bdk, t_k))
            dve("bdv")
            done(mm(Y4[:, 3, NT:2 * NT], bdv, t_v))
            norm("k", t_k0, mat("group"), "k0")
            dve("vi")
            done(te.transpose(Y4[0:NT, 3, 2 * NT:2 * NT + P], t_vi, mat("ident")))
            dve("vi_sb")
            te.wait_ge(rep_in, 16)
            for b in range(NB):
                last = mm(PR[:, 0, b * P:(b + 1) * P], t_rep[0:NT, b * P:(b + 1) * P], t_vsb[0:NT, :])
            done(last)
            dve("vblk1")
            for t in ITERS:
                if t:
                    dve(f"qcur{t - 1}")
                done(mm(Y4[:, 2, 0:NT], bdq, t_q))
                norm(f"q{t}", t_q0, mat("group"), f"q0{t}")
                dve(f"n_q{t}")
                for b in range(NB):
                    last = mm(PF[32 * b:32 * (b + 1), 0, 0:NH * EFF], qpad[:, 32 * b:32 * (b + 1)],
                              kblk[:, b * NH * EFF:(b + 1) * NH * EFF], tile_position=(0, 32 * b))
                done(last)
                dve(f"prob{t}")
                for hf in range(2):
                    last = te.transpose(PF[:, 1, hf * P:(hf + 1) * P], prob[:, hf * P:(hf + 1) * P], mat("ident"))
                done(last)
                dve(f"pt{t}")
                for b in range(NB):
                    for hf in range(2):
                        last = mm(Y4[:, 3, b * EFF:(b + 1) * EFF], vblk[:, (hf * NB + b) * P:(hf * NB + b + 1) * P],
                                  pT[:, hf * P + 32 * b:hf * P + 32 * b + EFF], start=(hf == 0), stop=(hf == 1))
                done(last)
                if t == 1:
                    te.wait_ge(S.sem, S.after("abs1"))
                    done(mm(Y4[:, 2, NT:NT + 1], mean_w[:, :], tiny[:, 0:1]))
            dve("sel")
            done(mm(Y4[:, 2, 0:NT], mat("ow"), att[0]))
            norm("f", x3, mean_w[:, :], "x3")
            dve("n_f")
            for m in range(MT):
                mm(Y4[:, 2, m * NT:(m + 1) * NT], mat("w1", m, P), t_n)
                last = mm(Y4[:, 3, m * NT:(m + 1) * NT], mat("w2", m, P), t_n)
            done(last)

            def hidden(ps, stage, src):
                for m in range(MT):
                    for k in range(MT):
                        lo = MAT_AT[stage][0] + k * HID + m * P
                        last = mm(ps[:, m * NT:(m + 1) * NT], M[:, lo:lo + P], src[:, k * NT:(k + 1) * NT],
                                  start=(k == 0), stop=(k == MT - 1))
                done(last)

            dve(f"act{MT - 1}")
            hidden(Y4[:, 0, :], "h1", f_h0)
            te.wait_ge(S.sem, S.after(f"gelu_a{MT - 1}"))
            hidden(Y4[:, 1, :], "h2", f_h1)
            te.wait_ge(S.sem, S.after(f"gelu_b{MT - 1}"))
            for k in range(MT):
                last = mm(PF[:, 0, 0:NT], mat("w3", k, D), f_h2[:, k * NT:(k + 1) * NT], start=(k == 0), stop=(k == MT - 1))
            done(last)


def rows(v, n=1):
    v = np.asarray(v)
    v = v.reshape(n, P, -1)
    return np.ascontiguousarray(v.transpose(1, 0, 2).reshape(P, -1))


def layout(i):
    f = lambda n: np.asarray(i[n])
    mats = np.zeros((P, NMAT), np.float32)
    cols = np.zeros((P, NCOL), np.float32)

    def m(name, v):
        lo, hi = MAT_AT[name]
        mats[:, lo:hi] = v

    def c(name, v):
        lo, hi = COL_AT[name]
        cols[:, lo:hi] = v

    m("w_in", f("L0_attn_a_W_in"))
    xp = f("L0_attn_a_W_xproj").reshape(DT, P, DTR + 2 * NS)
    lo = MAT_AT["w_xproj"][0]
    for d in range(DT):
        at = lo + d * 104
        mats[:, at:at + 32] = xp[d][:, DTR:]
        mats[:, at + 64:at + 96] = xp[d][:, DTR:]
        mats[:, at + 96:at + 104] = xp[d][:, :DTR]
    m("w_out", rows(f("L0_attn_a_W_out"), DT))
    lo, hi = MAT_AT["w_dt"]
    mats[96:104, lo:hi] = f("L0_attn_a_W_dt")
    m("w1", f("L0_ffn_w1_w").T)
    m("w2", f("L0_ffn_w2_w").T)
    m("h1", rows(f("L0_ffn_h1_w").T, MT))
    m("h2", rows(f("L0_ffn_h2_w").T, MT))
    m("w3", rows(f("L0_ffn_w3_w").T, MT))
    for name in ("qw", "kw", "vw", "ow"):
        m(name, f("L0_attn_b_" + name).T)
    part = np.arange(P)
    m("ident", part[:, None] == part[None, :])
    m("group", np.where(part[:, None] // HD == part[None, :] // HD, np.float32(1.0 / HD), np.float32(0)))

    c("conv_w", rows(f("L0_attn_a_conv_w"), DT))
    c("conv_b", rows(f("L0_attn_a_conv_b"), DT))
    c("b_dt", rows(f("L0_attn_a_b_dt"), DT))
    c("a_log", rows(f("L0_attn_a_A_log"), DT))
    c("d_param", rows(f("L0_attn_a_D_param"), DT))
    c("s1", rows(f("L0_ffn_w1_s"), MT))
    c("s2", rows(f("L0_ffn_w2_s"), MT))
    c("sh1", rows(f("L0_ffn_h1_s"), MT))
    c("sh2", rows(f("L0_ffn_h2_s"), MT))
    c("s3", rows(f("L0_ffn_w3_s")))
    for name, key in (("qb", "qb"), ("vb", "vb"), ("ob", "ob"), ("lna", "lna_w"), ("lnb", "lnb_w")):
        c(name, rows(f("L0_attn_b_" + key)))
    for name, key in (("lnc", "lnc_w"), ("lnd", "lnd_w"), ("lqb", "lqb"), ("lkb", "lkb"), ("lvb", "lvb")):
        c(name, np.tile(f("L0_attn_b_" + key), NH)[:, None])
    for name in ("lqw", "lkw", "lvw"):
        c(name, np.tile(f("L0_attn_b_" + name).T, (NH, 1)))
    n = np.arange(2 * NS)
    c("pick", (part[:, None] == n[None, :]) | (part[:, None] == 64 + n[None, :]))
    heads = np.arange(NH)
    c("head_of", part[:, None] // HD == heads[None, :])
    c("vhead_of", np.concatenate([part[:, None] // EFF + (NH // 2) * hf == heads[None, :] for hf in range(2)], axis=1))
    token = np.arange(NT)
    rep = np.concatenate([token[:, None] == b * EFF + part[None, :] % EFF for b in range(NB)], axis=1)
    return mats, cols, rep.astype(np.float32)


def kernel(**inputs):
    import concourse.bacc as bacc
    from concourse.bass_utils import run_bass_kernel_spmd

    x = np.asarray(inputs["L0_attn_a_x"])
    mats, cols, rep = layout(inputs)
    arrays = {"xT": np.ascontiguousarray(x.reshape(NB * T, D).T), "mats": mats, "cols": cols, "rep": rep}
    nc = bacc.Bacc("TRN2", target_bir_lowering=False, num_devices=1)
    args = [nc.dram_tensor(n, a.shape, mybir.dt.from_np(a.dtype), kind="ExternalInput").ap() for n, a in arrays.items()]
    out = nc.dram_tensor("outT", (D, NB * T), mybir.dt.float32, kind="ExternalOutput").ap()
    hybrid_kernel(nc, *args, out)
    r = run_bass_kernel_spmd(nc, [arrays], core_ids=[0])
    return np.ascontiguousarray(r.results[0]["outT"].T).reshape(NB, T, D)
```

```python
from contextlib import ExitStack

import numpy as np

import concourse.bass as bass
from concourse import mybir

P = 128
D = 128
NB, T = 4, 1024
H = 512
NCH = NB * T // H
DI, NS, DC, DTR = 256, 16, 4, 8
DT = DI // P
HID = 512
MT = HID // P
NH, HD, EFF = 16, 8, 16
NT = NB * EFF
EPS = 1e-5
NP = NS // 2
NA = 4
NU = 3
LAG = 2

MATS = [("w_in", 2 * DI), ("w_xproj", DT * 104), ("w_out", DT * D), ("w_dt", DI), ("qw", D), ("kw", D), ("vw", D),
        ("ow", D), ("ident", P), ("group", P)]
FMATS = [("w1", HID), ("w2", HID), ("h1", MT * HID), ("h2", MT * HID), ("w3", MT * D)]
COLS = [("conv_w", DT * DC), ("conv_b", DT), ("b_dt", DT), ("a_log", DT * NS), ("d_param", DT), ("s1", MT), ("s2", MT),
        ("sh1", MT), ("sh2", MT), ("s3", 1), ("qb", 1), ("vb", 1), ("ob", 1), ("lna", 1), ("lnb", 1), ("lnc", 1),
        ("lnd", 1), ("lqb", 1), ("lkb", 1), ("lvb", 1), ("lqw", HD), ("lkw", HD), ("lvw", HD), ("pick", 2 * NS),
        ("head_of", NH), ("vhead_of", 2 * NH)]


def offsets(parts):
    at, out = 0, {}
    for name, n in parts:
        out[name] = (at, at + n)
        at += n
    return out, at


MAT_AT, NMAT = offsets(MATS)
FMAT_AT, NFMAT = offsets(FMATS)
COL_AT, NCOL = offsets(COLS)


class Signal:

    def __init__(self, ctx, nc, name, per, start=0):
        self.sem, self.per, self.start = ctx.enter_context(nc.semaphore(name)), per, start

    def at(self, c, n):
        return c * self.per + n + self.start


class Steps:

    def __init__(self, ctx, nc, name, names):
        self.sem = ctx.enter_context(nc.semaphore(name))
        self.names = list(names)

    def after(self, name):
        return self.names.index(name) + 1


DVE_ORDER = """
cin keep yadd yz bdr res bhi fc0 blo fn0 fx0 dl mu0 cent hi0 lo0 mu1 dx hi1 mu2 lo1 hi2 u0 mu3 hi3
lo2 take lo3 scan0 u1 lo4 lo5 scan1 lo6 lo7 u2 scan2 dskip lo8 lo9 lo10 lo11 u3 fres0 scan3 fc1 u4
norm fn1 fx1 scan4 mu12 u5 mu13 hi12 lo12 hi13 mu14 lo13 hi14 lo14 mu15 hi15 lo15 scan5 u6 lo16 lo17
scan6 lo18 lo19 tap0 u7 tap1 scan7 lo20 lo21 lo22 lo23 tap2 tap3 fres1
""".split()
ACT_ORDER = """
sx fs0 sr0 sa0 fr0 sr1 sa1 se sl si0 si1 sq si2 si3 dec0 cc0 dec1 ge4 ge5 ge6 cc1 ge7 dec2 ge8 ge9
cc2 ge10 ge11 dec3 cc3 dec4 fs1 rs fr1 dec5 cc4 si12 si13 sz cc5 si14 ev0 si15 dec6 ge16 ge17 ev1
ge18 cc6 ge19 dec7 ge20 ge21 cc7 ge22 ge23 ev2 ev3
""".split()
PE_ORDER = """
sum6 sum7 xp out fm0 dt0 fv0 B0 dt1 mean up0 up1 up2 up3 C0 B1 h4 h5 C1 h6 h7 sum0 B2 h8 h9 C2 h10
h11 var B3 dn0 C3 B4 fm1 sum1 fv1 C4 proj0 up12 B5 sum2 up13 sum3 C5 up14 up15 B6 proj1 proj2 h16
h17 h18 C6 h19 B7 sum4 h20 proj3 h21 C7 h22 h23 sum5 dn1
""".split()
POOL_ORDER = """
g0 ga0 g1 ga1 g2 ga2 g3 ga3 g4 ga4 g5 ga5 g6 ga6 g7 ga7
""".split()


BEHIND = ("keep", "sum6", "sum7", "yadd", "yz", "out", "res", "fm", "fc", "fs", "fv", "fr", "fn", "fx", "up", "si", "mu", "hi",
          "lo", "h", "ge", "dn", "fres")
AHEAD = ("mean", "cent", "sq", "var", "rs", "norm", "proj", "ev", "cin", "tap")


def split(name):
    stem = name.rstrip("0123456789")
    return stem, int(name[len(stem):] or 0)


def play(order, units, i, behind=True, state=True, ahead=True):
    for name in order:
        stem, k = split(name)
        if name in BEHIND or stem in BEHIND:
            if behind:
                units[stem](i - 1, k)
        elif stem in AHEAD:
            if ahead:
                units[stem](i + 1, k)
        elif state:
            units[stem](i, k)


def first_ffn(order, units):
    stages = ["fm", "fc", "fs", "fv", "fr", "fn", "fx"] + ["up", "si", "mu", "hi", "lo"] + ["h", "ge"] + ["dn", "fres"]
    own = [n for n in order if split(n)[0] in stages and n not in ("fm1", "fc1", "fs1", "fv1", "fr1", "fn1", "fx1", "dn1", "fres1")]
    for name in sorted((n for n in own if split(n)[1] < 3 * MT), key=lambda n: rank(*split(n))):
        stem, k = split(name)
        units[stem](NCH, k)


def rank(stem, k):
    if stem in ("fm", "fc", "fs", "fv", "fr", "fn", "fx"):
        return -1, ("fm", "fc", "fs", "fv", "fr", "fn", "fx").index(stem)
    if stem in ("dn", "fres"):
        return 3 * MT, ("dn", "fres").index(stem)
    return k, ("up", "si", "mu", "hi", "h", "ge", "lo").index(stem)


def hybrid_kernel(nc, xT, mats, fmats, cols, rep, outT):
    fp32, f32r, i32 = mybir.dt.float32, mybir.dt.float32r, mybir.dt.int32
    ALU, ACT, AX = mybir.AluOpType, mybir.ActivationFunctionType, mybir.AxisListType

    ctx = ExitStack()
    with ctx:
        def sb(name, shape, dt=fp32):
            return ctx.enter_context(nc.sbuf_tensor(name, shape, dt))

        def ps(name, shape):
            return ctx.enter_context(nc.psum_tensor(name, shape, fp32))

        def signal(name, per, start=0):
            return Signal(ctx, nc, name, per, start)

        def sem(name):
            return ctx.enter_context(nc.semaphore(name))

        M = sb("M", [P, NMAT])
        WH = sb("WH", [P, NFMAT], f32r)
        WL = sb("WL", [P, NFMAT], f32r)
        C = sb("C", [P, NCOL])
        mean_w = sb("mean_w", [P, P])
        eps_col = sb("eps_col", [P, 1])
        one_col = sb("one_col", [P, 1])
        w_rest = sb("w_rest", [P, 2])
        w_split = sb("w_split", [P, 1], i32)
        pick = sb("pick", [P, 2 * NS], f32r)
        a_neg = sb("a_neg", [P, DT * NS])
        XM = sb("XM", [P, H])
        mc = sb("mc", [P, H])
        mr = sb("mr", [P, H])
        xb = sb("xb", [P, DT, H + DC - 1])
        cv = sb("cv", [P, DT, H])
        zr = sb("zr", [P, DT, H])
        xs = sb("xs", [P, DT, H])
        zs = sb("zs", [P, DT, H])
        dl = sb("dl", [P, DT, H])
        dx = sb("dx", [P, DT, H])
        bc = sb("bc", [P, H], f32r)
        dr = mc
        A = sb("A", [P, NA, DT, 2, H])
        U = sb("U", [P, NU, DT, 2, H])
        cs = sb("cs", [P, 2, H])
        tail = sb("tail", [P, NCH + NB, DT, DC - 1])
        state = sb("state", [P, NCH + NB, NP * DT * 2])
        state_in = sb("state_in", [P, NP * DT * 2])
        state_out = sb("state_out", [P, NP * DT * 2])
        XR = sb("XR", [P, H])
        yd = sb("yd", [P, DT, H])
        XF = sb("XF", [P, H])
        fc = sb("fc", [P, H])
        fr = sb("fr", [P, H])
        XO = fr
        xh = sb("xh", [P, H], f32r)
        xl = sb("xl", [P, H], f32r)
        ht = sb("ht", [P, 2, H])
        hAh = sb("hAh", [P, MT, H], f32r)
        hAl = sb("hAl", [P, MT, H], f32r)
        hBh = sb("hBh", [P, MT, H], f32r)
        hBl = sb("hBl", [P, MT, H], f32r)
        spec = sb("spec", [P, NCH * EFF])

        PY = ps("PY", [P, DT, H])
        PR = ps("PR", [P, 2, H])
        PN = ps("PN", [P, 2, H])
        PF = ps("PF", [P, 2, H])

        def mat(name, k=0, w=None, rows=slice(0, P)):
            lo, hi = MAT_AT[name]
            w = w or hi - lo
            return M[rows, lo + k * w:lo + (k + 1) * w]

        def col(name, k=0, w=1):
            lo, _ = COL_AT[name]
            return C[:, lo + k * w:lo + (k + 1) * w]

        cols_in, mats_in, fmats_in = sem("cols_in"), sem("mats_in"), sem("fmats_in")
        xm_in, xr_in, rep_in, stored = sem("xm_in"), sem("xr_in"), sem("rep_in"), sem("stored")
        s_set, s_aneg, s_pick = sem("constants_set"), sem("a_neg_set"), sem("pick_set")
        s_wh, s_wl, s_rest, s_count, s_split = sem("w_high"), sem("w_low"), sem("w_rest"), sem("w_count"), sem("w_split_known")
        m_mean, m_cent, m_sq, m_var = signal("m_mean", 1), signal("m_cent", 1), signal("m_sq", 1), signal("m_var", 1)
        m_ln, m_rs, m_norm = signal("m_ln", 1), signal("m_rs", 1), signal("m_norm", 1)
        m_proj, m_evac = signal("m_proj", 2 * DT), signal("m_evac", 2 * DT)
        m_tail, m_conv, m_kept = signal("m_tail", 1), signal("m_conv", DC * DT), signal("m_kept", 1)
        m_xs, m_zs, m_xp = signal("m_xs", 1), signal("m_zs", 1), signal("m_xp", 1)
        m_dr, m_hi, m_bc, m_dps = signal("m_dr", 1), signal("m_hi", 1), signal("m_bc", 1), signal("m_dps", DT)
        m_abs, m_relu, m_exp, m_soft = signal("m_abs", DT), signal("m_relu", DT), signal("m_exp", 1), signal("m_soft", 1)
        m_dl, m_dx, m_skip = signal("m_dl", 1), signal("m_dx", 1), signal("m_skip", DT)
        b_ready, c_ready, c_copied = signal("b_ready", NP), signal("c_ready", NP), signal("c_copied", NP)
        a_ready = signal("a_ready", 2 * DT * NP)
        u_ready, h_scan, h_ready = signal("u_ready", NP), signal("h_scan", 2 * DT * NP), signal("h_ready", NP)
        g_prod, g_ready, g_summed = signal("g_prod", NP), signal("g_ready", NP), signal("g_summed", NP)
        m_take, m_keep = signal("m_take", 1), signal("m_keep", 1)
        m_yd, m_yz, m_out, m_res = signal("m_yd", 1), signal("m_yz", 1), signal("m_out", 1), signal("m_res", 1)
        f_mean, f_cent, f_sq, f_var = signal("f_mean", 2), signal("f_cent", 2), signal("f_sq", 2), signal("f_var", 2)
        f_ln, f_rs, f_norm, f_xh, f_xl = (signal(n, 2) for n in ("f_ln", "f_rs", "f_norm", "f_xh", "f_xl"))
        f_gu, f_silu, f_mul, f_hi = (signal(n, 2 * MT) for n in ("f_gu", "f_silu", "f_mul", "f_hi"))
        f_lo = signal("f_lo", 6 * MT)
        f_hps, f_gelu = signal("f_hps", 4 * MT), signal("f_gelu", 8 * MT)
        f_ops, f_res, f_ob, f_spec = signal("f_ops", 2), signal("f_res", 2, start=1), signal("f_ob", 1), signal("f_spec", 1)
        xo_free = signal("xo_free", 1, start=1)

        ITERS = range(3)
        V = Steps(ctx, nc, "attn_dve", ["zero", "c_o", "n_o", "c_i", "n_i", "qa", "ka", "q", "k", "v", "bdq", "bdk", "bdv", "k0", "vi",
                                        "c_k", "n_k", "kblk", "vi_sb", "v_sb", "vblk0", "vblk1"]
                  + [f"{n}{t}" for t in ITERS for n in ("q0", "c_q", "n_q", "max", "sub", "sum", "rec", "prob", "pt", "att")
                     + (("qcur",) if t < 2 else ()) + (("diff", ) if t == 1 else ())]
                  + ["mean_abs", "limit", "brk", "keep", "old", "sel", "x3"])
        S = Steps(ctx, nc, "attn_act", ["sq_o", "ln_o", "rs_o", "sq_i", "ln_i", "rs_i", "sq_k", "ln_k", "rs_k"]
                  + [f"{n}{t}" for t in ITERS for n in ("sq_q", "ln_q", "rs_q", "exp") + (("abs",) if t == 1 else ())])
        E = Steps(ctx, nc, "attn_pe", ["mean_o", "var_o", "mean_i", "var_i", "q", "k", "v", "kk", "vv", "mean_k", "var_k", "vi_t", "rep"]
                  + [f"{n}{t}" for t in ITERS for n in ("qq", "mean_q", "var_q", "logits", "pt", "att") + (("diff",) if t == 1 else ())]
                  + ["ow"])

        AT = A[:, :, :, :, :].rearrange("p a d s t -> p (a d s t)")
        at_used = [0]

        def part(n):
            at_used[0] += n
            return AT[:, at_used[0] - n:at_used[0]]

        t_c, t_r, t_n, t_qa, t_ka = (part(NT) for _ in range(5))
        t_q, t_k, t_v, t_k0, t_kn, t_vi, t_q0, t_qn = (part(NT) for _ in range(8))
        bdq, bdk, bdv = (part(P) for _ in range(3))
        t_vsb = part(P)
        t_rep = part(NB * P)
        qpad = part(NB * 32)
        kblk = part(NB * NH * EFF)
        vrep = part(NB * P)
        vblk = part(2 * NB * P)
        prob = part(NH * EFF)
        pT = part(2 * P)
        att = [part(NT) for _ in ITERS]
        t_d, t_old = part(NT), part(NT)
        tiny = part(8)
        smax, ssum = part(NH), part(NH)
        x3, x5 = part(NT), part(NT)
        Y4 = {0: PY[:, 0, :], 1: PY[:, 1, :], 2: PN[:, 0, :], 3: PN[:, 1, :]}
        staged = U[:, :, :, :, :].rearrange("p a d s t -> p (a d s t)")[:, 0:NFMAT]

        block = ctx.enter_context(nc.Block())

        def place(k):
            f, r = divmod(k, 3 * MT)
            layer, m = divmod(r, MT)
            return f, layer, m, (MT * f + m if layer == 0 else k - MT * (f + 1))

        def tokens(c):
            return NT if isinstance(c, int) and c == NCH else H

        def later(c):
            return not isinstance(c, int) or c > 0

        @block.sync
        def _(sp):
            def load_ahead(c):
                if later(c):
                    sp.wait_ge(m_cent.sem, m_cent.at(c, 0))
                sp.dma_start(XM[:, :], xT[:, bass.ds(c * H, H)]).then_inc(xm_in, 16)

            def load_residual(c):
                if later(c):
                    sp.wait_ge(m_res.sem, m_res.at(c, 0))
                sp.dma_start(XR[:, :], xT[:, bass.ds(c * H, H)]).then_inc(xr_in, 16)

            def store(c, skip):
                sp.wait_ge(f_res.sem, f_res.at(c, 2))
                sp.dma_start(outT[:, bass.ds(c * H + skip, H - skip)], XO[:, skip:H]).then_inc(stored, 16)
                sp.wait_ge(stored, 16 * (c + 1))
                sp.sem_inc(xo_free.sem, 1)

            load_ahead(0)
            sp.dma_start(C[:, :], cols).then_inc(cols_in, 16)
            sp.dma_start(M[:, :], mats).then_inc(mats_in, 16)
            load_residual(0)
            sp.dma_start(staged, fmats).then_inc(fmats_in, 16)
            load_ahead(1)
            load_ahead(2)
            with sp.Fori(1, NB + 1) as i:
                load_residual(i)
                load_ahead(i + 2)
                store(i - 1, EFF)
            for i in range(NB + 1, NCH):
                load_residual(i)
                if i + 2 < NCH:
                    load_ahead(i + 2)
                store(i - 1, 0)
            sp.wait_ge(h_scan.sem, h_scan.at(NCH, 0))
            sp.dma_start(t_rep[0:NT, :], rep).then_inc(rep_in, 16)
            store(NCH - 1, 0)
            sp.wait_ge(f_res.sem, f_res.at(NCH, 1))
            sp.dma_start(outT.rearrange("p (b t) -> p b t", t=H)[:, 0:NB, 0:EFF],
                         x5.rearrange("p (b t) -> p b t", b=NB)).then_inc(stored, 16)
            sp.wait_ge(stored, 16 * (NCH + 1))

        @block.gpsimd
        def _(pool):
            pool.memset(mean_w[:, :], 1.0 / P).then_inc(s_set, 1)
            pool.memset(eps_col[:, :], EPS).then_inc(s_set, 1)
            pool.memset(one_col[:, :], 1.0).then_inc(s_set, 1)
            pool.memset(bc[:, :].bitcast(fp32), 0.0).then_inc(s_set, 1)
            pool.memset(tail[:, 0:NB], 0.0).then_inc(s_set, 1)
            pool.memset(state[:, 0:NB], 0.0).then_inc(s_set, 1)
            pool.sem_inc(xo_free.sem, 1)
            pool.sem_inc(f_res.sem, 1)

            both = cs[:, :, :].rearrange("p s t -> p (s t)").unsqueeze(1).broadcast_to([P, DT, 2 * H])

            def g(c, p):
                flat = U[:, p % NU, :, :, :].rearrange("p d s t -> p d (s t)")
                pool.wait_ge(c_copied.sem, c_copied.at(c, p + 1))
                pool.wait_ge(h_ready.sem, h_ready.at(c, p + 1))
                pool.tensor_tensor(flat, flat, both, ALU.mult).then_inc(g_prod.sem, 1)

            def ga(c, p):
                u = U[:, p % NU, :, :, :]
                pool.wait_ge(g_prod.sem, g_prod.at(c, p + 1))
                pool.tensor_tensor(u[:, :, 0, :], u[:, :, 0, :], u[:, :, 1, :], ALU.add).then_inc(g_ready.sem, 1)

            units = {"g": g, "ga": ga}
            play(POOL_ORDER, units, 0, behind=False)
            with pool.Fori(1, NCH - 1) as i:
                play(POOL_ORDER, units, i)
            play(POOL_ORDER, units, NCH - 1, ahead=False)

        @block.scalar
        def _(act):
            act.wait_ge(cols_in, 16)
            act.wait_ge(s_set, 6)
            act.activation(a_neg[:, :], C[:, slice(*COL_AT["a_log"])], ACT.Exp).then_inc(s_aneg, 1)
            loaded = [None]

            def tables(name):
                if name == "ln" and loaded[0] != "ln":
                    act.preload_act_table_set("natural_log_exp_and_others")
                loaded[0] = name

            def rsqrt(src, dst, ln, rs, c, n, from_pe):
                tables("ln")
                act.wait_ge(from_pe.sem, from_pe.at(c, n + 1))
                act.activation(dst, src, ACT.Ln, bias=eps_col[:, :]).then_inc(ln.sem, 1)
                act.wait_ge(ln.sem, ln.at(c, n + 1))
                act.activation(dst, dst, ACT.Exp, scale=-0.5).then_inc(rs.sem, 1)

            def sq(c, _):
                act.wait_ge(m_cent.sem, m_cent.at(c, 1))
                act.activation(mr[:, :], mc[:, :], ACT.Square).then_inc(m_sq.sem, 1)

            def rs(c, _):
                rsqrt(PN[:, 1, :], mr[:, :], m_ln, m_rs, c, 0, m_var)

            def ev(c, m):
                act.wait_ge(m_proj.sem, m_proj.at(c, m + 1))
                if later(c):
                    prior = m_kept if m < DT else m_zs
                    act.wait_ge(prior.sem, prior.at(c, 0))
                dst = xb[:, m, DC - 1:] if m < DT else zr[:, m - DT, :]
                act.activation(dst, PN[:, m % 2, :], ACT.Copy).then_inc(m_evac.sem, 1)

            def sx(c, _):
                tables("silu")
                act.wait_ge(m_conv.sem, m_conv.at(c, DC * DT))
                if later(c):
                    act.wait_ge(m_skip.sem, m_skip.at(c, 0))
                    act.wait_ge(m_dx.sem, m_dx.at(c, 0))
                    act.wait_ge(m_xp.sem, m_xp.at(c, 0))
                act.activation(xs[:, :, :], cv[:, :, :], ACT.Silu).then_inc(m_xs.sem, 1)

            def sz(c, _):
                tables("silu")
                act.wait_ge(m_evac.sem, m_evac.at(c, 2 * DT))
                if later(c):
                    act.wait_ge(m_yz.sem, m_yz.at(c, 0))
                act.activation(zs[:, :, :], zr[:, :, :], ACT.Silu).then_inc(m_zs.sem, 1)

            def sa(c, d):
                act.wait_ge(m_dps.sem, m_dps.at(c, d + 1))
                if later(c):
                    act.wait_ge(u_ready.sem, u_ready.at(c, 0))
                act.activation(dx[:, d, :], PN[:, d, :], ACT.Abs, bias=col("b_dt", d)).then_inc(m_abs.sem, 1)

            def sr(c, d):
                act.wait_ge(m_dps.sem, m_dps.at(c, d + 1))
                if later(c):
                    act.wait_ge(a_ready.sem, a_ready.at(c, 0))
                    act.wait_ge(m_dx.sem, m_dx.at(c, 0))
                act.activation(dl[:, d, :], PN[:, d, :], ACT.Relu, bias=col("b_dt", d)).then_inc(m_relu.sem, 1)

            def se(c, _):
                tables("ln")
                act.wait_ge(m_abs.sem, m_abs.at(c, DT))
                act.activation(dx[:, :, :], dx[:, :, :], ACT.Exp, scale=-1.0).then_inc(m_exp.sem, 1)

            def sl(c, _):
                tables("ln")
                act.wait_ge(m_exp.sem, m_exp.at(c, 1))
                act.activation(dx[:, :, :], dx[:, :, :], ACT.Ln, bias=one_col[:, :]).then_inc(m_soft.sem, 1)

            def dec(c, p):
                tables("ln")
                act.wait_ge(m_dl.sem, m_dl.at(c, 1))
                if p == 0 and not later(c):
                    act.wait_ge(s_aneg, 2)
                if p >= NA or later(c):
                    act.wait_ge(h_scan.sem, h_scan.at(c, 2 * DT * (p - NA + 1)))
                for d in range(DT):
                    for s in range(2):
                        n = d * NS + 2 * p + s
                        act.activation(A[:, p % NA, d, s, :], dl[:, d, :], ACT.Exp, scale=a_neg[:, n:n + 1]).then_inc(a_ready.sem, 1)

            def cc(c, p):
                act.wait_ge(c_ready.sem, c_ready.at(c, p + 1))
                if p or later(c):
                    act.wait_ge(g_prod.sem, g_prod.at(c, p))
                act.activation(cs[:, :, :], PR[:, :, :], ACT.Copy).then_inc(c_copied.sem, 1)

            def fs(c, f):
                n = tokens(c)
                act.wait_ge(f_cent.sem, f_cent.at(c, f + 1))
                if f == 0:
                    act.wait_ge(xo_free.sem, xo_free.at(c, 0))
                act.activation(fr[:, 0:n], fc[:, 0:n], ACT.Square).then_inc(f_sq.sem, 1)

            def fr_(c, f):
                n = tokens(c)
                rsqrt(PF[:, 1, 0:n], fr[:, 0:n], f_ln, f_rs, c, f, f_var)

            def si(c, k):
                f, _, m, nth = place(k)
                n = tokens(c)
                tables("silu")
                act.wait_ge(f_gu.sem, f_gu.at(c, nth + 1))
                if k >= 2:
                    act.wait_ge(f_lo.sem, f_lo.at(c, k - 1))
                act.activation(ht[:, k % 2, 0:n], PF[:, 0, 0:n], ACT.Silu, scale=col("s1", m)).then_inc(f_silu.sem, 1)

            def ge(c, k):
                f, layer, m, nth = place(k)
                n = tokens(c)
                tables("gelu")
                src, scale = PF[:, m % 2, 0:n], col(("sh1", "sh2")[layer - 1], m)
                act.wait_ge(f_hps.sem, f_hps.at(c, nth + 1))
                act.activation((hBh, hAh)[layer - 1][:, m, 0:n], src, ACT.Gelu, scale=scale).then_inc(f_gelu.sem, 1)
                act.wait_ge(f_lo.sem, f_lo.at(c, k - 1))
                act.activation(ht[:, k % 2, 0:n], src, ACT.Gelu, scale=scale).then_inc(f_gelu.sem, 1)

            units = {"sq": sq, "rs": rs, "ev": ev, "sx": sx, "sz": sz, "sa": sa, "sr": sr, "se": se, "sl": sl, "dec": dec,
                     "cc": cc, "fs": fs, "fr": fr_, "si": si, "ge": ge}
            play(ACT_ORDER, units, -1, behind=False, state=False)
            play(ACT_ORDER, units, 0, behind=False)
            loaded[0] = None
            with act.Fori(1, NCH - 1) as i:
                play(ACT_ORDER, units, i)
            loaded[0] = None
            play(ACT_ORDER, units, NCH - 1, ahead=False)
            play(ACT_ORDER, units, NCH, state=False, ahead=False)
            tables("ln")

            def a_rsqrt(pe_step, n, src, w):
                act.wait_ge(E.sem, E.after(pe_step))
                act.activation(w, src, ACT.Ln, bias=eps_col[:, :]).then_inc(S.sem, 1)
                act.wait_ge(S.sem, S.after("ln_" + n))
                act.activation(w, w, ACT.Exp, scale=-0.5).then_inc(S.sem, 1)

            def a_square(dve_step):
                act.wait_ge(V.sem, V.after(dve_step))
                act.activation(t_r, t_c, ACT.Square).then_inc(S.sem, 1)

            for n in ("o", "i", "k"):
                a_square("c_" + n)
                a_rsqrt("var_" + n, n, Y4[1][:, 0:NT], t_r)
            for t in ITERS:
                a_square(f"c_q{t}")
                a_rsqrt(f"var_q{t}", f"q{t}", Y4[1][:, 0:NT], t_r)
                act.wait_ge(V.sem, V.after(f"sub{t}"))
                act.activation(prob, prob, ACT.Exp, scale=float(HD) ** -0.5).then_inc(S.sem, 1)
                if t == 1:
                    act.wait_ge(V.sem, V.after("diff1"))
                    act.activation(t_old, t_d, ACT.Abs, accum_out=tiny[:, 0:1]).then_inc(S.sem, 1)
            first_ffn(ACT_ORDER, units)

        @block.vector
        def _(dve):
            dve.wait_ge(cols_in, 16)
            dve.wait_ge(s_set, 6)
            dve.tensor_copy(pick[:, :], C[:, slice(*COL_AT["pick"])]).then_inc(s_pick, 1)
            dve.wait_ge(s_aneg, 1)
            dve.tensor_scalar(a_neg[:, :], a_neg[:, :], -1.0, None, ALU.mult).then_inc(s_aneg, 1)

            def cent(c, _):
                dve.wait_ge(m_mean.sem, m_mean.at(c, 1))
                if later(c):
                    dve.wait_ge(m_dps.sem, m_dps.at(c, 0))
                dve.tensor_tensor(mc[:, :], XM[:, :], PN[:, 0, :], ALU.subtract).then_inc(m_cent.sem, 1)

            def norm(c, _):
                dve.wait_ge(m_rs.sem, m_rs.at(c, 1))
                dve.tensor_tensor(mc[:, :], mc[:, :], mr[:, :], ALU.mult).then_inc(m_norm.sem, 1)

            def cin(c, _):
                if later(c):
                    dve.wait_ge(m_kept.sem, m_kept.at(c, 0))
                dve.tensor_copy(xb[:, :, 0:DC - 1], tail[:, bass.ds(c, 1), :, :].rearrange("p a d t -> p (a d) t")).then_inc(m_tail.sem, 1)

            def tap(c, k):
                for d in range(DT):
                    w = col("conv_w", DC * d + k)
                    src = xb[:, d, k:k + H]
                    if k == 0:
                        dve.wait_ge(m_evac.sem, m_evac.at(c, d + 1))
                        dve.wait_ge(m_tail.sem, m_tail.at(c, 1))
                        if later(c):
                            dve.wait_ge(m_xs.sem, m_xs.at(c, 0))
                        dve.tensor_scalar(cv[:, d, :], src, w, col("conv_b", d), ALU.mult, ALU.add).then_inc(m_conv.sem, 1)
                    else:
                        dve.wait_ge(m_conv.sem, m_conv.at(c, DT * (k - 1) + d + 1))
                        dve.scalar_tensor_tensor(cv[:, d, :], src, w, cv[:, d, :], ALU.mult, ALU.add).then_inc(m_conv.sem, 1)
                if k == DC - 1:
                    dve.tensor_copy(tail[:, bass.ds(c + NB, 1), :, :].rearrange("p a d t -> p (a d) t"), xb[:, :, H:]).then_inc(m_kept.sem, 1)

            def bdr(c, _):
                dve.wait_ge(m_xp.sem, m_xp.at(c, 1))
                dve.wait_ge(m_proj.sem, m_proj.at(c, 2 * DT))
                dve.tensor_copy(dr[96:104, :], PN[96:104, 1, :]).then_inc(m_dr.sem, 1)

            def bhi(c, _):
                dve.wait_ge(m_xp.sem, m_xp.at(c, 1))
                if later(c):
                    dve.wait_ge(c_ready.sem, c_ready.at(c, 0))
                dve.tensor_copy(bc[0:96, :], PN[0:96, 1, :]).then_inc(m_hi.sem, 1)

            def blo(c, _):
                dve.wait_ge(m_hi.sem, m_hi.at(c, 1))
                dve.tensor_tensor(bc[64:96, :], PN[64:96, 1, :], bc[64:96, :].bitcast(fp32), ALU.subtract).then_inc(m_bc.sem, 1)

            def dl_(c, _):
                dve.wait_ge(m_soft.sem, m_soft.at(c, 1))
                dve.wait_ge(m_relu.sem, m_relu.at(c, DT))
                dve.tensor_tensor(dl[:, :, :], dl[:, :, :], dx[:, :, :], ALU.add).then_inc(m_dl.sem, 1)

            def dx_(c, _):
                dve.wait_ge(m_dl.sem, m_dl.at(c, 1))
                dve.tensor_tensor(dx[:, :, :], dl[:, :, :], xs[:, :, :], ALU.mult).then_inc(m_dx.sem, 1)

            def dskip(c, _):
                for d in range(DT):
                    dve.wait_ge(m_xs.sem, m_xs.at(c, 1))
                    if later(c):
                        dve.wait_ge(m_out.sem, m_out.at(c, 0))
                    dve.tensor_scalar(yd[:, d, :], xs[:, d, :], col("d_param", d), None, ALU.mult).then_inc(m_skip.sem, 1)

            def take(c, _):
                if later(c):
                    dve.wait_ge(m_keep.sem, m_keep.at(c, 0))
                    dve.wait_ge(h_scan.sem, h_scan.at(c, 0))
                dve.tensor_copy(state_in[:, :], state[:, bass.ds(c, 1), :].rearrange("p a n -> p (a n)")).then_inc(m_take.sem, 1)

            def keep(c, _):
                dve.wait_ge(h_ready.sem, h_ready.at(c, NP))
                dve.tensor_copy(state[:, bass.ds(c + NB, 1), :].rearrange("p a n -> p (a n)"), state_out[:, :]).then_inc(m_keep.sem, 1)

            def u_(c, p):
                dve.wait_ge(b_ready.sem, b_ready.at(c, p + 1))
                dve.wait_ge(m_dx.sem, m_dx.at(c, 1))
                if p >= NU or later(c):
                    before = p - NU if p >= NU else max(q for q in range(NP) if q % NU == p) - NP
                    dve.wait_ge(g_summed.sem, g_summed.at(c, before + 1))
                dve.tensor_tensor(U[:, p % NU, :, :, :], dx[:, :, :].unsqueeze(2).broadcast_to([P, DT, 2, H]),
                                  PR[:, :, :].unsqueeze(1).broadcast_to([P, DT, 2, H]), ALU.mult).then_inc(u_ready.sem, 1)

            def scan(c, p):
                u = U[:, p % NU, :, :, :]
                dve.wait_ge(u_ready.sem, u_ready.at(c, p + 1))
                dve.wait_ge(m_take.sem, m_take.at(c, 1))
                for d in range(DT):
                    for s in range(2):
                        n = (p * DT + d) * 2 + s
                        dve.wait_ge(a_ready.sem, a_ready.at(c, n + 1))
                        dve.tensor_tensor_scan(u[:, d, s, :], A[:, p % NA, d, s, :], u[:, d, s, :], state_in[:, n:n + 1],
                                               ALU.mult, ALU.add).then_inc(h_scan.sem, 1)
                if later(c):
                    dve.wait_ge(m_keep.sem, m_keep.at(c, 0))
                dve.wait_ge(h_scan.sem, h_scan.at(c, 2 * DT * (p + 1)))
                dve.tensor_copy(state_out[:, 2 * DT * p:2 * DT * (p + 1)].rearrange("p (d s) -> p d s", d=DT),
                                u[:, :, :, H - 1]).then_inc(h_ready.sem, 1)

            def yadd(c, _):
                dve.wait_ge(g_summed.sem, g_summed.at(c, NP))
                dve.wait_ge(m_skip.sem, m_skip.at(c, DT))
                dve.tensor_tensor(yd[:, :, :], PY[:, :, :], yd[:, :, :], ALU.add).then_inc(m_yd.sem, 1)

            def yz(c, _):
                dve.wait_ge(m_yd.sem, m_yd.at(c, 1))
                dve.wait_ge(m_zs.sem, m_zs.at(c, 1))
                dve.tensor_tensor(yd[:, :, :], yd[:, :, :], zs[:, :, :], ALU.mult).then_inc(m_yz.sem, 1)

            def res(c, _):
                dve.wait_ge(m_out.sem, m_out.at(c, 1))
                dve.wait_ge(xr_in, 16 * (c + 1))
                dve.wait_ge(f_res.sem, f_res.at(c, 0))
                dve.tensor_tensor(XF[:, :], XR[:, :], PN[:, 0, :], ALU.add).then_inc(m_res.sem, 1)

            def stream(c):
                return x3 if tokens(c) == NT else XF

            def fc_(c, f):
                n = tokens(c)
                dve.wait_ge(f_mean.sem, f_mean.at(c, f + 1))
                dve.tensor_tensor(fc[:, 0:n], stream(c)[:, 0:n], PF[:, 0, 0:n], ALU.subtract).then_inc(f_cent.sem, 1)

            def fn(c, f):
                n = tokens(c)
                dve.wait_ge(f_rs.sem, f_rs.at(c, f + 1))
                dve.tensor_tensor(fc[:, 0:n], fc[:, 0:n], fr[:, 0:n], ALU.mult).then_inc(f_norm.sem, 1)

            def fx(c, f):
                n = tokens(c)
                dve.wait_ge(f_norm.sem, f_norm.at(c, f + 1))
                dve.tensor_copy(xh[:, 0:n], fc[:, 0:n]).then_inc(f_xh.sem, 1)
                dve.wait_ge(f_xh.sem, f_xh.at(c, f + 1))
                dve.tensor_tensor(xl[:, 0:n], fc[:, 0:n], xh[:, 0:n].bitcast(fp32), ALU.subtract).then_inc(f_xl.sem, 1)

            def mu(c, k):
                f, _, m, nth = place(k)
                n = tokens(c)
                t = ht[:, k % 2, 0:n]
                dve.wait_ge(f_silu.sem, f_silu.at(c, nth + 1))
                dve.scalar_tensor_tensor(t, PF[:, 1, 0:n], col("s2", m), t, ALU.mult, ALU.mult).then_inc(f_mul.sem, 1)

            def hi(c, k):
                f, _, m, nth = place(k)
                n = tokens(c)
                dve.wait_ge(f_mul.sem, f_mul.at(c, nth + 1))
                dve.tensor_copy(hAh[:, m, 0:n], ht[:, k % 2, 0:n]).then_inc(f_hi.sem, 1)

            def lo(c, k):
                f, layer, m, nth = place(k)
                n = tokens(c)
                high, low = ((hAh, hAl), (hBh, hBl), (hAh, hAl))[layer]
                if layer == 0:
                    dve.wait_ge(f_hi.sem, f_hi.at(c, nth + 1))
                else:
                    dve.wait_ge(f_gelu.sem, f_gelu.at(c, 2 * (nth + 1)))
                dve.tensor_tensor(low[:, m, 0:n], ht[:, k % 2, 0:n], high[:, m, 0:n].bitcast(fp32), ALU.subtract).then_inc(f_lo.sem, 1)

            def fres(c, f):
                n = tokens(c)
                dst = x5 if n == NT else (XF, XO)[f]
                dve.wait_ge(f_ops.sem, f_ops.at(c, f + 1))
                dve.scalar_tensor_tensor(dst[:, 0:n], PF[:, 0, 0:n], col("s3"), stream(c)[:, 0:n], ALU.mult, ALU.add).then_inc(f_res.sem, 1)
                if f == 0 and n == H:
                    dve.wait_ge(f_res.sem, f_res.at(c, 1))
                    dve.tensor_copy(spec[:, bass.ds(c * EFF, EFF)], XF[:, 0:EFF]).then_inc(f_spec.sem, 1)
                    dve.wait_ge(f_spec.sem, f_spec.at(c, 1))
                    dve.tensor_scalar(XF[:, :], XF[:, :], col("ob"), None, ALU.add).then_inc(f_ob.sem, 1)

            units = {"cent": cent, "norm": norm, "cin": cin, "tap": tap, "bdr": bdr, "bhi": bhi, "blo": blo, "dl": dl_, "dx": dx_,
                     "dskip": dskip, "take": take, "keep": keep, "u": u_, "scan": scan, "yadd": yadd, "yz": yz, "res": res,
                     "fc": fc_, "fn": fn, "fx": fx, "mu": mu, "hi": hi, "lo": lo, "fres": fres}
            play(DVE_ORDER, units, -1, behind=False, state=False)

            dve.wait_ge(fmats_in, 16)
            dve.tensor_copy(WH[:, :], staged).then_inc(s_wh, 1)
            dve.wait_ge(s_wh, 1)
            dve.tensor_tensor(WL[:, :], staged, WH[:, :].bitcast(fp32), ALU.subtract).then_inc(s_wl, 1)
            dve.wait_ge(s_wl, 1)
            dve.tensor_reduce(w_rest[:, 0:1], WL[:, :].bitcast(fp32), AX.X, ALU.max, apply_absolute_value=True).then_inc(s_rest, 1)
            dve.wait_ge(s_rest, 1)
            dve.tensor_scalar(w_rest[:, 1:2], w_rest[:, 0:1], 0.0, None, ALU.is_gt).then_inc(s_rest, 1)
            dve.wait_ge(s_count, 1)
            dve.tensor_scalar(w_split[:, :], PF[:, 0, 0:1], float(P), None, ALU.mult).then_inc(s_split, 1)

            play(DVE_ORDER, units, 0, behind=False)
            with dve.Fori(1, NCH - 1) as i:
                play(DVE_ORDER, units, i)
            play(DVE_ORDER, units, NCH - 1, ahead=False)
            play(DVE_ORDER, units, NCH, state=False, ahead=False)

            def step(ins):
                return ins.then_inc(V.sem, 1)

            def pe(name):
                dve.wait_ge(E.sem, E.after(name))

            def own(name):
                dve.wait_ge(V.sem, V.after(name))

            def act_done(name):
                dve.wait_ge(S.sem, S.after(name))

            dve.wait_ge(f_res.sem, f_res.at(NCH - 1, 2))
            step(dve.memset(qpad, 0.0))
            src = spec[:, 0:NT]
            for n in ("o", "i"):
                pe("mean_" + n)
                step(dve.tensor_tensor(t_c, src, Y4[0][:, 0:NT], ALU.subtract))
                act_done("rs_" + n)
                step(dve.tensor_tensor(t_n, t_c, t_r, ALU.mult))
                own("n_" + n)
                src = t_n
            step(dve.tensor_scalar(t_qa, t_n, col("lna"), None, ALU.mult))
            step(dve.tensor_scalar(t_ka, t_n, col("lnb"), None, ALU.mult))
            pe("v")
            step(dve.tensor_scalar(t_q, Y4[2][:, 0:NT], col("qb"), None, ALU.add))
            step(dve.tensor_copy(t_k, Y4[2][:, NT:2 * NT]))
            step(dve.tensor_scalar(t_v, Y4[2][:, 2 * NT:3 * NT], col("vb"), None, ALU.add))
            heads = C[:, slice(*COL_AT["head_of"])]
            for bd, w in ((bdq, "lqw"), (bdk, "lkw"), (bdv, "lvw")):
                wide = C[:, slice(*COL_AT[w])].unsqueeze(1).broadcast_to([P, NH, HD])
                step(dve.tensor_tensor(bd.rearrange("p (h d) -> p h d", h=NH), wide,
                                       heads.unsqueeze(2).broadcast_to([P, NH, HD]), ALU.mult))
            pe("vv")
            step(dve.tensor_scalar(t_k0, Y4[3][:, 0:NT], col("lkb"), None, ALU.add))
            step(dve.tensor_scalar(t_vi, Y4[3][:, NT:2 * NT], col("lvb"), None, ALU.add))
            pe("mean_k")
            step(dve.tensor_tensor(t_c, t_k0, Y4[0][:, 0:NT], ALU.subtract))
            act_done("rs_k")
            step(dve.scalar_tensor_tensor(t_kn, t_c, col("lnd"), t_r, ALU.mult, ALU.mult))
            own("n_k")
            step(dve.tensor_tensor(kblk.rearrange("p (b h k) -> p b h k", b=NB, h=NH),
                                   t_kn.rearrange("p (b k) -> p b k", b=NB).unsqueeze(2).broadcast_to([P, NB, NH, EFF]),
                                   heads.unsqueeze(1).unsqueeze(3).broadcast_to([P, NB, NH, EFF]), ALU.mult))
            pe("vi_t")
            step(dve.tensor_copy(t_vsb[0:NT, :], Y4[3][0:NT, 2 * NT:2 * NT + P]))
            pe("rep")
            step(dve.tensor_copy(vrep, PR[:, 0, :]))
            own("v_sb")
            for hf in range(2):
                mask = C[:, COL_AT["vhead_of"][0] + hf * NH:COL_AT["vhead_of"][0] + (hf + 1) * NH]
                step(dve.tensor_tensor(vblk[:, hf * NB * P:(hf + 1) * NB * P].rearrange("p (b h d) -> p b h d", b=NB, h=NH),
                                       vrep.rearrange("p (b h d) -> p b h d", b=NB, h=NH),
                                       mask.unsqueeze(1).unsqueeze(3).broadcast_to([P, NB, NH, HD]), ALU.mult))
            lg = PF[:, 0, 0:NH * EFF].rearrange("p (h k) -> p h k", h=NH)
            pr3 = prob.rearrange("p (h k) -> p h k", h=NH)
            for t in ITERS:
                pe(f"qq{t}")
                step(dve.tensor_scalar(t_q0, Y4[2][:, 0:NT], col("lqb"), None, ALU.add))
                pe(f"mean_q{t}")
                step(dve.tensor_tensor(t_c, t_q0, Y4[0][:, 0:NT], ALU.subtract))
                act_done(f"rs_q{t}")
                step(dve.scalar_tensor_tensor(qpad.rearrange("p (b q) -> p b q", b=NB)[:, :, 0:EFF],
                                              t_c.rearrange("p (b q) -> p b q", b=NB), col("lnc"),
                                              t_r.rearrange("p (b q) -> p b q", b=NB), ALU.mult, ALU.mult))
                pe(f"logits{t}")
                step(dve.reduce_max(smax, lg, AX.X))
                own(f"max{t}")
                step(dve.tensor_tensor(pr3, lg, smax.unsqueeze(2).broadcast_to([P, NH, EFF]), ALU.subtract))
                act_done(f"exp{t}")
                step(dve.tensor_reduce(ssum, pr3, AX.X, ALU.add))
                own(f"sum{t}")
                step(dve.reciprocal(ssum, ssum))
                own(f"rec{t}")
                step(dve.tensor_tensor(pr3, pr3, ssum.unsqueeze(2).broadcast_to([P, NH, EFF]), ALU.mult))
                pe(f"pt{t}")
                step(dve.tensor_copy(pT, PF[:, 1, 0:2 * P]))
                pe(f"att{t}")
                step(dve.tensor_copy(att[t], Y4[3][:, 0:NT]))
                own(f"att{t}")
                if t < 2:
                    step(dve.tensor_tensor(t_q, t_q, att[t], ALU.add))
                if t == 1:
                    step(dve.tensor_tensor(t_d, att[1], att[0], ALU.subtract))
            pe("diff1")
            step(dve.tensor_scalar(tiny[:, 1:2], Y4[2][:, NT:NT + 1], float(P) / (NB * NH * T * HD), None, ALU.mult))
            own("mean_abs")
            step(dve.tensor_scalar(tiny[:, 2:3], tiny[:, 1:2], 0.1, 0.01, ALU.mult, ALU.add))
            own("limit")
            step(dve.tensor_tensor(tiny[:, 3:4], tiny[:, 1:2], tiny[:, 2:3], ALU.is_lt))
            own("brk")
            step(dve.tensor_scalar(tiny[:, 4:5], tiny[:, 3:4], -1.0, 1.0, ALU.mult, ALU.add))
            step(dve.tensor_scalar(t_d, att[1], tiny[:, 3:4], None, ALU.mult))
            own("old")
            step(dve.scalar_tensor_tensor(att[0], att[2], tiny[:, 4:5], t_d, ALU.mult, ALU.add))
            pe("ow")
            step(dve.scalar_tensor_tensor(x3, Y4[2][:, 0:NT], col("ob"), spec[:, 0:NT], ALU.add, ALU.add))
            own("x3")
            first_ffn(DVE_ORDER, units)

        @block.tensor
        def _(te):
            def mean(c, _):
                te.wait_ge(xm_in, 16 * (c + 1))
                if later(c):
                    te.wait_ge(m_relu.sem, m_relu.at(c - 1, 1))
                    te.wait_ge(m_abs.sem, m_abs.at(c - 1, 1))
                te.matmul(PN[:, 0, :], mean_w[:, :], XM[:, :], start=True, stop=True).then_inc(m_mean.sem, 1)

            def var(c, _):
                te.wait_ge(m_sq.sem, m_sq.at(c, 1))
                if later(c):
                    te.wait_ge(m_relu.sem, m_relu.at(c, 0))
                    te.wait_ge(m_abs.sem, m_abs.at(c, 0))
                te.matmul(PN[:, 1, :], mean_w[:, :], mr[:, :], start=True, stop=True).then_inc(m_var.sem, 1)

            def proj(c, m):
                te.wait_ge(m_norm.sem, m_norm.at(c, 1))
                if m >= 2:
                    te.wait_ge(m_evac.sem, m_evac.at(c, m - 1))
                te.matmul(PN[:, m % 2, :], mat("w_in", m, P), mc[:, :], start=True, stop=True).then_inc(m_proj.sem, 1)

            def xp(c, _):
                te.wait_ge(m_evac.sem, m_evac.at(c, 2 * DT))
                te.wait_ge(m_xs.sem, m_xs.at(c, 1))
                for d in range(DT):
                    last = te.matmul(PN[0:104, 1, :], mat("w_xproj", d, 104), xs[:, d, :], start=(d == 0), stop=(d == DT - 1))
                last.then_inc(m_xp.sem, 1)

            def dt(c, d):
                te.wait_ge(m_dr.sem, m_dr.at(c, 1))
                if d == 0:
                    te.wait_ge(m_evac.sem, m_evac.at(c, 2 * DT))
                    if later(c):
                        te.wait_ge(m_res.sem, m_res.at(c, 0))
                else:
                    te.wait_ge(m_bc.sem, m_bc.at(c, 1))
                te.matmul(PN[:, d, :], mat("w_dt", d, P, slice(96, 104)), dr[96:104, :], start=True, stop=True).then_inc(m_dps.sem, 1)

            def spread(n, done):
                for s in range(2):
                    last = te.matmul(PR[:, s, :], pick[0:96, n + s:n + s + 1].broadcast_to([96, P]), bc[0:96, :],
                                     start=True, stop=True)
                last.then_inc(done.sem, 1)

            def b_(c, p):
                te.wait_ge(m_bc.sem, m_bc.at(c, 1))
                if p or later(c):
                    te.wait_ge(c_copied.sem, c_copied.at(c, p))
                spread(2 * p, b_ready)

            def c_(c, p):
                te.wait_ge(u_ready.sem, u_ready.at(c, p + 1))
                spread(NS + 2 * p, c_ready)

            def sum_(c, p):
                te.wait_ge(g_ready.sem, g_ready.at(c, p + 1))
                if p == 0 and later(c):
                    te.wait_ge(m_yd.sem, m_yd.at(c, 0))
                for d in range(DT):
                    last = te.matmul(PY[:, d, :], mat("ident"), U[:, p % NU, d, 0, :], start=(p == 0), stop=(p == NP - 1))
                last.then_inc(g_summed.sem, 1)

            def out(c, _):
                te.wait_ge(m_yz.sem, m_yz.at(c, 1))
                if not isinstance(c, int) or c + 1 < NCH:
                    te.wait_ge(m_evac.sem, m_evac.at(c + 1, DT + 1))
                else:
                    te.wait_ge(m_relu.sem, m_relu.at(c, DT))
                    te.wait_ge(m_abs.sem, m_abs.at(c, DT))
                for d in range(DT):
                    last = te.matmul(PN[:, 0, :], mat("w_out", d, D), yd[:, d, :], start=(d == 0), stop=(d == DT - 1))
                last.then_inc(m_out.sem, 1)

            mixer = {"mean": mean, "var": var, "proj": proj, "xp": xp, "dt": dt, "B": b_, "C": c_, "sum": sum_, "out": out}

            def run(exact):
                def product(out, name, m, w, hi, lo, n, tiles):
                    for k in range(tiles):
                        at = FMAT_AT[name][0] + k * w + m * P
                        for W in (WH,) if exact else (WH, WL):
                            for x in (hi, lo):
                                end = k == tiles - 1 and x is lo and (exact or W is WL)
                                last = te.matmul(out, W[:, at:at + P], x[:, k, 0:n],
                                                 start=(k == 0 and W is WH and x is hi), stop=end)
                    return last

                xn = [t[:, :].unsqueeze(1) for t in (xh, xl)]

                def fm(c, f):
                    n = tokens(c)
                    if n == NT:
                        te.wait_ge(V.sem, V.after("x3"))
                    elif f == 0:
                        te.wait_ge(m_res.sem, m_res.at(c, 1))
                    else:
                        te.wait_ge(f_ob.sem, f_ob.at(c, 1))
                    te.matmul(PF[:, 0, 0:n], mean_w[:, :], (x3 if n == NT else XF)[:, 0:n], start=True, stop=True).then_inc(f_mean.sem, 1)

                def fv(c, f):
                    n = tokens(c)
                    te.wait_ge(f_sq.sem, f_sq.at(c, f + 1))
                    te.matmul(PF[:, 1, 0:n], mean_w[:, :], fr[:, 0:n], start=True, stop=True).then_inc(f_var.sem, 1)

                def up(c, k):
                    f, _, m, nth = place(k)
                    n = tokens(c)
                    te.wait_ge(f_xl.sem, f_xl.at(c, f + 1))
                    if m:
                        te.wait_ge(f_mul.sem, f_mul.at(c, nth))
                    product(PF[:, 0, 0:n], "w1", m, HID, *xn, n, 1)
                    product(PF[:, 1, 0:n], "w2", m, HID, *xn, n, 1).then_inc(f_gu.sem, 1)

                def h_(c, k):
                    f, layer, m, nth = place(k)
                    n = tokens(c)
                    high, low = (hAh, hAl) if layer == 1 else (hBh, hBl)
                    te.wait_ge(f_lo.sem, f_lo.at(c, k - m))
                    if m >= 2 or layer == 2:
                        te.wait_ge(f_gelu.sem, f_gelu.at(c, 2 * (nth - 1)))
                    product(PF[:, m % 2, 0:n], ("h1", "h2")[layer - 1], m, HID, high, low, n, MT).then_inc(f_hps.sem, 1)

                def dn(c, f):
                    n = tokens(c)
                    te.wait_ge(f_lo.sem, f_lo.at(c, 3 * MT * (f + 1)))
                    product(PF[:, 0, 0:n], "w3", 0, D, hAh, hAl, n, MT).then_inc(f_ops.sem, 1)

                units = mixer | {"fm": fm, "fv": fv, "up": up, "h": h_, "dn": dn}
                play(PE_ORDER, units, 0, behind=False)
                with te.Fori(1, NCH - 1) as i:
                    play(PE_ORDER, units, i)
                play(PE_ORDER, units, NCH - 1, ahead=False)
                play(PE_ORDER, units, NCH, state=False, ahead=False)

                def mm(out, w, x, **kw):
                    kw = {"start": True, "stop": True} | kw
                    return te.matmul(out, w, x, **kw)

                def dve(name):
                    te.wait_ge(V.sem, V.after(name))

                def done(ins):
                    ins.then_inc(E.sem, 1)

                def attn_norm(n, src, w, before=None):
                    if before:
                        dve(before)
                    done(mm(Y4[0][:, 0:NT], w, src))
                    te.wait_ge(S.sem, S.after("sq_" + n))
                    done(mm(Y4[1][:, 0:NT], w, t_r))

                te.wait_ge(f_res.sem, f_res.at(NCH - 1, 2))
                attn_norm("o", spec[:, 0:NT], mean_w[:, :])
                attn_norm("i", t_n, mean_w[:, :], "n_o")
                dve("qa")
                done(mm(Y4[2][:, 0:NT], mat("qw"), t_qa))
                dve("ka")
                done(mm(Y4[2][:, NT:2 * NT], mat("kw"), t_ka))
                done(mm(Y4[2][:, 2 * NT:3 * NT], mat("vw"), t_ka))
                dve("bdk")
                done(mm(Y4[3][:, 0:NT], bdk, t_k))
                dve("bdv")
                done(mm(Y4[3][:, NT:2 * NT], bdv, t_v))
                attn_norm("k", t_k0, mat("group"), "k0")
                dve("vi")
                done(te.transpose(Y4[3][0:NT, 2 * NT:2 * NT + P], t_vi, mat("ident")))
                dve("vi_sb")
                te.wait_ge(rep_in, 16)
                for b in range(NB):
                    last = mm(PR[:, 0, b * P:(b + 1) * P], t_rep[0:NT, b * P:(b + 1) * P], t_vsb[0:NT, :])
                done(last)
                dve("vblk1")
                for t in ITERS:
                    if t:
                        dve(f"qcur{t - 1}")
                    done(mm(Y4[2][:, 0:NT], bdq, t_q))
                    attn_norm(f"q{t}", t_q0, mat("group"), f"q0{t}")
                    dve(f"n_q{t}")
                    for b in range(NB):
                        last = mm(PF[32 * b:32 * (b + 1), 0, 0:NH * EFF], qpad[:, 32 * b:32 * (b + 1)],
                                  kblk[:, b * NH * EFF:(b + 1) * NH * EFF], tile_position=(0, 32 * b))
                    done(last)
                    dve(f"prob{t}")
                    for hf in range(2):
                        last = te.transpose(PF[:, 1, hf * P:(hf + 1) * P], prob[:, hf * P:(hf + 1) * P], mat("ident"))
                    done(last)
                    dve(f"pt{t}")
                    for b in range(NB):
                        for hf in range(2):
                            last = mm(Y4[3][:, b * EFF:(b + 1) * EFF], vblk[:, (hf * NB + b) * P:(hf * NB + b + 1) * P],
                                      pT[:, hf * P + 32 * b:hf * P + 32 * b + EFF], start=(hf == 0), stop=(hf == 1))
                    done(last)
                    if t == 1:
                        te.wait_ge(S.sem, S.after("abs1"))
                        done(mm(Y4[2][:, NT:NT + 1], mean_w[:, :], tiny[:, 0:1]))
                dve("sel")
                done(mm(Y4[2][:, 0:NT], mat("ow"), att[0]))
                first_ffn(PE_ORDER, units)

            te.wait_ge(mats_in, 16)
            te.wait_ge(s_set, 6)
            te.wait_ge(s_pick, 1)
            play(PE_ORDER, mixer, -1, behind=False, state=False)
            te.wait_ge(s_rest, 2)
            te.matmul(PF[:, 0, 0:1], mean_w[:, :], w_rest[:, 1:2], start=True, stop=True).then_inc(s_count, 1)
            te.wait_ge(s_split, 1)
            inexact = te.value_load(w_split[0:1, 0:1])
            with te.If_eq(te.to_reg(inexact), 0):
                run(True)
            with te.Else():
                run(False)


def rows(v, n=1):
    v = np.asarray(v)
    v = v.reshape(n, P, -1)
    return np.ascontiguousarray(v.transpose(1, 0, 2).reshape(P, -1))


def layout(i):
    f = lambda n: np.asarray(i[n])
    mats = np.zeros((P, NMAT), np.float32)
    cols = np.zeros((P, NCOL), np.float32)

    def m(name, v):
        lo, hi = MAT_AT[name]
        mats[:, lo:hi] = v

    def c(name, v):
        lo, hi = COL_AT[name]
        cols[:, lo:hi] = v

    m("w_in", f("L0_attn_a_W_in"))
    xp = f("L0_attn_a_W_xproj").reshape(DT, P, DTR + 2 * NS)
    lo = MAT_AT["w_xproj"][0]
    for d in range(DT):
        at = lo + d * 104
        mats[:, at:at + 32] = xp[d][:, DTR:]
        mats[:, at + 64:at + 96] = xp[d][:, DTR:]
        mats[:, at + 96:at + 104] = xp[d][:, :DTR]
    m("w_out", rows(f("L0_attn_a_W_out"), DT))
    lo, hi = MAT_AT["w_dt"]
    mats[96:104, lo:hi] = f("L0_attn_a_W_dt")
    fmats = np.concatenate([f("L0_ffn_w1_w").T, f("L0_ffn_w2_w").T]
                           + [rows(f(f"L0_ffn_{n}_w").T, MT) for n in ("h1", "h2", "w3")], axis=1)
    for name in ("qw", "kw", "vw", "ow"):
        m(name, f("L0_attn_b_" + name).T)
    part = np.arange(P)
    m("ident", part[:, None] == part[None, :])
    m("group", np.where(part[:, None] // HD == part[None, :] // HD, np.float32(1.0 / HD), np.float32(0)))

    c("conv_w", rows(f("L0_attn_a_conv_w"), DT))
    c("conv_b", rows(f("L0_attn_a_conv_b"), DT))
    c("b_dt", rows(f("L0_attn_a_b_dt"), DT))
    c("a_log", rows(f("L0_attn_a_A_log"), DT))
    c("d_param", rows(f("L0_attn_a_D_param"), DT))
    c("s1", rows(f("L0_ffn_w1_s"), MT))
    c("s2", rows(f("L0_ffn_w2_s"), MT))
    c("sh1", rows(f("L0_ffn_h1_s"), MT))
    c("sh2", rows(f("L0_ffn_h2_s"), MT))
    c("s3", rows(f("L0_ffn_w3_s")))
    for name, key in (("qb", "qb"), ("vb", "vb"), ("ob", "ob"), ("lna", "lna_w"), ("lnb", "lnb_w")):
        c(name, rows(f("L0_attn_b_" + key)))
    for name, key in (("lnc", "lnc_w"), ("lnd", "lnd_w"), ("lqb", "lqb"), ("lkb", "lkb"), ("lvb", "lvb")):
        c(name, np.tile(f("L0_attn_b_" + key), NH)[:, None])
    for name in ("lqw", "lkw", "lvw"):
        c(name, np.tile(f("L0_attn_b_" + name).T, (NH, 1)))
    n = np.arange(2 * NS)
    c("pick", (part[:, None] == n[None, :]) | (part[:, None] == 64 + n[None, :]))
    heads = np.arange(NH)
    c("head_of", part[:, None] // HD == heads[None, :])
    c("vhead_of", np.concatenate([part[:, None] // EFF + (NH // 2) * hf == heads[None, :] for hf in range(2)], axis=1))
    token = np.arange(NT)
    rep = np.concatenate([token[:, None] == b * EFF + part[None, :] % EFF for b in range(NB)], axis=1)
    return mats, fmats, cols, rep.astype(np.float32)


def kernel(**inputs):
    import concourse.bacc as bacc
    from concourse.bass_utils import run_bass_kernel_spmd

    x = np.asarray(inputs["L0_attn_a_x"]).reshape(NB, 2, H, D)
    mats, fmats, cols, rep = layout(inputs)
    arrays = {"xT": np.ascontiguousarray(x.transpose(3, 1, 0, 2).reshape(D, NB * T)), "mats": mats, "fmats": np.ascontiguousarray(fmats), "cols": cols, "rep": rep}
    nc = bacc.Bacc("TRN2", target_bir_lowering=False, num_devices=1)
    args = [nc.dram_tensor(n, a.shape, mybir.dt.from_np(a.dtype), kind="ExternalInput").ap() for n, a in arrays.items()]
    out = nc.dram_tensor("outT", (D, NB * T), mybir.dt.float32, kind="ExternalOutput").ap()
    hybrid_kernel(nc, *args, out)
    r = run_bass_kernel_spmd(nc, [arrays], core_ids=[0])
    y = np.asarray(r.results[0]["outT"]).reshape(D, 2, NB, H)
    return np.ascontiguousarray(y.transpose(2, 1, 3, 0)).reshape(NB, T, D)
```

```python
from contextlib import ExitStack
from functools import partial

import numpy as np

import concourse.bass as bass
from concourse import mybir

P = 128
D = 128
NB, T = 4, 1024
H = 512
NCH = NB * T // H
DI, NS, DC, DTR = 256, 16, 4, 8
DT = DI // P
HID = 512
MT = HID // P
NH, HD, EFF = 16, 8, 16
NT = NB * EFF
EPS = 1e-5
NP = NS // 2
NA = 3
NU = 4

MATS = [("ident", P), ("w_z", DI), ("w3", MT * D), ("w_xproj", DT * 104), ("w_out", DT * D), ("w_dt", DI), ("qw", D), ("kw", D), ("vw", D),
        ("ow", D), ("group", P)]
FMATS = [("w1", HID), ("w2", HID), ("h1", MT * HID), ("h2", MT * HID)]
COLS = [("conv_w", DT * DC), ("conv_b", DT), ("b_dt", DT), ("a_log", DT * NS), ("d_param", DT), ("s1", MT), ("s2", MT),
        ("sh1", MT), ("sh2", MT), ("s3", 1), ("qb", 1), ("vb", 1), ("ob", 1), ("lna", 1), ("lnb", 1), ("lnc", 1),
        ("lnd", 1), ("lqb", 1), ("lkb", 1), ("lvb", 1), ("lqw", HD), ("lkw", HD), ("lvw", HD), ("pick", 2 * NS),
        ("head_of", NH), ("vhead_of", 2 * NH)]


def offsets(parts):
    at, out = 0, {}
    for name, n in parts:
        out[name] = (at, at + n)
        at += n
    return out, at


MAT_AT, NMAT = offsets(MATS)
FMAT_AT, NFMAT = offsets(FMATS)
COL_AT, NCOL = offsets(COLS)


class Signal:

    def __init__(self, ctx, nc, name, per, start=0):
        self.sem, self.per, self.start = ctx.enter_context(nc.semaphore(name)), per, start

    def at(self, c, n):
        return c * self.per + n + self.start


class Steps:

    def __init__(self, ctx, nc, name, names):
        self.sem = ctx.enter_context(nc.semaphore(name))
        self.names = list(names)

    def after(self, name):
        return self.names.index(name) + 1


class Ffn:

    def __init__(self, signal, name, n, layers, start):
        self.n = n
        self.s_cent = signal(name + "_cent", layers)
        self.s_sq = signal(name + "_sq", layers)
        self.s_var = signal(name + "_var", layers)
        self.s_ln = signal(name + "_ln", layers)
        self.s_rs = signal(name + "_rs", layers)
        self.s_norm = signal(name + "_norm", layers)
        self.s_high = signal(name + "_high", layers)
        self.s_low = signal(name + "_low", layers)
        self.s_down = signal(name + "_down", layers)
        self.s_gate = signal(name + "_gate", layers * MT)
        self.s_up = signal(name + "_up", layers * MT)
        self.s_silu = signal(name + "_silu", layers * MT)
        self.s_mul = signal(name + "_mul", layers * MT)
        self.s_hi = signal(name + "_hi", layers * MT)
        self.s_lo, self.s_hps = signal(name + "_lo", 2 * layers * MT), signal(name + "_hps", 2 * layers * MT)
        self.s_gelu = signal(name + "_gelu", 3 * layers * MT)
        self.s_res = signal(name + "_res", layers, start=start)


DVE_ORDER = """
bhi bdr blo yadd yz res dl dx u0 u1 keep fn0 take fx0 scan0 scan1 cin mu0 hi0 lo0 mu1 hi1 lo1 u2 mu2 u3 hi2 mu3 lo2
scan2 hi3 scan3 lo3 u4 u5 scan4 lo4 lo5 scan5 lo6 u6 lo7 u7 scan6 scan7 dskip u8 u9 norm fres0 scan8 scan9 u10 fn1 fx1
u11 scan10 scan11 mu12 hi12 lo12 mu13 hi13 lo13 mu14 hi14 ktail lo14 mu15 hi15 lo15 u12 u13 scan12 scan13 lo16 lo17
u14 lo18 u15 lo19 scan14 scan15 fres1
""".split()
ACT_ORDER = """
sa0 sr0 sa1 se sr1 sl fs0 dec0 fr0 dec1 dec2 dec3 si0 cc0 si1 sq si2 si3 dec4 dec5 dec6 cc1 dec7 ge4 ge5 cc2 ge6 ge7
ge8 ge9 cc3 sz ge10 ge11 rs dec8 dec9 cc4 fs1 dec10 fr1 dec11 dec12 dec13 si12 sx0 si13 sx1 si14 cc5 si15 dec14 dec15
ge16 cc6 ge17 ge18 ge19 ge20 cc7 ge21 ge22 ev2 ev3 ge23
""".split()
PE_ORDER = """
xp sum7 dt0 dt1 out B0 fm0 fv0 C0 mean gp0 vp0 gp1 vp1 gp2 B1 gp3 vp2 vp3 var C1 ha4 B2 ha5 h4 h5 C2 h6 h7 B3 ha8 ha9
h8 C3 h9 h10 h11 B4 da0 dn0 C4 sum1 fm1 B5 fv1 proj0 gp12 vp12 proj1 gp13 C5 vp13 gp14 vp14 gp15 proj2 B6 vp15 sum3
ha16 h16 ha17 h17 C6 h18 B7 h19 proj3 ha20 C7 h20 ha21 h21 h22 h23 sum5 da1 dn1
""".split()
POOL_ORDER = """
g0 ga0 g1 ga1 g2 gx1 ga2 g3 ga3 gx3 g4 ga4 g5 ga5 gx5 g6 ga6 g7 ga7 gx7
""".split()

DVE_START = """
cin bdr bhi blo dskip dl take dx u0 scan0 u1 scan1 u2 scan2 u3 scan3 u4 u5 scan4 u6 scan5 u7 scan6 scan7 u8 u9 scan8
scan9 u10 u11 scan10 scan11 u12 u13 norm scan12 scan13 u14 scan14 some u15 scan15 ktail
""".split()
ACT_START = """
sr0 sa0 sa1 se sr1 sl cc0 dec0 dec1 dec2 dec3 dec4 dec5 sq cc1 dec6 dec7 cc2 dec8 rest0 cc3 dec9 rs cc4 dec10 rest1
dec11 cc5 dec12 dec13 dec14 cc6 rest2 dec15 sx0 sz cc7 ev2 sx1 ev3
""".split()
PE_START = """
xp dt0 dt1 mean C0 B0 C1 B1 B2 C2 B3 sum0 C3 var B4 sum1 C4 sum2 B5 sum3 B6 C5 sum4 C6 B7 proj0 proj1 C7 proj2 sum5
proj3 count
""".split()
POOL_START = """
g0 ga0 g1 ga1 g2 ga2 g3 ga3 g4 ga4 g5 ga5 g6 ga6 g7 ga7 gx7
""".split()

DVE_END = """
yadd a_start keep yz res a_co a_no a_ci fn0 fx0 a_ni a_qkv mu0 hi0 a_inner lo0 mu1 a_ck hi1 lo1 mu2 a_vsb hi2 lo2 mu3
hi3 lo3 a_nk a_vblk lo4 a_qq0 a_cq0 lo5 a_nq0 lo6 a_max0 a_prob0 a_pt0 lo7 a_att0 a_qq1 a_cq1 a_nq1 a_max1 a_prob1
a_pt1 fres0 a_att1 a_qq2 a_cq2 a_nq2 a_max2 a_prob2 fn1 a_pt2 fx1 a_att2 a_brk a_sel a_done mu12 hi12 lo12 mu13 x_fn0
x_fx0 hi13 lo13 x_mu0 x_hi0 mu14 x_lo0 hi14 x_mu1 lo14 x_mu2 x_hi1 mu15 x_lo1 x_hi2 hi15 x_lo2 lo15 x_mu3 x_hi3 x_lo3
lo16 lo17 lo18 x_lo4 x_lo5 x_lo6 lo19 x_lo7 fres1 x_fres0
""".split()
ACT_END = """
a_sqo fs0 a_rso fr0 a_sqi a_rsi si0 si1 si2 a_sqk si3 a_rsk ge4 ge5 ge6 a_sqq0 a_rsq0 a_exp0 ge7 ge8 ge9 a_sqq1 a_rsq1
ge10 ge11 a_exp1 a_abs fs1 a_sqq2 a_rsq2 fr1 a_exp2 si12 si13 x_fs0 x_fr0 x_si0 si14 x_si1 si15 x_si2 x_si3 ge16 ge17
x_ge4 x_ge5 ge18 ge19 x_ge6 x_ge7 ge20 x_ge8 x_ge9 ge21 x_ge10 ge22 ge23 x_ge11
""".split()
PE_END = """
sum7 out a_mo fm0 fv0 a_vo a_mi a_vi gp0 a_qkv vp0 a_inner gp1 vp1 a_mk gp2 vp2 gp3 a_vk a_tv vp3 a_rep ha4 h4 ha5 h5
h6 a_qq0 a_mq0 a_vq0 h7 a_logit0 ha8 a_pt0 a_att0 ha9 h8 a_qq1 h9 a_mq1 h10 a_vq1 h11 a_logit1 da0 dn0 a_pt1 a_att1
fm1 a_diff a_qq2 a_mq2 a_vq2 fv1 a_logit2 a_pt2 a_att2 gp12 vp12 a_ow gp13 x_fm0 vp13 gp14 x_fv0 x_gp0 vp14 x_vp0
x_gp1 gp15 x_vp1 x_gp2 vp15 x_vp2 x_gp3 ha16 ha17 h16 x_vp3 x_ha4 h17 x_ha5 x_h4 x_h5 h18 h19 x_h6 x_h7 ha20 ha21 h20
x_ha8 x_h8 x_ha9 x_h9 h21 h22 x_h10 x_h11 h23 da1 dn1 x_da0 x_dn0
""".split()

BEHIND = ("keep", "sum7", "yadd", "yz", "out", "res", "fm", "fs", "fv", "fr", "fn", "fx", "gp", "vp", "si", "mu", "hi",
          "lo", "ha", "h", "ge", "da", "dn", "fres")
AHEAD = ("mean", "sq", "var", "rs", "norm", "proj", "ev", "cin", "ktail", "sx")


def split(name):
    stem = name.rstrip("0123456789")
    return stem, int(name[len(stem):] or 0)


def body(order, units, i, behind=True, state=True, ahead=True):
    for name in order:
        stem, k = split(name)
        if name in BEHIND or stem in BEHIND:
            if behind:
                units[stem](i - 1, k)
        elif stem in AHEAD:
            if ahead:
                units[stem](i + 1, k)
        elif state:
            units[stem](i, k)


def ending(order, units, attention):
    for name in order:
        stem, k = split(name)
        if stem in units:
            units[stem](NCH - 1, k)
        else:
            attention[stem](k)


def hybrid_kernel(nc, xT, mats, fmats, taps, w_x, cols, rep, outT):
    fp32, f32r, i32 = mybir.dt.float32, mybir.dt.float32r, mybir.dt.int32
    ALU, ACT, AX = mybir.AluOpType, mybir.ActivationFunctionType, mybir.AxisListType

    ctx = ExitStack()
    with ctx:
        def sb(name, shape, dt=fp32):
            return ctx.enter_context(nc.sbuf_tensor(name, shape, dt))

        def ps(name, shape):
            return ctx.enter_context(nc.psum_tensor(name, shape, fp32))

        def signal(name, per, start=0):
            return Signal(ctx, nc, name, per, start)

        def sem(name):
            return ctx.enter_context(nc.semaphore(name))

        M = sb("M", [P, NMAT])
        WH = sb("WH", [P, NFMAT], f32r)
        WL = sb("WL", [P, NFMAT], f32r)
        C = sb("C", [P, NCOL])
        mean_w = sb("mean_w", [P, P])
        cent_w = sb("cent_w", [P, P])
        eps_col = sb("eps_col", [P, 1])
        one_col = sb("one_col", [P, 1])
        w_rest = sb("w_rest", [P, 6])
        w_split = sb("w_split", [P, 1], i32)
        pick = sb("pick", [P, 2 * NS], f32r)
        a_neg = sb("a_neg", [P, DT * NS])
        XM = sb("XM", [P, H])
        mc = sb("mc", [P, DC - 1 + H])
        mr = sb("mr", [P, H])
        WC = sb("WC", [P, DC, DI])
        zr = sb("zr", [P, DT, H])
        xs = sb("xs", [P, DT, H])
        zs = sb("zs", [P, DT, H])
        dl = sb("dl", [P, DT, H])
        dx = sb("dx", [P, DT, H])
        bc = sb("bc", [P, H], f32r)
        dr = mc[:, DC - 1:]
        A = sb("A", [P, NA, DT, 2, H])
        U = sb("U", [P, NU, DT, 2, H])
        cs = sb("cs", [P, 2, H])
        tail = sb("tail", [P, NCH + NB, DC - 1])
        state = sb("state", [P, NCH + NB, NP * DT * 2])
        state_in = sb("state_in", [P, NP * DT * 2])
        state_out = sb("state_out", [P, NP * DT * 2])
        XR = sb("XR", [P, H])
        yd = sb("yd", [P, DT, H])
        XF = sb("XF", [P, H])
        fr = sb("fr", [P, H])
        XO = fr
        spec = sb("spec", [P, NCH * EFF])

        PY = ps("PY", [P, DT, H])
        PR = ps("PR", [P, 2, H])
        PN = ps("PN", [P, 2, H])
        PF = ps("PF", [P, 2, H])

        def mat(name, k=0, w=None, rows=slice(0, P)):
            lo, hi = MAT_AT[name]
            w = w or hi - lo
            return M[rows, lo + k * w:lo + (k + 1) * w]

        def col(name, k=0, w=1):
            lo, _ = COL_AT[name]
            return C[:, lo + k * w:lo + (k + 1) * w]

        ident_in, taps_in, wx_in = sem("ident_in"), sem("taps_in"), sem("wx_in")
        cols_in, mats_in, fmats_in = sem("cols_in"), sem("mats_in"), sem("fmats_in")
        xm_in, xr_in, rep_in, stored = sem("xm_in"), sem("xr_in"), sem("rep_in"), sem("stored")
        s_set, s_aneg, s_pick = sem("constants_set"), sem("a_neg_set"), sem("pick_set")
        s_first, s_cent, s_conv = sem("first_summed"), sem("cent_weights"), sem("conv_weights")
        s_wh, s_wl, s_rest, s_some = sem("w_high"), sem("w_low"), sem("w_rest"), sem("w_some")
        s_count, s_split = sem("w_count"), sem("w_split_known")
        m_cent, m_sq, m_var = signal("m_cent", 1), signal("m_sq", 1), signal("m_var", 1)
        m_ln, m_rs, m_norm = signal("m_ln", 1), signal("m_rs", 1), signal("m_norm", 1)
        m_proj, m_evac = signal("m_proj", 2 * DT), signal("m_evac", DT)
        m_tail, m_kept = signal("m_tail", 1), signal("m_kept", 1)
        m_xs, m_zs, m_xp = signal("m_xs", DT), signal("m_zs", 1), signal("m_xp", 1)
        m_dr, m_hi, m_bc, m_dps = signal("m_dr", 1), signal("m_hi", 1), signal("m_bc", 1), signal("m_dps", DT)
        m_abs, m_relu, m_exp, m_soft = signal("m_abs", DT), signal("m_relu", DT), signal("m_exp", 1), signal("m_soft", 1)
        m_dl, m_dx, m_skip = signal("m_dl", 1), signal("m_dx", 1), signal("m_skip", DT)
        b_ready, c_ready, c_copied = signal("b_ready", NP), signal("c_ready", NP), signal("c_copied", NP)
        a_ready = signal("a_ready", 2 * DT * NP)
        u_ready, h_scan, h_ready = signal("u_ready", DT * NP), signal("h_scan", 2 * DT * NP), signal("h_ready", NP)
        g_prod, g_pair = signal("g_prod", NP), signal("g_pair", NP)
        g_ready, g_summed = signal("g_ready", NP // 2), signal("g_summed", NP // 2)
        m_take, m_keep = signal("m_take", 1), signal("m_keep", 1)
        m_yd, m_yz, m_out, m_res = signal("m_yd", 1), signal("m_yz", 1), signal("m_out", 1), signal("m_res", 1)
        chunk_ffn = Ffn(signal, "f", n=H, layers=2, start=1)
        f_ob, f_spec = signal("f_ob", 1), signal("f_spec", 1)
        xo_free = signal("xo_free", 1, start=1)

        ITERS = range(3)
        V = Steps(ctx, nc, "attn_dve", ["zero", "bdq", "bdk", "bdv", "c_o", "n_o", "c_i", "n_i", "qa", "ka", "q", "k", "v",
                                        "k0", "vi", "c_k", "vi_sb", "n_k", "kblk", "v_sb", "vblk0", "vblk1"]
                  + [f"{n}{t}" for t in ITERS for n in ("q0", "c_q", "n_q", "max", "sub", "sum", "rec", "prob", "pt", "att")
                     + (("qcur",) if t < 2 else ()) + (("diff", ) if t == 1 else ())]
                  + ["mean_abs", "limit", "brk", "keep", "old", "sel", "x3"])
        S = Steps(ctx, nc, "attn_act", ["sq_o", "ln_o", "rs_o", "sq_i", "ln_i", "rs_i", "sq_k", "ln_k", "rs_k"]
                  + [f"{n}{t}" for t in ITERS for n in ("sq_q", "ln_q", "rs_q", "exp") + (("abs",) if t == 1 else ())])
        E = Steps(ctx, nc, "attn_pe", ["mean_o", "var_o", "mean_i", "var_i", "q", "k", "v", "kk", "vv", "mean_k", "var_k", "vi_t", "rep"]
                  + [f"{n}{t}" for t in ITERS for n in ("qq", "mean_q", "var_q", "logits", "pt", "att") + (("diff",) if t == 1 else ())]
                  + ["ow"])

        AT = A[:, :, :, :, :].rearrange("p a d s t -> p (a d s t)")
        at_used = [0]

        def part(n):
            at_used[0] += n
            return AT[:, at_used[0] - n:at_used[0]]

        t_c, t_r, t_n, t_qa, t_ka = (part(NT) for _ in range(5))
        t_q, t_k, t_v, t_k0, t_kn, t_vi, t_q0, t_qn = (part(NT) for _ in range(8))
        bdq, bdk, bdv = (part(P) for _ in range(3))
        t_vsb = part(P)
        t_rep = part(NB * P)
        qpad = part(NB * 32)
        kblk = part(NB * NH * EFF)
        vrep = part(NB * P)
        vblk = part(2 * NB * P)
        prob = part(NH * EFF)
        pT = part(2 * P)
        att = [part(NT) for _ in ITERS]
        t_d, t_old = part(NT), part(NT)
        tiny = part(8)
        smax, ssum = part(NH), part(NH)
        x3, x5 = part(NT), part(NT)
        assert at_used[0] <= NA * DT * 2 * H
        attn_ffn = Ffn(signal, "x", n=NT, layers=1, start=0)
        UT = U[:, :, :, :, :].rearrange("p a d s t -> p (a d s t)")
        for F, width in ((chunk_ffn, H), (attn_ffn, NT)):
            used = [0]

            def buffer(name, tiles=1, dt=fp32):
                if F is chunk_ffn:
                    t = sb(name, [P, tiles, H], dt)[:, :, :]
                elif name in ("hAh", "hAl"):
                    at = MT * NT * (name == "hAl")
                    t = bc[:, at:at + MT * NT].rearrange("p (m t) -> p m t", t=NT)
                elif dt is f32r:
                    t = sb("x_" + name, [P, tiles, NT], dt)[:, :, :]
                else:
                    t = UT[:, used[0]:used[0] + tiles * NT].rearrange("p (m t) -> p m t", t=NT)
                    used[0] += tiles * NT
                return t

            F.c = buffer("fc")
            F.xh, F.xl = buffer("xh", 1, f32r), buffer("xl", 1, f32r)
            F.t = buffer("ht", 2)
            F.Ah, F.Al = buffer("hAh", MT, f32r), buffer("hAl", MT, f32r)
            F.Bh, F.Bl = buffer("hBh", MT, f32r), buffer("hBl", MT, f32r)
            F.A = buffer("hA", MT)
        attn_ffn.r = UT[:, 2 * H * DT - NT:2 * H * DT].unsqueeze(1)
        chunk_ffn.r = fr[:, :].unsqueeze(1)
        chunk_ffn.ps, attn_ffn.ps = PF, PR
        chunk_ffn.src, attn_ffn.src = XF[:, :], x3
        Y4 = {0: PY[:, 0, :], 1: PY[:, 1, :], 2: PN[:, 0, :], 3: PN[:, 1, :]}
        staged = U[:, :, :, :, :].rearrange("p a d s t -> p (a d s t)")[:, 0:NFMAT]

        block = ctx.enter_context(nc.Block())

        def place(k):
            f, r = divmod(k, 3 * MT)
            return f, r // MT, r % MT

        def later(c):
            return not isinstance(c, int) or c > 0

        @block.sync
        def _(sp):
            def load_ahead(c):
                if later(c):
                    sp.wait_ge(m_cent.sem, m_cent.at(c, 0))
                sp.dma_start(XM[:, :], xT[:, bass.ds(c * H, H)]).then_inc(xm_in, 16)

            def load_residual(c):
                if later(c):
                    sp.wait_ge(m_res.sem, m_res.at(c, 0))
                sp.dma_start(XR[:, :], xT[:, bass.ds(c * H, H)]).then_inc(xr_in, 16)

            def store(c, skip):
                sp.wait_ge(chunk_ffn.s_res.sem, chunk_ffn.s_res.at(c, 2))
                sp.dma_start(outT[:, bass.ds(c * H + skip, H - skip)], XO[:, skip:H]).then_inc(stored, 16)
                sp.wait_ge(stored, 16 * (c + 1))
                sp.sem_inc(xo_free.sem, 1)

            load_ahead(0)
            sp.dma_start(M[:, 0:P], mats[:, 0:P]).then_inc(ident_in, 16)
            sp.dma_start(C[:, :], cols).then_inc(cols_in, 16)
            sp.dma_start(WC[:, :, :].rearrange("p k n -> p (k n)"), taps).then_inc(taps_in, 16)
            sp.dma_start(yd[:, 0, 0:DI], w_x).then_inc(wx_in, 16)
            sp.dma_start(M[:, P:], mats[:, P:]).then_inc(mats_in, 16)
            load_residual(0)
            sp.dma_start(staged, fmats).then_inc(fmats_in, 16)
            load_ahead(1)
            load_ahead(2)
            with sp.Fori(1, NB + 1) as i:
                load_residual(i)
                load_ahead(i + 2)
                store(i - 1, EFF)
            for i in range(NB + 1, NCH):
                load_residual(i)
                if i + 2 < NCH:
                    load_ahead(i + 2)
                store(i - 1, 0)
            sp.wait_ge(h_scan.sem, h_scan.at(NCH, 0))
            sp.dma_start(t_rep[0:NT, :], rep).then_inc(rep_in, 16)
            store(NCH - 1, 0)
            sp.wait_ge(attn_ffn.s_res.sem, 1)
            sp.dma_start(outT.rearrange("p (b t) -> p b t", t=H)[:, 0:NB, 0:EFF],
                         x5.rearrange("p (b t) -> p b t", b=NB)).then_inc(stored, 16)
            sp.wait_ge(stored, 16 * (NCH + 1))

        @block.gpsimd
        def _(pool):
            pool.memset(mean_w[:, :], 1.0 / P).then_inc(s_set, 1)
            pool.memset(eps_col[:, :], EPS).then_inc(s_set, 1)
            pool.memset(one_col[:, :], 1.0).then_inc(s_set, 1)
            pool.memset(bc[:, :].bitcast(fp32), 0.0).then_inc(s_set, 1)
            pool.memset(tail[:, 0:NB], 0.0).then_inc(s_set, 1)
            pool.memset(state[:, 0:NB], 0.0).then_inc(s_set, 1)
            pool.sem_inc(xo_free.sem, 1)
            pool.sem_inc(chunk_ffn.s_res.sem, 1)

            both = cs[:, :, :].rearrange("p s t -> p (s t)").unsqueeze(1).broadcast_to([P, DT, 2 * H])

            def g(c, p):
                flat = U[:, p % NU, :, :, :].rearrange("p d s t -> p d (s t)")
                pool.wait_ge(c_copied.sem, c_copied.at(c, p + 1))
                pool.wait_ge(h_ready.sem, h_ready.at(c, p + 1))
                pool.tensor_tensor(flat, flat, both, ALU.mult).then_inc(g_prod.sem, 1)

            def ga(c, p):
                if not later(c) and p < NP - 2:
                    pool.sem_inc(g_pair.sem, 1)
                    return
                u = U[:, p % NU, :, :, :]
                pool.wait_ge(g_prod.sem, g_prod.at(c, p + 1))
                pool.tensor_tensor(u[:, :, 0, :], u[:, :, 0, :], u[:, :, 1, :], ALU.add).then_inc(g_pair.sem, 1)

            def gx(c, p):
                if not later(c):
                    if p < NP - 1:
                        return
                    pool.wait_ge(g_ready.sem, g_ready.at(c, NP // 2 - 1))
                pool.wait_ge(g_pair.sem, g_pair.at(c, p + 1))
                u, before = U[:, p % NU, :, 0, :], U[:, (p - 1) % NU, :, 0, :]
                pool.tensor_tensor(u, u, before, ALU.add).then_inc(g_ready.sem, 1)

            units = {"g": g, "ga": ga, "gx": gx}
            body(POOL_START, units, 0, behind=False)
            with pool.Fori(1, NCH - 1) as i:
                body(POOL_ORDER, units, i)
            body(POOL_ORDER, units, NCH - 1, ahead=False)

        @block.scalar
        def _(act):
            act.wait_ge(cols_in, 16)
            act.wait_ge(s_set, 6)
            act.activation(a_neg[:, :], C[:, slice(*COL_AT["a_log"])], ACT.Exp).then_inc(s_aneg, 1)
            loaded = [None]

            def tables(name):
                if name == "ln" and loaded[0] != "ln":
                    act.preload_act_table_set("natural_log_exp_and_others")
                loaded[0] = name

            def rsqrt(src, dst, ln, rs, c, n, from_pe):
                tables("ln")
                act.wait_ge(from_pe.sem, from_pe.at(c, n + 1))
                act.activation(dst, src, ACT.Ln, bias=eps_col[:, :]).then_inc(ln.sem, 1)
                act.wait_ge(ln.sem, ln.at(c, n + 1))
                act.activation(dst, dst, ACT.Exp, scale=-0.5).then_inc(rs.sem, 1)

            def sq(c, _):
                act.wait_ge(m_cent.sem, m_cent.at(c, 1))
                if later(c):
                    act.wait_ge(m_norm.sem, m_norm.at(c, 0))
                act.activation(mr[:, :], PN[:, 0, :], ACT.Square).then_inc(m_sq.sem, 1)

            def rs(c, _):
                rsqrt(PN[:, 1, :], mr[:, :], m_ln, m_rs, c, 0, m_var)

            def ev(c, m):
                tables("silu")
                act.wait_ge(m_proj.sem, m_proj.at(c, m + 1))
                if later(c):
                    act.wait_ge(m_zs.sem, m_zs.at(c, 0))
                act.activation(zr[:, m - DT, :], PN[:, m % 2, :], ACT.Silu).then_inc(m_evac.sem, 1)

            def sx(c, d):
                tables("silu")
                act.wait_ge(m_proj.sem, m_proj.at(c, d + 1))
                if d == 0 and later(c):
                    act.wait_ge(m_skip.sem, m_skip.at(c, 0))
                    act.wait_ge(m_dx.sem, m_dx.at(c, 0))
                    act.wait_ge(m_xp.sem, m_xp.at(c, 0))
                act.activation(xs[:, d, :], PN[:, d, :], ACT.Silu, bias=col("conv_b", d)).then_inc(m_xs.sem, 1)

            def sz(c, _):
                act.wait_ge(m_evac.sem, m_evac.at(c, DT))
                if later(c):
                    act.wait_ge(m_yz.sem, m_yz.at(c, 0))
                act.activation(zs[:, :, :], zr[:, :, :], ACT.Copy).then_inc(m_zs.sem, 1)

            def sa(c, d):
                act.wait_ge(m_dps.sem, m_dps.at(c, d + 1))
                if later(c):
                    act.wait_ge(u_ready.sem, u_ready.at(c, 0))
                act.activation(dx[:, d, :], PN[:, d, :], ACT.Abs, bias=col("b_dt", d)).then_inc(m_abs.sem, 1)

            def sr(c, d):
                act.wait_ge(m_dps.sem, m_dps.at(c, d + 1))
                if later(c):
                    act.wait_ge(a_ready.sem, a_ready.at(c, 0))
                    act.wait_ge(m_dx.sem, m_dx.at(c, 0))
                act.activation(dl[:, d, :], PN[:, d, :], ACT.Relu, bias=col("b_dt", d)).then_inc(m_relu.sem, 1)

            def se(c, _):
                tables("ln")
                act.wait_ge(m_abs.sem, m_abs.at(c, DT))
                act.activation(dx[:, :, :], dx[:, :, :], ACT.Exp, scale=-1.0).then_inc(m_exp.sem, 1)

            def sl(c, _):
                tables("ln")
                act.wait_ge(m_exp.sem, m_exp.at(c, 1))
                act.activation(dx[:, :, :], dx[:, :, :], ACT.Ln, bias=one_col[:, :]).then_inc(m_soft.sem, 1)

            def dec(c, q):
                p, d = divmod(q, DT)
                tables("ln")
                act.wait_ge(m_dl.sem, m_dl.at(c, 1))
                if q == 0 and not later(c):
                    act.wait_ge(s_aneg, 2)
                if p >= NA or later(c):
                    before = p - NA if p >= NA else max(r for r in range(NP) if r % NA == p) - NP
                    act.wait_ge(h_scan.sem, h_scan.at(c, 2 * (DT * before + d + 1)))
                for s in range(2):
                    n = d * NS + 2 * p + s
                    act.activation(A[:, p % NA, d, s, :], dl[:, d, :], ACT.Exp, scale=a_neg[:, n:n + 1]).then_inc(a_ready.sem, 1)

            def cc(c, p):
                act.wait_ge(c_ready.sem, c_ready.at(c, p + 1))
                if p or later(c):
                    act.wait_ge(g_prod.sem, g_prod.at(c, p))
                act.activation(cs[:, :, :], (PR if later(c) else PF)[:, :, :], ACT.Copy).then_inc(c_copied.sem, 1)

            def ffn_units(F):
                n = F.n

                def fs(c, f):
                    act.wait_ge(F.s_cent.sem, F.s_cent.at(c, f + 1))
                    if F is chunk_ffn and f == 0:
                        act.wait_ge(xo_free.sem, xo_free.at(c, 0))
                    act.activation(F.r[:, 0, :], F.ps[:, 0, 0:n], ACT.Square).then_inc(F.s_sq.sem, 1)

                def fr_(c, f):
                    rsqrt(F.ps[:, 1, 0:n], F.r[:, 0, :], F.s_ln, F.s_rs, c, f, F.s_var)

                def si(c, k):
                    f, _, m = place(k)
                    tables("silu")
                    act.wait_ge(F.s_gate.sem, F.s_gate.at(c, MT * f + m + 1))
                    if m >= 2:
                        act.wait_ge(F.s_lo.sem, F.s_lo.at(c, 2 * MT * f + m - 1))
                    act.activation(F.t[:, k % 2, :], F.ps[:, 0, 0:n], ACT.Silu, scale=col("s1", m)).then_inc(F.s_silu.sem, 1)

                def ge(c, k):
                    f, layer, m = place(k)
                    tables("gelu")
                    src, scale = F.ps[:, m % 2, 0:n], col(("sh1", "sh2")[layer - 1], m)
                    act.wait_ge(F.s_hps.sem, F.s_hps.at(c, 2 * MT * f + k % (3 * MT) - MT + 1))
                    if layer == 2:
                        act.activation(F.A[:, m, :], src, ACT.Gelu, scale=scale).then_inc(F.s_gelu.sem, 1)
                        return
                    act.activation(F.Bh[:, m, :], src, ACT.Gelu, scale=scale).then_inc(F.s_gelu.sem, 1)
                    act.wait_ge(F.s_lo.sem, F.s_lo.at(c, 2 * MT * f + k % (3 * MT) - 1))
                    act.activation(F.t[:, k % 2, :], src, ACT.Gelu, scale=scale).then_inc(F.s_gelu.sem, 1)

                return {"fs": fs, "fr": fr_, "si": si, "ge": ge}

            units = {"sq": sq, "rs": rs, "ev": ev, "sx": sx, "sz": sz, "sa": sa, "sr": sr, "se": se, "sl": sl, "dec": dec,
                     "cc": cc} | ffn_units(chunk_ffn)
            body(ACT_ORDER, units, -1, behind=False, state=False)
            def rest(_, k):
                dump, w = (chunk_ffn.Ah, chunk_ffn.Al, chunk_ffn.Bh)[k], min(MT * H, NFMAT - k * MT * H)
                act.wait_ge(s_wl, 1)
                act.activation(dump.rearrange("p m t -> p (m t)")[:, 0:w], WL[:, k * MT * H:k * MT * H + w].bitcast(fp32),
                               ACT.Abs, accum_out=w_rest[:, k:k + 1]).then_inc(s_rest, 1)

            body(ACT_START, units | {"rest": rest}, 0, behind=False)
            loaded[0] = None
            with act.Fori(1, NCH - 1) as i:
                body(ACT_ORDER, units, i)
            loaded[0] = None
            body(ACT_ORDER, units, NCH - 1, ahead=False)

            def a_sq(_, n):
                act.wait_ge(V.sem, V.after("c_" + n))
                act.activation(t_r, t_c, ACT.Square).then_inc(S.sem, 1)

            def a_rs(_, n):
                tables("ln")
                act.wait_ge(E.sem, E.after("var_" + n))
                act.activation(t_r, Y4[1][:, 0:NT], ACT.Ln, bias=eps_col[:, :]).then_inc(S.sem, 1)
                act.wait_ge(S.sem, S.after("ln_" + n))
                act.activation(t_r, t_r, ACT.Exp, scale=-0.5).then_inc(S.sem, 1)

            def a_exp(t):
                tables("ln")
                act.wait_ge(V.sem, V.after(f"sub{t}"))
                act.activation(prob, prob, ACT.Exp, scale=float(HD) ** -0.5).then_inc(S.sem, 1)

            def a_abs(_):
                act.wait_ge(V.sem, V.after("diff1"))
                act.activation(t_old, t_d, ACT.Abs, accum_out=tiny[:, 0:1]).then_inc(S.sem, 1)

            attention = {"a_exp": a_exp, "a_abs": a_abs}
            for n in ("o", "i", "k", "q"):
                def key(t, n=n):
                    return n + (str(t) if n == "q" else "")
                attention["a_sq" + n] = lambda t, key=key: a_sq(t, key(t))
                attention["a_rs" + n] = lambda t, key=key: a_rs(t, key(t))
            ending(ACT_END, units, attention | {"x_" + n: partial(u, 0) for n, u in ffn_units(attn_ffn).items()})

        @block.vector
        def _(dve):
            dve.wait_ge(s_set, 6)
            dve.wait_ge(ident_in, 16)
            dve.tensor_tensor(cent_w[:, :], mat("ident"), mean_w[:, :], ALU.subtract).then_inc(s_cent, 1)
            dve.wait_ge(cols_in, 16)
            dve.tensor_copy(pick[:, :], C[:, slice(*COL_AT["pick"])]).then_inc(s_pick, 1)
            dve.wait_ge(s_aneg, 1)
            dve.tensor_scalar(a_neg[:, :], a_neg[:, :], -1.0, None, ALU.mult).then_inc(s_aneg, 1)

            dve.wait_ge(taps_in, 16)
            dve.wait_ge(wx_in, 16)
            dve.tensor_tensor(WC[:, :, :], WC[:, :, :], yd[:, 0, 0:DI].unsqueeze(1).broadcast_to([P, DC, DI]), ALU.mult).then_inc(s_conv, 1)

            def norm(c, _):
                dve.wait_ge(m_rs.sem, m_rs.at(c, 1))
                if later(c):
                    dve.wait_ge(m_dps.sem, m_dps.at(c, 0))
                dve.tensor_tensor(mc[:, DC - 1:], PN[:, 0, :], mr[:, :], ALU.mult).then_inc(m_norm.sem, 1)

            def cin(c, _):
                if later(c):
                    dve.wait_ge(m_kept.sem, m_kept.at(c, 0))
                    dve.wait_ge(m_proj.sem, m_proj.at(c, 0))
                dve.tensor_copy(mc[:, 0:DC - 1], tail[:, bass.ds(c, 1), :].rearrange("p a t -> p (a t)")).then_inc(m_tail.sem, 1)

            def ktail(c, _):
                dve.wait_ge(m_norm.sem, m_norm.at(c, 1))
                dve.tensor_copy(tail[:, bass.ds(c + NB, 1), :].rearrange("p a t -> p (a t)"), mc[:, H:]).then_inc(m_kept.sem, 1)

            def bdr(c, _):
                dve.wait_ge(m_xp.sem, m_xp.at(c, 1))
                dve.wait_ge(m_proj.sem, m_proj.at(c, 2 * DT))
                dve.wait_ge(m_kept.sem, m_kept.at(c, 1))
                dve.tensor_copy(dr[96:104, :], PN[96:104, 1, :]).then_inc(m_dr.sem, 1)

            def bhi(c, _):
                dve.wait_ge(m_xp.sem, m_xp.at(c, 1))
                if later(c):
                    dve.wait_ge(c_ready.sem, c_ready.at(c, 0))
                dve.tensor_copy(bc[0:96, :], PN[0:96, 1, :]).then_inc(m_hi.sem, 1)

            def blo(c, _):
                dve.wait_ge(m_hi.sem, m_hi.at(c, 1))
                dve.tensor_tensor(bc[64:96, :], PN[64:96, 1, :], bc[64:96, :].bitcast(fp32), ALU.subtract).then_inc(m_bc.sem, 1)

            def dl_(c, _):
                dve.wait_ge(m_soft.sem, m_soft.at(c, 1))
                dve.wait_ge(m_relu.sem, m_relu.at(c, DT))
                dve.tensor_tensor(dl[:, :, :], dl[:, :, :], dx[:, :, :], ALU.add).then_inc(m_dl.sem, 1)

            def dx_(c, _):
                dve.wait_ge(m_dl.sem, m_dl.at(c, 1))
                dve.tensor_tensor(dx[:, :, :], dl[:, :, :], xs[:, :, :], ALU.mult).then_inc(m_dx.sem, 1)

            def dskip(c, _):
                for d in range(DT):
                    dve.wait_ge(m_xs.sem, m_xs.at(c, DT))
                    if later(c):
                        dve.wait_ge(m_out.sem, m_out.at(c, 0))
                    dve.tensor_scalar(yd[:, d, :], xs[:, d, :], col("d_param", d), None, ALU.mult).then_inc(m_skip.sem, 1)

            def take(c, _):
                if later(c):
                    dve.wait_ge(m_keep.sem, m_keep.at(c, 0))
                    dve.wait_ge(h_scan.sem, h_scan.at(c, 0))
                dve.tensor_copy(state_in[:, :], state[:, bass.ds(c, 1), :].rearrange("p a n -> p (a n)")).then_inc(m_take.sem, 1)

            def keep(c, _):
                dve.wait_ge(h_ready.sem, h_ready.at(c, NP))
                dve.tensor_copy(state[:, bass.ds(c + NB, 1), :].rearrange("p a n -> p (a n)"), state_out[:, :]).then_inc(m_keep.sem, 1)

            def u_(c, q):
                p, d = divmod(q, DT)
                dve.wait_ge(b_ready.sem, b_ready.at(c, p + 1))
                dve.wait_ge(m_dx.sem, m_dx.at(c, 1))
                if q == 0 and not later(c):
                    dve.wait_ge(s_wl, 1)
                if p >= NU or later(c):
                    before = p - NU
                    if later(c):
                        read = g_ready if p % 2 == 0 else g_summed
                        dve.wait_ge(read.sem, read.at(c, before // 2 + 1))
                    else:
                        dve.wait_ge(s_first, before + 1)
                both = dx[:, d, :].unsqueeze(1).broadcast_to([P, 2, H])
                dve.tensor_tensor(U[:, p % NU, d, :, :], both, PR[:, :, :], ALU.mult).then_inc(u_ready.sem, 1)

            def scan(c, q):
                p, d = divmod(q, DT)
                u = U[:, p % NU, :, :, :]
                dve.wait_ge(a_ready.sem, a_ready.at(c, 2 * (q + 1)))
                dve.wait_ge(u_ready.sem, u_ready.at(c, q + 1))
                dve.wait_ge(m_take.sem, m_take.at(c, 1))
                for s in range(2):
                    n = 2 * q + s
                    dve.tensor_tensor_scan(u[:, d, s, :], A[:, p % NA, d, s, :], u[:, d, s, :], state_in[:, n:n + 1],
                                           ALU.mult, ALU.add).then_inc(h_scan.sem, 1)
                if d == DT - 1:
                    if later(c) and p == 0:
                        dve.wait_ge(m_keep.sem, m_keep.at(c, 0))
                    dve.wait_ge(h_scan.sem, h_scan.at(c, 2 * DT * (p + 1)))
                    dve.tensor_copy(state_out[:, 2 * DT * p:2 * DT * (p + 1)].rearrange("p (d s) -> p d s", d=DT),
                                    u[:, :, :, H - 1]).then_inc(h_ready.sem, 1)

            def yadd(c, _):
                dve.wait_ge(g_summed.sem, g_summed.at(c, NP // 2))
                dve.wait_ge(m_skip.sem, m_skip.at(c, DT))
                dve.tensor_tensor(yd[:, :, :], PY[:, :, :], yd[:, :, :], ALU.add).then_inc(m_yd.sem, 1)

            def yz(c, _):
                dve.wait_ge(m_yd.sem, m_yd.at(c, 1))
                dve.wait_ge(m_zs.sem, m_zs.at(c, 1))
                dve.tensor_tensor(yd[:, :, :], yd[:, :, :], zs[:, :, :], ALU.mult).then_inc(m_yz.sem, 1)

            def res(c, _):
                dve.wait_ge(m_out.sem, m_out.at(c, 1))
                dve.wait_ge(xr_in, 16 * (c + 1))
                dve.wait_ge(chunk_ffn.s_res.sem, chunk_ffn.s_res.at(c, 0))
                dve.tensor_tensor(XF[:, :], XR[:, :], PN[:, 0, :], ALU.add).then_inc(m_res.sem, 1)

            def ffn_units(F):
                n = F.n

                def fn(c, f):
                    dve.wait_ge(F.s_rs.sem, F.s_rs.at(c, f + 1))
                    dve.tensor_tensor(F.c[:, 0, :], F.ps[:, 0, 0:n], F.r[:, 0, :], ALU.mult).then_inc(F.s_norm.sem, 1)

                def fx(c, f):
                    dve.wait_ge(F.s_norm.sem, F.s_norm.at(c, f + 1))
                    dve.tensor_copy(F.xh[:, 0, :], F.c[:, 0, :]).then_inc(F.s_high.sem, 1)
                    dve.wait_ge(F.s_high.sem, F.s_high.at(c, f + 1))
                    dve.tensor_tensor(F.xl[:, 0, :], F.c[:, 0, :], F.xh[:, 0, :].bitcast(fp32), ALU.subtract).then_inc(F.s_low.sem, 1)

                def mu(c, k):
                    f, _, m = place(k)
                    t = F.t[:, k % 2, :]
                    dve.wait_ge(F.s_silu.sem, F.s_silu.at(c, MT * f + m + 1))
                    dve.wait_ge(F.s_up.sem, F.s_up.at(c, MT * f + m + 1))
                    dve.scalar_tensor_tensor(t, F.ps[:, 1, 0:n], col("s2", m), t, ALU.mult, ALU.mult).then_inc(F.s_mul.sem, 1)

                def hi(c, k):
                    f, _, m = place(k)
                    dve.wait_ge(F.s_mul.sem, F.s_mul.at(c, MT * f + m + 1))
                    dve.tensor_copy(F.Ah[:, m, :], F.t[:, k % 2, :]).then_inc(F.s_hi.sem, 1)

                def lo(c, k):
                    f, layer, m = place(k)
                    high, low = ((F.Ah, F.Al), (F.Bh, F.Bl))[layer]
                    if layer == 0:
                        dve.wait_ge(F.s_hi.sem, F.s_hi.at(c, MT * f + m + 1))
                    else:
                        dve.wait_ge(F.s_gelu.sem, F.s_gelu.at(c, 3 * MT * f + 2 * (m + 1)))
                    dve.tensor_tensor(low[:, m, :], F.t[:, k % 2, :], high[:, m, :].bitcast(fp32), ALU.subtract).then_inc(F.s_lo.sem, 1)

                def fres(c, f):
                    dst = x5 if F is attn_ffn else (XF, XO)[f][:, :]
                    dve.wait_ge(F.s_down.sem, F.s_down.at(c, f + 1))
                    dve.scalar_tensor_tensor(dst, F.ps[:, 0, 0:n], col("s3"), F.src, ALU.mult, ALU.add).then_inc(F.s_res.sem, 1)
                    if F is chunk_ffn and f == 0:
                        dve.wait_ge(F.s_res.sem, F.s_res.at(c, 1))
                        dve.tensor_copy(spec[:, bass.ds(c * EFF, EFF)], XF[:, 0:EFF]).then_inc(f_spec.sem, 1)
                        dve.wait_ge(f_spec.sem, f_spec.at(c, 1))
                        dve.tensor_scalar(XF[:, :], XF[:, :], col("ob"), None, ALU.add).then_inc(f_ob.sem, 1)

                return {"fn": fn, "fx": fx, "mu": mu, "hi": hi, "lo": lo, "fres": fres}

            units = {"norm": norm, "cin": cin, "ktail": ktail, "bdr": bdr, "bhi": bhi, "blo": blo, "dl": dl_, "dx": dx_,
                     "dskip": dskip, "take": take, "keep": keep, "u": u_, "scan": scan, "yadd": yadd, "yz": yz,
                     "res": res} | ffn_units(chunk_ffn)
            body(DVE_ORDER, units, -1, behind=False, state=False)

            dve.wait_ge(fmats_in, 16)
            dve.tensor_copy(WH[:, :], staged).then_inc(s_wh, 1)
            dve.wait_ge(s_wh, 1)
            dve.tensor_tensor(WL[:, :], staged, WH[:, :].bitcast(fp32), ALU.subtract).then_inc(s_wl, 1)


            def some(_, k):
                dve.wait_ge(s_rest, 3)
                dve.tensor_scalar(w_rest[:, 3:6], w_rest[:, 0:3], 0.0, None, ALU.is_gt).then_inc(s_some, 1)

            body(DVE_START, units | {"some": some}, 0, behind=False)
            dve.wait_ge(s_count, 1)
            dve.tensor_scalar(w_split[:, :], PF[:, 0, 0:1], float(P), None, ALU.mult).then_inc(s_split, 1)
            with dve.Fori(1, NCH - 1) as i:
                body(DVE_ORDER, units, i)
            body(DVE_ORDER, units, NCH - 1, ahead=False)

            def step(ins):
                return ins.then_inc(V.sem, 1)

            def pe(name):
                dve.wait_ge(E.sem, E.after(name))

            def own(name):
                dve.wait_ge(V.sem, V.after(name))

            def act_done(name):
                dve.wait_ge(S.sem, S.after(name))

            heads = C[:, slice(*COL_AT["head_of"])]
            lg = PR[:, 0, 0:NH * EFF].rearrange("p (h k) -> p h k", h=NH)
            pr3 = prob.rearrange("p (h k) -> p h k", h=NH)

            def a_start(_):
                dve.wait_ge(h_scan.sem, h_scan.at(NCH, 0))
                step(dve.memset(qpad, 0.0))
                for bd, w in ((bdq, "lqw"), (bdk, "lkw"), (bdv, "lvw")):
                    wide = C[:, slice(*COL_AT[w])].unsqueeze(1).broadcast_to([P, NH, HD])
                    step(dve.tensor_tensor(bd.rearrange("p (h d) -> p h d", h=NH), wide,
                                           heads.unsqueeze(2).broadcast_to([P, NH, HD]), ALU.mult))

            def centre(n, src):
                pe("mean_" + n)
                step(dve.tensor_tensor(t_c, src, Y4[0][:, 0:NT], ALU.subtract))

            def scaled(n):
                act_done("rs_" + n)
                step(dve.tensor_tensor(t_n, t_c, t_r, ALU.mult))

            def a_co(_):
                centre("o", spec[:, 0:NT])

            def a_no(_):
                scaled("o")

            def a_ci(_):
                own("n_o")
                centre("i", t_n)

            def a_ni(_):
                scaled("i")
                own("n_i")
                step(dve.tensor_scalar(t_qa, t_n, col("lna"), None, ALU.mult))
                step(dve.tensor_scalar(t_ka, t_n, col("lnb"), None, ALU.mult))

            def a_qkv(_):
                pe("v")
                step(dve.tensor_scalar(t_q, Y4[2][:, 0:NT], col("qb"), None, ALU.add))
                step(dve.tensor_copy(t_k, Y4[2][:, NT:2 * NT]))
                step(dve.tensor_scalar(t_v, Y4[2][:, 2 * NT:3 * NT], col("vb"), None, ALU.add))

            def a_inner(_):
                pe("vv")
                step(dve.tensor_scalar(t_k0, Y4[3][:, 0:NT], col("lkb"), None, ALU.add))
                step(dve.tensor_scalar(t_vi, Y4[3][:, NT:2 * NT], col("lvb"), None, ALU.add))

            def a_ck(_):
                own("k0")
                centre("k", t_k0)

            def a_nk(_):
                act_done("rs_k")
                step(dve.scalar_tensor_tensor(t_kn, t_c, col("lnd"), t_r, ALU.mult, ALU.mult))
                own("n_k")
                step(dve.tensor_tensor(kblk.rearrange("p (b h k) -> p b h k", b=NB, h=NH),
                                       t_kn.rearrange("p (b k) -> p b k", b=NB).unsqueeze(2).broadcast_to([P, NB, NH, EFF]),
                                       heads.unsqueeze(1).unsqueeze(3).broadcast_to([P, NB, NH, EFF]), ALU.mult))

            def a_vsb(_):
                pe("vi_t")
                step(dve.tensor_copy(t_vsb[0:NT, :], Y4[3][0:NT, 2 * NT:2 * NT + P]))

            def a_vblk(_):
                pe("rep")
                step(dve.tensor_copy(vrep, PR[:, 0, :]))
                own("v_sb")
                for hf in range(2):
                    mask = C[:, COL_AT["vhead_of"][0] + hf * NH:COL_AT["vhead_of"][0] + (hf + 1) * NH]
                    step(dve.tensor_tensor(vblk[:, hf * NB * P:(hf + 1) * NB * P].rearrange("p (b h d) -> p b h d", b=NB, h=NH),
                                           vrep.rearrange("p (b h d) -> p b h d", b=NB, h=NH),
                                           mask.unsqueeze(1).unsqueeze(3).broadcast_to([P, NB, NH, HD]), ALU.mult))

            def a_qq(t):
                pe(f"qq{t}")
                step(dve.tensor_scalar(t_q0, Y4[2][:, 0:NT], col("lqb"), None, ALU.add))

            def a_cq(t):
                own(f"q0{t}")
                centre(f"q{t}", t_q0)

            def a_nq(t):
                act_done(f"rs_q{t}")
                step(dve.scalar_tensor_tensor(qpad.rearrange("p (b q) -> p b q", b=NB)[:, :, 0:EFF],
                                              t_c.rearrange("p (b q) -> p b q", b=NB), col("lnc"),
                                              t_r.rearrange("p (b q) -> p b q", b=NB), ALU.mult, ALU.mult))

            def a_max(t):
                pe(f"logits{t}")
                step(dve.reduce_max(smax, lg, AX.X))
                own(f"max{t}")
                step(dve.tensor_tensor(pr3, lg, smax.unsqueeze(2).broadcast_to([P, NH, EFF]), ALU.subtract))

            def a_prob(t):
                act_done(f"exp{t}")
                step(dve.tensor_reduce(ssum, pr3, AX.X, ALU.add))
                own(f"sum{t}")
                step(dve.reciprocal(ssum, ssum))
                own(f"rec{t}")
                step(dve.tensor_tensor(pr3, pr3, ssum.unsqueeze(2).broadcast_to([P, NH, EFF]), ALU.mult))

            def a_pt(t):
                pe(f"pt{t}")
                step(dve.tensor_copy(pT, PR[:, 1, 0:2 * P]))

            def a_att(t):
                pe(f"att{t}")
                step(dve.tensor_copy(att[t], Y4[3][:, 0:NT]))
                own(f"att{t}")
                if t < 2:
                    step(dve.tensor_tensor(t_q, t_q, att[t], ALU.add))
                if t == 1:
                    step(dve.tensor_tensor(t_d, att[1], att[0], ALU.subtract))

            def a_brk(_):
                pe("diff1")
                step(dve.tensor_scalar(tiny[:, 1:2], Y4[2][:, NT:NT + 1], float(P) / (NB * NH * T * HD), None, ALU.mult))
                own("mean_abs")
                step(dve.tensor_scalar(tiny[:, 2:3], tiny[:, 1:2], 0.1, 0.01, ALU.mult, ALU.add))
                own("limit")
                step(dve.tensor_tensor(tiny[:, 3:4], tiny[:, 1:2], tiny[:, 2:3], ALU.is_lt))
                own("brk")
                step(dve.tensor_scalar(tiny[:, 4:5], tiny[:, 3:4], -1.0, 1.0, ALU.mult, ALU.add))
                step(dve.tensor_scalar(t_d, att[1], tiny[:, 3:4], None, ALU.mult))

            def a_sel(_):
                own("old")
                step(dve.scalar_tensor_tensor(att[0], att[2], tiny[:, 4:5], t_d, ALU.mult, ALU.add))

            def a_done(_):
                pe("ow")
                step(dve.scalar_tensor_tensor(x3, Y4[2][:, 0:NT], col("ob"), spec[:, 0:NT], ALU.add, ALU.add))

            attention = {"a_start": a_start, "a_co": a_co, "a_no": a_no, "a_ci": a_ci, "a_ni": a_ni, "a_qkv": a_qkv, "a_inner": a_inner,
                         "a_ck": a_ck, "a_nk": a_nk, "a_vsb": a_vsb, "a_vblk": a_vblk, "a_qq": a_qq, "a_cq": a_cq, "a_nq": a_nq,
                         "a_max": a_max, "a_prob": a_prob, "a_pt": a_pt, "a_att": a_att, "a_brk": a_brk, "a_sel": a_sel, "a_done": a_done}
            ending(DVE_END, units, attention | {"x_" + n: partial(u, 0) for n, u in ffn_units(attn_ffn).items()})

        @block.tensor
        def _(te):
            def mean(c, _):
                te.wait_ge(xm_in, 16 * (c + 1))
                if isinstance(c, int) and c == 1:
                    te.wait_ge(m_relu.sem, m_relu.at(c - 1, 1))
                    te.wait_ge(m_abs.sem, m_abs.at(c - 1, 1))
                elif later(c):
                    te.wait_ge(m_res.sem, m_res.at(c - 1, 0))
                te.matmul(PN[:, 0, :], cent_w[:, :], XM[:, :], start=True, stop=True).then_inc(m_cent.sem, 1)

            def var(c, _):
                te.wait_ge(m_sq.sem, m_sq.at(c, 1))
                if later(c):
                    te.wait_ge(m_relu.sem, m_relu.at(c, 0))
                    te.wait_ge(m_abs.sem, m_abs.at(c, 0))
                te.matmul(PN[:, 1, :], mean_w[:, :], mr[:, :], start=True, stop=True).then_inc(m_var.sem, 1)

            def proj(c, m):
                te.wait_ge(m_norm.sem, m_norm.at(c, 1))
                te.wait_ge(m_tail.sem, m_tail.at(c, 1))
                if m >= 2:
                    te.wait_ge(m_xs.sem, m_xs.at(c, m - 1))
                if m < DT:
                    for k in range(DC):
                        last = te.matmul(PN[:, m, :], WC[:, k, m * P:(m + 1) * P], mc[:, k:k + H], start=(k == 0), stop=(k == DC - 1))
                else:
                    last = te.matmul(PN[:, m % 2, :], mat("w_z", m - DT, P), mc[:, DC - 1:], start=True, stop=True)
                last.then_inc(m_proj.sem, 1)

            def xp(c, _):
                te.wait_ge(m_evac.sem, m_evac.at(c, DT))
                te.wait_ge(m_xs.sem, m_xs.at(c, DT))
                for d in range(DT):
                    last = te.matmul(PN[0:104, 1, :], mat("w_xproj", d, 104), xs[:, d, :], start=(d == 0), stop=(d == DT - 1))
                last.then_inc(m_xp.sem, 1)

            def dt(c, d):
                te.wait_ge(m_dr.sem, m_dr.at(c, 1))
                if d == 0:
                    te.wait_ge(m_evac.sem, m_evac.at(c, DT))
                else:
                    te.wait_ge(m_bc.sem, m_bc.at(c, 1))
                te.matmul(PN[:, d, :], mat("w_dt", d, P, slice(96, 104)), dr[96:104, :], start=True, stop=True).then_inc(m_dps.sem, 1)

            def spread(bank, n, done):
                for s in range(2):
                    last = te.matmul(bank[:, s, :], pick[0:96, n + s:n + s + 1].broadcast_to([96, P]), bc[0:96, :],
                                     start=True, stop=True)
                last.then_inc(done.sem, 1)

            def b_(c, p):
                te.wait_ge(m_bc.sem, m_bc.at(c, 1))
                if later(c):
                    te.wait_ge(c_copied.sem, c_copied.at(c, p))
                elif p:
                    te.wait_ge(u_ready.sem, u_ready.at(c, DT * p))
                spread(PR, 2 * p, b_ready)

            def c_(c, p):
                if later(c):
                    te.wait_ge(u_ready.sem, u_ready.at(c, DT * (p + 1)))
                    spread(PR, NS + 2 * p, c_ready)
                else:
                    te.wait_ge(m_bc.sem, m_bc.at(c, 1))
                    if p:
                        te.wait_ge(c_copied.sem, c_copied.at(c, p))
                    spread(PF, NS + 2 * p, c_ready)

            def sum_(c, p):
                if not later(c):
                    te.wait_ge(g_prod.sem, g_prod.at(c, p + 1))
                    for s in range(2):
                        for d in range(DT):
                            last = te.matmul(PY[:, d, :], mat("ident"), U[:, p % NU, d, s, :], start=(p == 0 and s == 0), stop=False)
                    last.then_inc(s_first, 1)
                    if p % 2:
                        te.wait_ge(s_first, p + 1)
                        te.sem_inc(g_summed.sem, 1)
                        te.sem_inc(g_ready.sem, 1)
                    return
                te.wait_ge(g_ready.sem, g_ready.at(c, p // 2 + 1))
                if p == 1:
                    te.wait_ge(m_yd.sem, m_yd.at(c, 0))
                for d in range(DT):
                    last = te.matmul(PY[:, d, :], mat("ident"), U[:, p % NU, d, 0, :], start=(p == 1), stop=(p == NP - 1))
                last.then_inc(g_summed.sem, 1)

            def out(c, _):
                te.wait_ge(m_yz.sem, m_yz.at(c, 1))
                following = not isinstance(c, int) or c + 1 < NCH
                te.wait_ge(m_relu.sem, m_relu.at(c + 1, 1 if following else 0))
                te.wait_ge(m_abs.sem, m_abs.at(c + 1, 1 if following else 0))
                for d in range(DT):
                    last = te.matmul(PN[:, 0, :], mat("w_out", d, D), yd[:, d, :], start=(d == 0), stop=(d == DT - 1))
                last.then_inc(m_out.sem, 1)

            mixer = {"mean": mean, "var": var, "proj": proj, "xp": xp, "dt": dt, "B": b_, "C": c_, "sum": sum_, "out": out}

            def run(exact):
                def product(out, name, m, w, hi, lo, tiles, part=None):
                    for k in part or range(tiles):
                        at = FMAT_AT[name][0] + k * w + m * P
                        for W in (WH,) if exact else (WH, WL):
                            for x in (hi, lo):
                                end = k == tiles - 1 and x is lo and (exact or W is WL)
                                last = te.matmul(out, W[:, at:at + P], x[:, k, :],
                                                 start=(k == 0 and W is WH and x is hi), stop=end)
                    return last

                def ffn_units(F):
                    n = F.n

                    def fm(c, f):
                        if F is attn_ffn:
                            te.wait_ge(V.sem, V.after("x3"))
                        elif f == 0:
                            te.wait_ge(m_res.sem, m_res.at(c, 1))
                        else:
                            te.wait_ge(f_ob.sem, f_ob.at(c, 1))
                        te.matmul(F.ps[:, 0, 0:n], cent_w[:, :], F.src, start=True, stop=True).then_inc(F.s_cent.sem, 1)

                    def fv(c, f):
                        te.wait_ge(F.s_sq.sem, F.s_sq.at(c, f + 1))
                        te.matmul(F.ps[:, 1, 0:n], mean_w[:, :], F.r[:, 0, :], start=True, stop=True).then_inc(F.s_var.sem, 1)

                    def gp(c, k):
                        f, _, m = place(k)
                        te.wait_ge(F.s_low.sem, F.s_low.at(c, f + 1))
                        if m:
                            te.wait_ge(F.s_silu.sem, F.s_silu.at(c, MT * f + m))
                        product(F.ps[:, 0, 0:n], "w1", m, HID, F.xh, F.xl, 1).then_inc(F.s_gate.sem, 1)

                    def vp(c, k):
                        f, _, m = place(k)
                        te.wait_ge(F.s_low.sem, F.s_low.at(c, f + 1))
                        if m:
                            te.wait_ge(F.s_mul.sem, F.s_mul.at(c, MT * f + m))
                        product(F.ps[:, 1, 0:n], "w2", m, HID, F.xh, F.xl, 1).then_inc(F.s_up.sem, 1)

                    def h_(c, k, part=range(MT)):
                        f, layer, m = place(k)
                        high, low = (F.Ah, F.Al) if layer == 1 else (F.Bh, F.Bl)
                        te.wait_ge(F.s_lo.sem, F.s_lo.at(c, MT * (2 * f + layer - 1) + part[-1] + 1))
                        if part[0] > 0:
                            pass
                        elif m >= 2 or layer == 2:
                            done = 3 * MT * f + (2 * (m - 1) if layer == 1 else 2 * MT + m - 1 if m >= 2 else 2 * (m + 3))
                            te.wait_ge(F.s_gelu.sem, F.s_gelu.at(c, done))
                        elif m == 0:
                            te.wait_ge(F.s_silu.sem, F.s_silu.at(c, MT * (f + 1)))
                        else:
                            te.wait_ge(F.s_mul.sem, F.s_mul.at(c, MT * (f + 1)))
                        last = product(F.ps[:, m % 2, 0:n], ("h1", "h2")[layer - 1], m, HID, high, low, MT, part)
                        if part[-1] == MT - 1:
                            last.then_inc(F.s_hps.sem, 1)

                    def ha(c, k):
                        h_(c, k, range(MT - 1))

                    def hb(c, k):
                        h_(c, k, range(MT - 1, MT) if k % MT < 2 else range(MT))

                    def down(c, f, part):
                        te.wait_ge(F.s_gelu.sem, F.s_gelu.at(c, 3 * MT * f + 2 * MT + part[-1] + 1))
                        for m in part:
                            last = te.matmul(F.ps[:, 0, 0:n], mat("w3", m, D), F.A[:, m, :], start=(m == 0), stop=(m == MT - 1))
                        return last

                    def da(c, f):
                        down(c, f, range(MT - 1))

                    def dn(c, f):
                        down(c, f, range(MT - 1, MT)).then_inc(F.s_down.sem, 1)

                    return {"fm": fm, "fv": fv, "gp": gp, "vp": vp, "ha": ha, "h": hb, "da": da, "dn": dn}

                units = mixer | ffn_units(chunk_ffn)
                with te.Fori(1, NCH - 1) as i:
                    body(PE_ORDER, units, i)
                body(PE_ORDER, units, NCH - 1, ahead=False)

                def mm(out, w, x, **kw):
                    kw = {"start": True, "stop": True} | kw
                    return te.matmul(out, w, x, **kw)

                def dve(name):
                    te.wait_ge(V.sem, V.after(name))

                def done(ins):
                    ins.then_inc(E.sem, 1)

                def mean_of(src, w=mean_w[:, :]):
                    done(mm(Y4[0][:, 0:NT], w, src))

                def variance(n, w=mean_w[:, :]):
                    te.wait_ge(S.sem, S.after("sq_" + n))
                    done(mm(Y4[1][:, 0:NT], w, t_r))

                def a_mo(_):
                    te.wait_ge(m_yd.sem, m_yd.at(NCH, 0))
                    te.wait_ge(f_spec.sem, f_spec.at(NB, 0))
                    mean_of(spec[:, 0:NT])

                def a_vo(_):
                    variance("o")

                def a_mi(_):
                    dve("n_o")
                    mean_of(t_n)

                def a_vi(_):
                    variance("i")

                def a_qkv(_):
                    te.wait_ge(m_res.sem, m_res.at(NCH, 0))
                    dve("qa")
                    done(mm(Y4[2][:, 0:NT], mat("qw"), t_qa))
                    dve("ka")
                    done(mm(Y4[2][:, NT:2 * NT], mat("kw"), t_ka))
                    done(mm(Y4[2][:, 2 * NT:3 * NT], mat("vw"), t_ka))

                def a_inner(_):
                    dve("k")
                    done(mm(Y4[3][:, 0:NT], bdk, t_k))
                    dve("v")
                    done(mm(Y4[3][:, NT:2 * NT], bdv, t_v))

                def a_mk(_):
                    dve("k0")
                    mean_of(t_k0, mat("group"))

                def a_vk(_):
                    variance("k", mat("group"))

                def a_tv(_):
                    dve("vi")
                    done(te.transpose(Y4[3][0:NT, 2 * NT:2 * NT + P], t_vi, mat("ident")))

                def a_rep(_):
                    dve("vi_sb")
                    te.wait_ge(rep_in, 16)
                    te.wait_ge(c_copied.sem, c_copied.at(NCH, 0))
                    for b in range(NB):
                        last = mm(PR[:, 0, b * P:(b + 1) * P], t_rep[0:NT, b * P:(b + 1) * P], t_vsb[0:NT, :])
                    done(last)

                def a_qq(t):
                    if t:
                        dve(f"qcur{t - 1}")
                    else:
                        dve("vblk1")
                    done(mm(Y4[2][:, 0:NT], bdq, t_q))

                def a_mq(t):
                    dve(f"q0{t}")
                    mean_of(t_q0, mat("group"))

                def a_vq(t):
                    variance(f"q{t}", mat("group"))

                def a_logit(t):
                    dve(f"n_q{t}")
                    for b in range(NB):
                        last = mm(PR[32 * b:32 * (b + 1), 0, 0:NH * EFF], qpad[:, 32 * b:32 * (b + 1)],
                                  kblk[:, b * NH * EFF:(b + 1) * NH * EFF], tile_position=(0, 32 * b))
                    done(last)

                def a_pt(t):
                    dve(f"prob{t}")
                    for hf in range(2):
                        last = te.transpose(PR[:, 1, hf * P:(hf + 1) * P], prob[:, hf * P:(hf + 1) * P], mat("ident"))
                    done(last)

                def a_att(t):
                    dve(f"pt{t}")
                    for b in range(NB):
                        for hf in range(2):
                            last = mm(Y4[3][:, b * EFF:(b + 1) * EFF], vblk[:, (hf * NB + b) * P:(hf * NB + b + 1) * P],
                                      pT[:, hf * P + 32 * b:hf * P + 32 * b + EFF], start=(hf == 0), stop=(hf == 1))
                    done(last)

                def a_diff(_):
                    te.wait_ge(S.sem, S.after("abs1"))
                    done(mm(Y4[2][:, NT:NT + 1], mean_w[:, :], tiny[:, 0:1]))

                def a_ow(_):
                    dve("sel")
                    done(mm(Y4[2][:, 0:NT], mat("ow"), att[0]))

                attention = {"a_mo": a_mo, "a_vo": a_vo, "a_mi": a_mi, "a_vi": a_vi, "a_qkv": a_qkv, "a_inner": a_inner, "a_mk": a_mk,
                             "a_vk": a_vk, "a_tv": a_tv, "a_rep": a_rep, "a_qq": a_qq, "a_mq": a_mq, "a_vq": a_vq, "a_logit": a_logit,
                             "a_pt": a_pt, "a_att": a_att, "a_diff": a_diff, "a_ow": a_ow}
                ending(PE_END, units, attention | {"x_" + n: partial(u, 0) for n, u in ffn_units(attn_ffn).items()})

            te.wait_ge(s_set, 6)
            te.wait_ge(s_cent, 1)
            te.wait_ge(ident_in, 16)
            mean(0, 0)
            var(0, 0)
            te.wait_ge(mats_in, 16)
            te.wait_ge(s_conv, 1)
            for m in range(2 * DT):
                proj(0, m)
            te.wait_ge(s_pick, 1)
            def count(c, _):
                te.wait_ge(s_some, 1)
                te.wait_ge(c_copied.sem, c_copied.at(c, NP))
                for k in range(3):
                    last = te.matmul(PF[:, 0, 0:1], mean_w[:, :], w_rest[:, 3 + k:4 + k], start=(k == 0), stop=(k == 2))
                last.then_inc(s_count, 1)

            body(PE_START, mixer | {"count": count}, 0, behind=False)
            te.wait_ge(s_split, 1)
            inexact = te.value_load(w_split[0:1, 0:1])
            with te.If_eq(te.to_reg(inexact), 0):
                run(True)
            with te.Else():
                run(False)


def rows(v, n=1):
    v = np.asarray(v)
    v = v.reshape(n, P, -1)
    return np.ascontiguousarray(v.transpose(1, 0, 2).reshape(P, -1))


def layout(i):
    f = lambda n: np.asarray(i[n])
    mats = np.zeros((P, NMAT), np.float32)
    cols = np.zeros((P, NCOL), np.float32)

    def m(name, v):
        lo, hi = MAT_AT[name]
        mats[:, lo:hi] = v

    def c(name, v):
        lo, hi = COL_AT[name]
        cols[:, lo:hi] = v

    m("w_z", f("L0_attn_a_W_in")[:, DI:])
    xp = f("L0_attn_a_W_xproj").reshape(DT, P, DTR + 2 * NS)
    lo = MAT_AT["w_xproj"][0]
    for d in range(DT):
        at = lo + d * 104
        mats[:, at:at + 32] = xp[d][:, DTR:]
        mats[:, at + 64:at + 96] = xp[d][:, DTR:]
        mats[:, at + 96:at + 104] = xp[d][:, :DTR]
    m("w_out", rows(f("L0_attn_a_W_out"), DT))
    lo, hi = MAT_AT["w_dt"]
    mats[96:104, lo:hi] = f("L0_attn_a_W_dt")
    fmats = np.concatenate([f("L0_ffn_w1_w").T, f("L0_ffn_w2_w").T]
                           + [rows(f(f"L0_ffn_{n}_w").T, MT) for n in ("h1", "h2")], axis=1)
    m("w3", rows(f("L0_ffn_w3_w").T, MT))
    taps = np.broadcast_to(f("L0_attn_a_conv_w").reshape(DI, DC).T.reshape(1, DC * DI), (P, DC * DI))
    for name in ("qw", "kw", "vw", "ow"):
        m(name, f("L0_attn_b_" + name).T)
    part = np.arange(P)
    m("ident", part[:, None] == part[None, :])
    m("group", np.where(part[:, None] // HD == part[None, :] // HD, np.float32(1.0 / HD), np.float32(0)))

    c("conv_w", rows(f("L0_attn_a_conv_w"), DT))
    c("conv_b", rows(f("L0_attn_a_conv_b"), DT))
    c("b_dt", rows(f("L0_attn_a_b_dt"), DT))
    c("a_log", rows(f("L0_attn_a_A_log"), DT))
    c("d_param", rows(f("L0_attn_a_D_param"), DT))
    c("s1", rows(f("L0_ffn_w1_s"), MT))
    c("s2", rows(f("L0_ffn_w2_s"), MT))
    c("sh1", rows(f("L0_ffn_h1_s"), MT))
    c("sh2", rows(f("L0_ffn_h2_s"), MT))
    c("s3", rows(f("L0_ffn_w3_s")))
    for name, key in (("qb", "qb"), ("vb", "vb"), ("ob", "ob"), ("lna", "lna_w"), ("lnb", "lnb_w")):
        c(name, rows(f("L0_attn_b_" + key)))
    for name, key in (("lnc", "lnc_w"), ("lnd", "lnd_w"), ("lqb", "lqb"), ("lkb", "lkb"), ("lvb", "lvb")):
        c(name, np.tile(f("L0_attn_b_" + key), NH)[:, None])
    for name in ("lqw", "lkw", "lvw"):
        c(name, np.tile(f("L0_attn_b_" + name).T, (NH, 1)))
    n = np.arange(2 * NS)
    c("pick", (part[:, None] == n[None, :]) | (part[:, None] == 64 + n[None, :]))
    heads = np.arange(NH)
    c("head_of", part[:, None] // HD == heads[None, :])
    c("vhead_of", np.concatenate([part[:, None] // EFF + (NH // 2) * hf == heads[None, :] for hf in range(2)], axis=1))
    token = np.arange(NT)
    rep = np.concatenate([token[:, None] == b * EFF + part[None, :] % EFF for b in range(NB)], axis=1)
    return mats, fmats, np.ascontiguousarray(taps), cols, rep.astype(np.float32)


def kernel(**inputs):
    import concourse.bacc as bacc
    from concourse.bass_utils import run_bass_kernel_spmd

    x = np.asarray(inputs["L0_attn_a_x"]).reshape(NB, 2, H, D)
    mats, fmats, taps, cols, rep = layout(inputs)
    arrays = {"xT": np.ascontiguousarray(x.transpose(3, 1, 0, 2).reshape(D, NB * T)), "mats": mats, "fmats": np.ascontiguousarray(fmats),
              "taps": taps, "w_x": np.ascontiguousarray(np.asarray(inputs["L0_attn_a_W_in"])[:, :DI]), "cols": cols, "rep": rep}
    nc = bacc.Bacc("TRN2", target_bir_lowering=False, num_devices=1)
    args = [nc.dram_tensor(n, a.shape, mybir.dt.from_np(a.dtype), kind="ExternalInput").ap() for n, a in arrays.items()]
    out = nc.dram_tensor("outT", (D, NB * T), mybir.dt.float32, kind="ExternalOutput").ap()
    hybrid_kernel(nc, *args, out)
    r = run_bass_kernel_spmd(nc, [arrays], core_ids=[0])
    y = np.asarray(r.results[0]["outT"]).reshape(D, 2, NB, H)
    return np.ascontiguousarray(y.transpose(2, 1, 3, 0)).reshape(NB, T, D)
```
